# Optimizing a Trainium2 kernel written in Bass

```python
import numpy as np
import jax
import jax.numpy as jnp

def _softmax(x, axis=-1):
    return jax.nn.softmax(x, axis=axis)

def _gelu(x):
    return jax.nn.gelu(x, approximate=True)

def _silu(x):
    return jax.nn.silu(x)

def _sigmoid(x):
    return jax.nn.sigmoid(x)

def _layernorm(x, axis=-1, eps=1e-05):
    m = jnp.mean(x, axis=axis, keepdims=True)
    v = jnp.var(x, axis=axis, keepdims=True)
    return (x - m) / jnp.sqrt(v + eps)

def _scatter_add(tgt, idx, src, axis=0):
    return tgt.at[idx].add(src)

def _segment_sum(src, seg, n):
    return jax.ops.segment_sum(src, seg, n)
kernel_name = 'mk_gnn_ffn_d4_gnn_r32_451f0a'

def setup_inputs(seed: int=0):
    np.random.seed(seed)
    _w = jnp.asarray

    def _rec_inputs():
        import jax
        import jax.numpy as jnp
        _gk = jax.random.key(seed)
        x = -8.776e-05 + 1 * jax.random.normal(jax.random.fold_in(_gk, 1), (625, 256), jnp.float32)
        src = jax.random.randint(jax.random.fold_in(_gk, 2), (10000,), 0, 625, jnp.int32)
        dst = jnp.minimum((625 * jax.random.uniform(jax.random.fold_in(_gk, 3), (10000,)) ** 2.0).astype(jnp.int32), 19999)
        _o = jnp.argsort(dst, stable=True)
        src = src[_o]
        dst = dst[_o]
        edge_attr_64 = -9.77346e-05 + 0.999888 * jax.random.normal(jax.random.fold_in(_gk, 12), (10000, 64), jnp.float32)
        edge_type_8 = jax.random.randint(jax.random.fold_in(_gk, 14), (10000,), 0, 8, jnp.int32)
        edge_weight = jax.random.uniform(jax.random.fold_in(_gk, 15), (10000,), jnp.float32, 0.0, 0.999999)
        return (x, src, dst, edge_attr_64, edge_type_8, edge_weight)
    x, src, dst, edge_attr_64, edge_type_8, edge_weight = _rec_inputs()

    def _L0_gnn_setup():
        import jax, jax.numpy as jnp
        import numpy as np
        N_NODES = 625
        N_EDGES = 10000
        D = 256
        R = 8

        def _xavier(key, shape):
            fan_in, fan_out = (shape[-2], shape[-1])
            bound = float(np.sqrt(6.0 / (fan_in + fan_out)))
            return jax.random.uniform(key, shape, jnp.float32, -bound, bound)

        def _rgcn_layer(x, W, self_w, b, src, dst, edge_type, num_nodes):
            xW = jnp.einsum('ni,rio->rno', x, W)
            msg = xW[edge_type, src]
            agg = jax.ops.segment_sum(msg, dst, num_segments=num_nodes)
            return agg + x @ self_w + b
        key = jax.random.key(seed)
        ks = jax.random.split(key, 10)
        x = jax.random.normal(ks[0], (N_NODES, D), jnp.float32)
        edge_index = jax.random.randint(ks[1], (2, N_EDGES), 0, N_NODES)
        edge_type = jax.random.randint(ks[2], (N_EDGES,), 0, R)
        W1 = _xavier(ks[3], (R, D, D))
        self_w1 = _xavier(ks[4], (D, D))
        b1 = jnp.zeros((D,), jnp.float32)
        W2 = _xavier(ks[5], (R, D, D))
        self_w2 = _xavier(ks[6], (D, D))
        b2 = jnp.zeros((D,), jnp.float32)
        return {'x': x, 'W1': W1, 'self_w1': self_w1, 'b1': b1, 'W2': W2, 'self_w2': self_w2, 'b2': b2, 'edge_index': edge_index, 'edge_type': edge_type}
    _L0_gnn_all = _L0_gnn_setup()
    _L0_gnn_in = {k: v for k, v in _L0_gnn_all.items() if k in ('W1', 'self_w1', 'b1', 'W2', 'self_w2', 'b2')}
    del _L0_gnn_all

    def _L0_ffn_setup():
        import jax, jax.numpy as jnp
        import numpy as np
        B, S, D, E, H, K = (4, 128, 256, 8, 512, 2)
        key = jax.random.key(seed)
        ks = jax.random.split(key, 6)
        x = jax.random.normal(ks[0], (B, S, D), jnp.float32)
        Wg = jax.random.normal(ks[1], (D, E), jnp.float32) * 0.02
        bg = jnp.zeros((E,), jnp.float32)
        W1 = jax.random.normal(ks[2], (E, D, H), jnp.float32) * 0.02
        b1 = jnp.zeros((E, H), jnp.float32)
        W2 = jax.random.normal(ks[3], (E, H, D), jnp.float32) * 0.02
        b2 = jnp.zeros((E, D), jnp.float32)
        return {'x': x, 'Wg': Wg, 'bg': bg, 'W1': W1, 'b1': b1, 'W2': W2, 'b2': b2}
    _L0_ffn_all = _L0_ffn_setup()
    _L0_ffn_in = {k: v for k, v in _L0_ffn_all.items() if k in ('Wg', 'bg', 'W1', 'b1', 'W2', 'b2')}
    del _L0_ffn_all

    def _L1_gnn_setup():
        import jax, jax.numpy as jnp
        import numpy as np
        N = 50000
        E = 25000
        DIN = 256
        DOUT = 256
        K = 3
        key = jax.random.key(seed)
        k1, k2, k3 = jax.random.split(key, 3)
        x = jax.random.normal(k1, (N, DIN), dtype=jnp.float32)
        edge_index = jax.random.randint(k2, (2, E), 0, N, dtype=jnp.int32)
        limit = float(np.sqrt(6.0 / (DIN + DOUT)))
        weight = jax.random.uniform(k3, (K + 1, DIN, DOUT), dtype=jnp.float32, minval=-limit, maxval=limit)
        bias = jnp.zeros((DOUT,), dtype=jnp.float32)
        return {'x': x, 'edge_index': edge_index, 'weight': weight, 'bias': bias}
    _L1_gnn_all = _L1_gnn_setup()
    _L1_gnn_in = {k: v for k, v in _L1_gnn_all.items() if k in ('weight', 'bias')}
    del _L1_gnn_all

    def _L1_ffn_setup():
        import jax, jax.numpy as jnp
        import numpy as np
        DIM = 256
        H = 8
        D = 64
        G = 64
        INNER = H * D
        SCALE = D ** (-0.5)
        key = jax.random.key(seed)
        ks = jax.random.split(key, 12)
        B, N = (4, 512)
        x = jax.random.normal(ks[0], (B, N, DIM), dtype=jnp.float32)
        s = lambda fan_in: 1.0 / np.sqrt(fan_in)
        W_fx = jax.random.normal(ks[1], (DIM, INNER), dtype=jnp.float32) * s(DIM)
        b_fx = jnp.zeros((INNER,), dtype=jnp.float32)
        W_x = jax.random.normal(ks[2], (DIM, INNER), dtype=jnp.float32) * s(DIM)
        b_x = jnp.zeros((INNER,), dtype=jnp.float32)
        A = jax.random.normal(ks[3], (G, D), dtype=jnp.float32)
        Q, _ = jnp.linalg.qr(A.T)
        W_slice = Q[:, :G].astype(jnp.float32)
        b_slice = jnp.zeros((G,), dtype=jnp.float32)
        W_q = jax.random.normal(ks[4], (D, D), dtype=jnp.float32) * s(D)
        W_k = jax.random.normal(ks[5], (D, D), dtype=jnp.float32) * s(D)
        W_v = jax.random.normal(ks[6], (D, D), dtype=jnp.float32) * s(D)
        W_out = jax.random.normal(ks[7], (INNER, DIM), dtype=jnp.float32) * s(INNER)
        b_out = jnp.zeros((DIM,), dtype=jnp.float32)
        temperature = jnp.ones((1, H, 1, 1), dtype=jnp.float32) * 0.5
        return {'x': x, 'W_fx': W_fx, 'b_fx': b_fx, 'W_x': W_x, 'b_x': b_x, 'W_slice': W_slice, 'b_slice': b_slice, 'W_q': W_q, 'W_k': W_k, 'W_v': W_v, 'W_out': W_out, 'b_out': b_out, 'temperature': temperature}
    _L1_ffn_all = _L1_ffn_setup()
    _L1_ffn_in = {k: v for k, v in _L1_ffn_all.items() if k in ('W_fx', 'b_fx', 'W_x', 'b_x', 'W_slice', 'b_slice', 'W_q', 'W_k', 'W_v', 'W_out', 'b_out', 'temperature')}
    del _L1_ffn_all

    def _L2_gnn_setup():
        import jax, jax.numpy as jnp
        import numpy as np
        N_NODES = 50000
        N_EDGES = 50000
        IN_F = 256
        OUT_F = 256
        key = jax.random.key(seed)
        k_x, k_ei, k_ew, k_w = jax.random.split(key, 4)
        x = jax.random.normal(k_x, (N_NODES, IN_F), dtype=jnp.float32)
        edge_index = jax.random.randint(k_ei, (2, N_EDGES), 0, N_NODES, dtype=jnp.int32)
        edge_weight = jax.random.uniform(k_ew, (N_EDGES,), dtype=jnp.float32)
        gain = 1.414
        limit = gain * np.sqrt(6.0 / (IN_F + OUT_F))
        W = jax.random.uniform(k_w, (OUT_F, IN_F), minval=-limit, maxval=limit, dtype=jnp.float32)
        b = jnp.zeros((OUT_F,), dtype=jnp.float32)
        return {'x': x, 'edge_index': edge_index, 'edge_weight': edge_weight, 'W': W, 'b': b}
    _L2_gnn_all = _L2_gnn_setup()
    _L2_gnn_in = {k: v for k, v in _L2_gnn_all.items() if k in ('W', 'b')}
    del _L2_gnn_all

    def _L2_ffn_setup():
        import jax, jax.numpy as jnp
        import numpy as np
        B, S, H, F, E, K = (8, 128, 256, 512, 16, 2)
        EPS = 1e-05
        key = jax.random.key(seed)
        ks = jax.random.split(key, 9)
        sc = 0.02
        return {'x': jax.random.normal(ks[0], (B, S, H), dtype=jnp.float32), 'gate_w': jax.random.normal(ks[1], (H, E), dtype=jnp.float32) * sc, 'gate_b': jnp.zeros((E,), dtype=jnp.float32), 'w1': jax.random.normal(ks[2], (E, H, F), dtype=jnp.float32) * sc, 'b1': jnp.zeros((E, F), dtype=jnp.float32), 'w2': jax.random.normal(ks[3], (E, F, H), dtype=jnp.float32) * sc, 'b2': jnp.zeros((E, H), dtype=jnp.float32), 'gamma': jnp.ones((H,), dtype=jnp.float32), 'beta': jnp.zeros((H,), dtype=jnp.float32)}
    _L2_ffn_all = _L2_ffn_setup()
    _L2_ffn_in = {k: v for k, v in _L2_ffn_all.items() if k in ('gate_w', 'gate_b', 'w1', 'b1', 'w2', 'b2', 'gamma', 'beta')}
    del _L2_ffn_all

    def _L3_gnn_setup():
        import jax, jax.numpy as jnp
        import numpy as np
        N_NODES = 50000
        key = jax.random.key(seed)
        k1, k2, k3, k4, k5 = jax.random.split(key, 5)
        N, E, F_IN, F_E, F_OUT = (N_NODES, 25000, 256, 64, 256)
        feat = jax.random.normal(k1, (N, F_IN), dtype=jnp.float32)
        edge_feat = jax.random.normal(k2, (E, F_E), dtype=jnp.float32)
        limit = float(np.sqrt(6.0 / (F_IN + F_E + F_OUT)))
        weight = jax.random.uniform(k3, (F_IN + F_E, F_OUT), minval=-limit, maxval=limit, dtype=jnp.float32)
        bias = jnp.zeros((F_OUT,), dtype=jnp.float32)
        src = jax.random.randint(k4, (E,), 0, N, dtype=jnp.int32)
        dst = jax.random.randint(k5, (E,), 0, N, dtype=jnp.int32)
        return {'feat': feat, 'edge_feat': edge_feat, 'weight': weight, 'bias': bias, 'src': src, 'dst': dst}
    _L3_gnn_all = _L3_gnn_setup()
    _L3_gnn_in = {k: v for k, v in _L3_gnn_all.items() if k in ('weight', 'bias')}
    del _L3_gnn_all

    def _L3_ffn_setup():
        import jax, jax.numpy as jnp
        import numpy as np
        INPUT_WIDTH = 256
        DEPTH = 7
        OUTPUT_WIDTH = 256
        N_NODES = 2 ** (DEPTH + 1) - 1
        key = jax.random.key(seed)
        k_x, k_w1, k_w2 = jax.random.split(key, 3)
        init1 = 1.0 / np.sqrt(INPUT_WIDTH)
        x = jax.random.normal(k_x, (2, 1024, INPUT_WIDTH), dtype=jnp.float32)
        w1s = jax.random.uniform(k_w1, (N_NODES, INPUT_WIDTH), jnp.float32, -init1, init1)
        b1s = jnp.zeros((N_NODES,), jnp.float32)
        w2s = jax.random.uniform(k_w2, (N_NODES, INPUT_WIDTH, OUTPUT_WIDTH), jnp.float32, -init1, init1)
        b2s = jnp.zeros((N_NODES, OUTPUT_WIDTH), jnp.float32)
        return {'x': x, 'w1s': w1s, 'b1s': b1s, 'w2s': w2s, 'b2s': b2s}
    _L3_ffn_all = _L3_ffn_setup()
    _L3_ffn_in = {k: v for k, v in _L3_ffn_all.items() if k in ('w1s', 'b1s', 'w2s', 'b2s')}
    del _L3_ffn_all
    return {'x': x, 'src': src, 'dst': dst, 'edge_attr_64': edge_attr_64, 'edge_type_8': edge_type_8, 'edge_weight': edge_weight, 'L0_gnn_W1': _L0_gnn_in['W1'], 'L0_gnn_self_w1': _L0_gnn_in['self_w1'], 'L0_gnn_b1': _L0_gnn_in['b1'], 'L0_gnn_W2': _L0_gnn_in['W2'], 'L0_gnn_self_w2': _L0_gnn_in['self_w2'], 'L0_gnn_b2': _L0_gnn_in['b2'], 'L0_ffn_Wg': _L0_ffn_in['Wg'], 'L0_ffn_bg': _L0_ffn_in['bg'], 'L0_ffn_W1': _L0_ffn_in['W1'], 'L0_ffn_b1': _L0_ffn_in['b1'], 'L0_ffn_W2': _L0_ffn_in['W2'], 'L0_ffn_b2': _L0_ffn_in['b2'], 'L1_gnn_weight': _L1_gnn_in['weight'], 'L1_gnn_bias': _L1_gnn_in['bias'], 'L1_ffn_W_fx': _L1_ffn_in['W_fx'], 'L1_ffn_b_fx': _L1_ffn_in['b_fx'], 'L1_ffn_W_x': _L1_ffn_in['W_x'], 'L1_ffn_b_x': _L1_ffn_in['b_x'], 'L1_ffn_W_slice': _L1_ffn_in['W_slice'], 'L1_ffn_b_slice': _L1_ffn_in['b_slice'], 'L1_ffn_W_q': _L1_ffn_in['W_q'], 'L1_ffn_W_k': _L1_ffn_in['W_k'], 'L1_ffn_W_v': _L1_ffn_in['W_v'], 'L1_ffn_W_out': _L1_ffn_in['W_out'], 'L1_ffn_b_out': _L1_ffn_in['b_out'], 'L1_ffn_temperature': _L1_ffn_in['temperature'], 'L2_gnn_W': _L2_gnn_in['W'], 'L2_gnn_b': _L2_gnn_in['b'], 'L2_ffn_gate_w': _L2_ffn_in['gate_w'], 'L2_ffn_gate_b': _L2_ffn_in['gate_b'], 'L2_ffn_w1': _L2_ffn_in['w1'], 'L2_ffn_b1': _L2_ffn_in['b1'], 'L2_ffn_w2': _L2_ffn_in['w2'], 'L2_ffn_b2': _L2_ffn_in['b2'], 'L2_ffn_gamma': _L2_ffn_in['gamma'], 'L2_ffn_beta': _L2_ffn_in['beta'], 'L3_gnn_weight': _L3_gnn_in['weight'], 'L3_gnn_bias': _L3_gnn_in['bias'], 'L3_ffn_w1s': _L3_ffn_in['w1s'], 'L3_ffn_b1s': _L3_ffn_in['b1s'], 'L3_ffn_w2s': _L3_ffn_in['w2s'], 'L3_ffn_b2s': _L3_ffn_in['b2s']}

def reference(x, src, dst, edge_attr_64, edge_type_8, edge_weight, L0_gnn_W1, L0_gnn_self_w1, L0_gnn_b1, L0_gnn_W2, L0_gnn_self_w2, L0_gnn_b2, L0_ffn_Wg, L0_ffn_bg, L0_ffn_W1, L0_ffn_b1, L0_ffn_W2, L0_ffn_b2, L1_gnn_weight, L1_gnn_bias, L1_ffn_W_fx, L1_ffn_b_fx, L1_ffn_W_x, L1_ffn_b_x, L1_ffn_W_slice, L1_ffn_b_slice, L1_ffn_W_q, L1_ffn_W_k, L1_ffn_W_v, L1_ffn_W_out, L1_ffn_b_out, L1_ffn_temperature, L2_gnn_W, L2_gnn_b, L2_ffn_gate_w, L2_ffn_gate_b, L2_ffn_w1, L2_ffn_b1, L2_ffn_w2, L2_ffn_b2, L2_ffn_gamma, L2_ffn_beta, L3_gnn_weight, L3_gnn_bias, L3_ffn_w1s, L3_ffn_b1s, L3_ffn_w2s, L3_ffn_b2s):
    import jax
    import jax.numpy as jnp

    def _L0_gnn_ref(x, W1, self_w1, b1, W2, self_w2, b2, edge_index, edge_type):
        import jax, jax.numpy as jnp
        import numpy as np
        N_NODES = 625
        N_EDGES = 10000
        D = 256
        R = 8

        def _xavier(key, shape):
            fan_in, fan_out = (shape[-2], shape[-1])
            bound = float(np.sqrt(6.0 / (fan_in + fan_out)))
            return jax.random.uniform(key, shape, jnp.float32, -bound, bound)

        def _rgcn_layer(x, W, self_w, b, src, dst, edge_type, num_nodes):
            xW = jnp.einsum('ni,rio->rno', x, W)
            msg = xW[edge_type, src]
            agg = jax.ops.segment_sum(msg, dst, num_segments=num_nodes)
            return agg + x @ self_w + b
        src, dst = (edge_index[0], edge_index[1])
        h = _rgcn_layer(x, W1, self_w1, b1, src, dst, edge_type, N_NODES)
        h = jax.nn.relu(h)
        out = _rgcn_layer(h, W2, self_w2, b2, src, dst, edge_type, N_NODES)
        return out

    def _L0_ffn_ref(x, Wg, bg, W1, b1, W2, b2):
        import jax, jax.numpy as jnp
        import numpy as np
        B, S, D, E, H, K = (4, 128, 256, 8, 512, 2)
        Bv, Sv, Dv = x.shape
        gate_scores = x @ Wg + bg
        _, idx = jax.lax.top_k(gate_scores, K)
        mask = jax.nn.one_hot(idx, E, dtype=x.dtype).sum(axis=-2)
        xf = x.reshape(-1, Dv)
        mf = mask.reshape(-1, E)
        h = jax.nn.gelu(jnp.einsum('td,edh->teh', xf, W1) + b1[None], approximate=False)
        y = jnp.einsum('teh,ehd->ted', h, W2) + b2[None]
        out = jnp.einsum('ted,te->td', y, mf)
        return out.reshape(Bv, Sv, Dv)

    def _L1_gnn_ref(x, edge_index, weight, bias):
        import jax, jax.numpy as jnp
        import numpy as np
        N = 50000
        E = 25000
        DIN = 256
        DOUT = 256
        K = 3
        num_nodes = x.shape[0]
        loops = jnp.arange(num_nodes, dtype=edge_index.dtype)
        row = jnp.concatenate([edge_index[0], loops])
        col = jnp.concatenate([edge_index[1], loops])
        deg = jax.ops.segment_sum(jnp.ones_like(row, dtype=x.dtype), row, num_segments=num_nodes)
        deg_inv_sqrt = jnp.where(deg > 0, jax.lax.rsqrt(jnp.maximum(deg, 1e-30)), 0.0)
        Lvals = -deg_inv_sqrt[row] * deg_inv_sqrt[col]
        Lvals = jnp.where(row == col, Lvals + 1.0, Lvals)

        def spmm(v):
            return jax.ops.segment_sum(Lvals[:, None] * v[col], row, num_segments=num_nodes)
        out = jnp.matmul(x, weight[0])
        Tx_0 = x
        Tx_1 = spmm(x)
        out = out + jnp.matmul(Tx_1, weight[1])
        for k in range(2, K + 1):
            Tx_2 = 2.0 * spmm(Tx_1) - Tx_0
            out = out + jnp.matmul(Tx_2, weight[k])
            Tx_0, Tx_1 = (Tx_1, Tx_2)
        return out + bias

    def _L1_ffn_ref(x, W_fx, b_fx, W_x, b_x, W_slice, b_slice, W_q, W_k, W_v, W_out, b_out, temperature):
        import jax, jax.numpy as jnp
        import numpy as np
        DIM = 256
        H = 8
        D = 64
        G = 64
        INNER = H * D
        SCALE = D ** (-0.5)
        B, N, _ = x.shape
        fx_mid = (x @ W_fx + b_fx).reshape(B, N, H, D).transpose(0, 2, 1, 3)
        x_mid = (x @ W_x + b_x).reshape(B, N, H, D).transpose(0, 2, 1, 3)
        temp = jnp.clip(temperature, 0.1, 5.0)
        slice_weights = jax.nn.softmax((x_mid @ W_slice + b_slice) / temp, axis=-1)
        slice_norm = slice_weights.sum(axis=2)
        slice_token = jnp.einsum('bhnc,bhng->bhgc', fx_mid, slice_weights)
        slice_token = slice_token / (slice_norm[..., None] + 1e-05)
        q = slice_token @ W_q
        k = slice_token @ W_k
        v = slice_token @ W_v
        attn = jax.nn.softmax(jnp.einsum('bhgc,bhkc->bhgk', q, k) * SCALE, axis=-1)
        out_slice = jnp.einsum('bhgk,bhkc->bhgc', attn, v)
        out_x = jnp.einsum('bhgc,bhng->bhnc', out_slice, slice_weights)
        out_x = out_x.transpose(0, 2, 1, 3).reshape(B, N, INNER)
        return out_x @ W_out + b_out

    def _L2_gnn_ref(x, edge_index, edge_weight, W, b):
        import jax, jax.numpy as jnp
        import numpy as np
        N_NODES = 50000
        N_EDGES = 50000
        IN_F = 256
        OUT_F = 256
        row, col = (edge_index[0], edge_index[1])
        msgs = edge_weight[:, None] * x[col]
        agg = jax.ops.segment_sum(msgs, row, num_segments=x.shape[0])
        return jnp.einsum('nf,of->no', agg, W) + b

    def _L2_ffn_ref(x, gate_w, gate_b, w1, b1, w2, b2, gamma, beta):
        import jax, jax.numpy as jnp
        import numpy as np
        B, S, H, F, E, K = (8, 128, 256, 512, 16, 2)
        EPS = 1e-05
        gate_logits = x @ gate_w + gate_b
        topk_vals, topk_idx = jax.lax.top_k(gate_logits, K)
        topk_w = jax.nn.softmax(topk_vals, axis=-1)
        h = jax.nn.relu(jnp.einsum('bsh,ehf->bsef', x, w1) + b1)
        expert_out = jnp.einsum('bsef,efh->bseh', h, w2) + b2
        sel = jnp.take_along_axis(expert_out, topk_idx[:, :, :, None], axis=2)
        moe = jnp.sum(topk_w[..., None] * sel, axis=2)
        y = x + moe
        mu = jnp.mean(y, axis=-1, keepdims=True)
        var = jnp.var(y, axis=-1, keepdims=True)
        return (y - mu) / jnp.sqrt(var + EPS) * gamma + beta

    def _L3_gnn_ref(feat, edge_feat, weight, bias, src, dst):
        import jax, jax.numpy as jnp
        import numpy as np
        N_NODES = 50000
        N, F_IN = feat.shape
        ones = jnp.ones(src.shape[0], dtype=jnp.float32)
        out_deg = jax.ops.segment_sum(ones, src, num_segments=N)
        norm_out = jnp.maximum(out_deg, 1.0) ** (-0.5)
        feat_n = feat * norm_out[:, None]
        agg_h = jax.ops.segment_sum(feat_n[src], dst, num_segments=N)
        agg_e = jax.ops.segment_sum(edge_feat, dst, num_segments=N)
        rst = jnp.concatenate([agg_h, agg_e], axis=1) @ weight
        in_deg = jax.ops.segment_sum(ones, dst, num_segments=N)
        norm_in = jnp.maximum(in_deg, 1.0) ** (-0.5)
        rst = rst * norm_in[:, None] + bias
        return jax.nn.relu(rst)

    def _L3_ffn_ref(x, w1s, b1s, w2s, b2s):
        import jax, jax.numpy as jnp
        import numpy as np
        INPUT_WIDTH = 256
        DEPTH = 7
        OUTPUT_WIDTH = 256
        N_NODES = 2 ** (DEPTH + 1) - 1
        B, S, D = x.shape
        flat_x = x.reshape(B * S, D)
        T = flat_x.shape[0]
        current = jnp.zeros((T,), dtype=jnp.int32)
        all_nodes = []
        all_logits = []
        for _ in range(DEPTH + 1):
            all_nodes.append(current)
            score = jnp.einsum('td,td->t', flat_x, w1s[current]) + b1s[current]
            all_logits.append(score)
            choice = ((jnp.sign(score) + 1.0) / 2.0).astype(jnp.int32)
            current = current * 2 + choice + 1
        logits = jnp.stack(all_logits, axis=1)
        path_weights = jax.nn.gelu(jnp.abs(logits), approximate=False)
        out = jnp.zeros((T, OUTPUT_WIDTH), dtype=x.dtype)
        for i in range(DEPTH + 1):
            nodes_i = all_nodes[i]
            t_i = jnp.einsum('td,tdo->to', flat_x, w2s[nodes_i]) + b2s[nodes_i]
            out = out + t_i * path_weights[:, i][:, None]
        return out.reshape(B, S, OUTPUT_WIDTH)
    edge_index = jnp.stack([src, dst])
    x = x + _L0_gnn_ref(_layernorm(x, axis=-1), L0_gnn_W1, L0_gnn_self_w1, L0_gnn_b1, L0_gnn_W2, L0_gnn_self_w2, L0_gnn_b2, edge_index, edge_type_8)
    x = x + _L0_ffn_ref(_layernorm(x, axis=-1)[None], L0_ffn_Wg, L0_ffn_bg, L0_ffn_W1, L0_ffn_b1, L0_ffn_W2, L0_ffn_b2)[0]
    x = x + _L1_gnn_ref(_layernorm(x, axis=-1), edge_index, L1_gnn_weight, L1_gnn_bias)
    x = x + _L1_ffn_ref(_layernorm(x, axis=-1)[None], L1_ffn_W_fx, L1_ffn_b_fx, L1_ffn_W_x, L1_ffn_b_x, L1_ffn_W_slice, L1_ffn_b_slice, L1_ffn_W_q, L1_ffn_W_k, L1_ffn_W_v, L1_ffn_W_out, L1_ffn_b_out, L1_ffn_temperature)[0]
    x = x + _L2_gnn_ref(_layernorm(x, axis=-1), edge_index, edge_weight, L2_gnn_W, L2_gnn_b)
    x = x + _L2_ffn_ref(_layernorm(x, axis=-1)[None], L2_ffn_gate_w, L2_ffn_gate_b, L2_ffn_w1, L2_ffn_b1, L2_ffn_w2, L2_ffn_b2, L2_ffn_gamma, L2_ffn_beta)[0]
    x = x + _L3_gnn_ref(_layernorm(x, axis=-1), edge_attr_64, L3_gnn_weight, L3_gnn_bias, src, dst)
    x = x + _L3_ffn_ref(_layernorm(x, axis=-1)[None], L3_ffn_w1s, L3_ffn_b1s, L3_ffn_w2s, L3_ffn_b2s)[0]
    return x

_drawn_inputs = setup_inputs


def setup_inputs(seed=0):
    import zlib

    import numpy as np

    out = dict(_drawn_inputs(seed))
    spreads = {'L0_gnn_b1': (0.0, 0.1),
     'L0_gnn_b2': (0.0, 0.8),
     'L0_ffn_bg': (0.0, 0.8),
     'L0_ffn_b1': (0.0, 0.8),
     'L0_ffn_b2': (0.0, 0.8),
     'L1_gnn_bias': (0.0, 0.8),
     'L1_ffn_b_fx': (0.0, 0.8),
     'L1_ffn_b_x': (0.0, 0.8),
     'L1_ffn_b_slice': (0.0, 2.0),
     'L1_ffn_b_out': (0.0, 0.8),
     'L1_ffn_temperature': (0.5, 0.6),
     'L2_gnn_b': (0.0, 0.8),
     'L2_ffn_gate_b': (0.0, 0.8),
     'L2_ffn_b1': (0.0, 2.0),
     'L2_ffn_b2': (0.0, 2.0),
     'L2_ffn_gamma': (1.0, 0.6),
     'L2_ffn_beta': (0.0, 0.8),
     'L3_gnn_bias': (0.0, 2.0),
     'L3_ffn_b1s': (0.0, 0.414),
     'L3_ffn_b2s': (0.0, 0.8)}
    factors = {'edge_attr_64': 4.094,
     'L0_ffn_Wg': 6.444,
     'L0_ffn_W1': 8.0,
     'L0_ffn_W2': 7.585,
     'L1_ffn_W_x': 8.0,
     'L1_ffn_W_slice': 8.0,
     'L1_ffn_W_q': 8.0,
     'L1_ffn_W_k': 8.0,
     'L2_ffn_gate_w': 8.0,
     'L2_ffn_w1': 8.0,
     'L2_ffn_w2': 8.0,
     'L3_gnn_weight': 2.674}
    for name, (base, spread) in spreads.items():
        noise = np.random.default_rng([zlib.crc32(name.encode()), seed]).standard_normal(out[name].shape)
        drawn = base * np.exp(spread * noise) if base else spread * noise
        out[name] = jnp.asarray(drawn.astype(out[name].dtype))
    for name, factor in factors.items():
        out[name] = (out[name] * factor).astype(out[name].dtype)
    return out
```

```python
from contextlib import ExitStack

import concourse.bass as bass
from concourse import mybir

F32 = mybir.dt.float32
BF16 = mybir.dt.bfloat16
F16 = mybir.dt.float16
I32 = mybir.dt.int32
U32 = mybir.dt.uint32
ALU = mybir.AluOpType
ACT = mybir.ActivationFunctionType
AX = mybir.AxisListType

N = 625
D = 256
P = 125
NT = N // P
KD = D // 128
E = 10000
CH = E // P
PAIRS = CH // 2
R = 8
FE = 64
HD = 64
HP = 4
HID = 512
MH = HID // 128
E0, E2 = 8, 16
NODES = 255
DEPTH = 8
LEAVES = 2 ** (DEPTH - 1)
TU = 6
STEPS = 252 + 12
SLOTS = 8
EPS = 1e-5
HALF = (313, 312)


def build(nc, a, out, stop=99):
    v, pe, act, pool, sp = nc.vector, nc.tensor, nc.scalar, nc.gpsimd, nc.sync
    table = nc.dram_tensor("relation_table", (R * N, D), F32).ap()

    with ExitStack() as ctx:
        def sb(name, shape, dt=F32):
            return ctx.enter_context(nc.sbuf_tensor(name, shape, dt))

        sems = {}

        def sem(name):
            if name not in sems:
                sems[name] = ctx.enter_context(nc.semaphore(name))
            return sems[name]

        PS = ctx.enter_context(nc.psum_tensor("PS", [128, 8, 512], F32))

        X = sb("X", [P, NT, D])
        XN = sb("XN", [P, NT, D])
        XT = sb("XT", [128, KD, N])
        XNk = XN[:].rearrange("p t (f k) -> p t k f", k=KD)
        C = sb("C", [P, NT, N])
        CW = sb("CW", [P, NT, N])
        CT = sb("CT", [P, NT, N])
        AET = sb("AET", [FE, N])
        ident = sb("ident", [128, 128])
        zeros = sb("zeros", [128, 320], BF16)
        ones = sb("ones", [P, 128])
        io16 = sb("io16", [P, N], F16)
        ioe = sb("ioe", [P, E2])
        EF = sb("EF", [P, 4, CH])
        GI = sb("GI", [P, CH], I32)
        WP3 = sb("WP3", [P, 3, CH])
        gis = sb("gis", [P, 2, SLOTS], I32)
        rng = sb("rng", [1, 3, NT], I32)
        bst = sb("bst", [P, NT, 6])
        mv = sb("mv", [P, NT, 2])
        var5 = sb("var5", [P, NT])
        std5 = sb("std5", [P, NT])
        rstd = sb("rstd", [P, NT])
        dis = sb("dis", [P, NT])
        q5 = sb("q5", [P, NT])
        dg5 = sb("dg5", [P, NT])
        nout = sb("nout", [P, NT])
        nin = sb("nin", [P, NT])
        sc5 = sb("sc5", [P, 4, NT])
        selfw = sb("selfw", [128, 2, KD, D])
        wg0 = sb("wg0", [128, KD, E0])
        wg2 = sb("wg2", [128, KD, E2])
        cheb = sb("cheb", [128, 4, KD, D])
        wfx = sb("wfx", [128, KD, 512])
        wx = sb("wx", [128, KD, 512])
        wout = sb("wout", [128, HP, D])
        bd = sb("bd", [128, 4, 128])
        w2T = sb("w2T", [128, KD, D])
        l3w = sb("l3w", [128, KD, D])
        l3we = sb("l3we", [FE, D])
        b2x0 = sb("b2x0", [E0, D])
        b2x2 = sb("b2x2", [E2, D])
        b1T = sb("b1T", [128, 32 + 64])
        bxT = sb("bxT", [128, HP])
        bias = sb("bias", [P, 8, D])
        bfx = sb("bfx", [P, 512])
        bsl = sb("bsl", [P, HD])
        temp = sb("temp", [P, 8])
        rtemp = sb("rtemp", [P, 8])
        bg0 = sb("bg0", [P, E0])
        bg2 = sb("bg2", [P, E2])
        gate = sb("gate", [P, NT, E2])
        gmax = sb("gmax", [P, NT, 8])
        gidx = sb("gidx", [P, NT, 8], U32)
        gidf = sb("gidf", [P, NT, 2])
        gwt = sb("gwt", [P, NT, 4])
        M = sb("M", [P, NT, E2])
        MT = sb("MT", [E2, N])
        ARENA = 25000
        arena = sb("arena", [128, ARENA])

        def view(off, shape, dt=F32):
            n = 1
            for s in shape[1:]:
                n *= s
            words = n if dt in (F32, I32) else (n + 1) // 2
            assert off + words <= ARENA, (off, words)
            w = arena[0:shape[0], off:off + words]
            if dt != F32:
                w = w.bitcast(dt)
            names = "abcdef"[:len(shape) - 1]
            if len(shape) > 2:
                w = w.rearrange("p (" + " ".join(names) + ") -> p " + " ".join(names),
                                **{k: s for k, s in zip(names, shape[1:])})
            return w

        MSG = view(0, [P, CH, D])
        RING = view(20480, [P, 2, SLOTS, D])
        EA = view(0, [P, CH, FE])
        AE = view(5120, [P, NT, FE])
        ei = view(5500, [CH, 3, P], I32)
        ef = view(6000, [CH, 4, P])
        red = view(6600, [CH, 2])
        TH = view(6700, [1, 3, NT, PAIRS])
        mm_ = view(7400, [1, 2, PAIRS])
        tou = view(7500, [1, 3, NT, PAIRS])
        lh = view(8200, [1, 4, NT])
        wtmp = view(8300, [P, 2, CH])
        wtb = view(8500, [P, CH], BF16)
        b1r = view(8600, [64, 2, 128])
        bxr = view(8900, [HP, 128])
        w2r = view(9200, [128, 2, D])
        OHS = view(9800, [P, 2, 626], BF16)
        OHB = view(10500, [P, 2, 4, 126], BF16)
        OHF = view(11100, [P, 2, P])
        iot = view(12000, [P, N], I32)
        RW = view(13000, [128, 2, KD, D])
        XW = view(14100, [P, 2, NT, D])
        OHG = view(24576, [P, 2, P])
        W1 = view(0, [128, 2, KD, HID])
        W2 = view(2048, [128, 2, MH, D])
        HT = view(4096, [128, 2, MH, N])
        Y = view(0, [P, 4, NT, D])
        U = view(5120, [P, NT, D])
        S1 = view(6400, [P, NT, D])
        S2 = view(7680, [P, NT, D])
        XMT = view(0, [128, HP, N])
        FX = view(2500, [P, NT, 512])
        SW = view(5060, [P, NT, 512])
        SWT = view(7620, [128, HP, N])
        OXT = view(10120, [128, HP, N])
        hm = view(12620, [P, NT, 8])
        hs = view(12660, [P, NT, 8])
        hr = view(12700, [P, NT, 8])
        rn = view(12740, [128, 512])
        STT = view(13252, [128, HP, 128])
        QT = view(13764, [128, HP, 128])
        KT = view(14276, [128, HP, 128])
        VV = view(14788, [128, HP, 128])
        AT = view(15300, [128, HP, HD])
        am = view(15560, [128, 3, HP])
        ABD = view(15600, [128, HP, 128])
        ATT = view(16112, [128, HP, 128])
        OS = view(16624, [128, HP, 128])
        blk = view(17140, [128, 128])
        w1r = view(0, [128, 2, D])
        w1T = view(512, [128, KD, D])
        b1s = view(1024, [P, D])
        b2s = view(1280, [128, 2, D])
        SCO = view(1792, [P, NT, D])
        TM = view(3072, [P, NT, D])
        COT = view(4352, [128, 2, N])
        CXI = view(5632, [P, NT, 512])
        CXS = view(8192, [P, NT, 512])
        PM = view(10752, [P, NT, N])
        LB = view(13900, [P, NT, LEAVES], BF16)
        GB = view(14220, [P, NT, LEAVES], BF16)
        CS = view(14540, [P, NT, D])
        tl = view(15820, [P, NT, LEAVES])
        lid = view(16460, [P, 2, NT])
        tn = view(16480, [NT, 9, STEPS])
        tls = view(18860, [NT, 2, LEAVES])
        tb = view(19120, [NT, 12, 16])
        tbi = view(19320, [NT, 2, 8, 2], I32)
        tcnt = view(19360, [NT, 2], I32)
        tnode = view(19364, [NT, 2, STEPS], I32)
        sid = view(19893, [P, NT], I32)
        TW = view(19900, [128, TU, KD, D])

        WEIGHTS_IN = 16 * (16 + 4 + 8 + 8)


        ones_b = sb("ones_b", [P, P], BF16)
        upper_b = sb("upper_b", [P, P], BF16)
        ioleaf = sb("ioleaf", [P, STEPS])
        pcol = sb("pcol", [P, 2])
        pcoli = sb("pcoli", [P, 1], I32)
        levelk = sb("levelk", [NT, 8])

        block = ctx.enter_context(nc.Block())

        def bank_pair(w):
            return [(w, 0, HALF[0]), (w + 1, HALF[0], N)]

        def yslot(t, base):
            return PS[0:P, base + t // 2, (t % 2) * D:(t % 2) * D + D]

        @block.sync
        def _(_sp):
            def bc(x, n=P):
                return x.partition_broadcast(n)

            def feat(w):
                return w.rearrange("(p k) n -> p k n", k=KD)

            for i, n in enumerate(("src", "dst", "edge_type_8")):
                sp.dma_start(ei[:, i, :], a[n].rearrange("(c p) -> c p", p=P)).then_inc(sem("edges_in"), 16)
            sp.dma_start(ef[:, 3, :], a["edge_weight"].rearrange("(c p) -> c p", p=P)).then_inc(sem("edges_in"), 16)
            sp.dma_start(X[:], a["x"].rearrange("(t p) d -> p t d", p=P)).then_inc(sem("x_in"), 16)
            sp.dma_start(EA, a["edge_attr_64"].rearrange("(c p) f -> p c f", p=P)).then_inc(sem("attr_in"), 16)
            sp.dma_start(b1r[0:32, 0, :], a["L0_ffn_b1"].rearrange("e (m p) -> (e m) p", p=128)).then_inc(sem("prep_in"), 16)
            sp.dma_start(b1r[0:64, 1, :], a["L2_ffn_b1"].rearrange("e (m p) -> (e m) p", p=128)).then_inc(sem("prep_in"), 16)
            sp.dma_start(bxr, a["L1_ffn_b_x"].rearrange("(m p) -> m p", p=128)).then_inc(sem("prep_in"), 16)
            sp.dma_start(w2r, a["L2_gnn_W"].rearrange("(o p) f -> p o f", p=128)).then_inc(sem("prep_in"), 16)
            loads = [
                (selfw[:, 0], feat(a["L0_gnn_self_w1"])), (selfw[:, 1], feat(a["L0_gnn_self_w2"])),
                (wg0[:], feat(a["L0_ffn_Wg"])), (wg2[:], feat(a["L2_ffn_gate_w"])),
                (wfx[:], feat(a["L1_ffn_W_fx"])), (wx[:], feat(a["L1_ffn_W_x"])),
                (wout[:], a["L1_ffn_W_out"].rearrange("(m p) n -> p m n", p=128)),
                (l3w[:], feat(a["L3_gnn_weight"][0:D, :])), (l3we[:], a["L3_gnn_weight"][D:D + FE, :]),
                (b2x0[:], a["L0_ffn_b2"]), (b2x2[:], a["L2_ffn_b2"]),
                (bfx[:], bc(a["L1_ffn_b_fx"])), (bsl[:], bc(a["L1_ffn_b_slice"])),
                (temp[:], bc(a["L1_ffn_temperature"].rearrange("a h b c -> (a h b c)"))),
                (bg0[:], bc(a["L0_ffn_bg"])), (bg2[:], bc(a["L2_ffn_gate_b"])),
            ]
            loads += [(cheb[:, k], feat(a["L1_gnn_weight"][k])) for k in range(4)]
            loads += [(bias[:, i, :], bc(a[n])) for i, n in enumerate(
                ("L0_gnn_b1", "L0_gnn_b2", "L1_gnn_bias", "L1_ffn_b_out", "L2_gnn_b",
                 "L2_ffn_gamma", "L2_ffn_beta", "L3_gnn_bias"))]
            for dst, src in loads:
                sp.dma_start(dst, src).then_inc(sem("weights_in"), 16)
            sp.wait_ge(sem("bd_zeroed"), 1)
            for i, n in enumerate(("L1_ffn_W_slice", "L1_ffn_W_q", "L1_ffn_W_k", "L1_ffn_W_v")):
                for h in range(2):
                    sp.dma_start(bd[h * HD:h * HD + HD, i, h * HD:h * HD + HD], a[n]).then_inc(sem("weights_in"), 16)
            assert 16 * (len(loads) + 8) == WEIGHTS_IN

            if stop > 0:
                for b in range(2):
                    sp.sem_inc(sem(f"xw_stored{b}"), 16)
                    sp.sem_inc(sem(f"xw_copied{b}"), 1)
                for layer, n in enumerate(("L0_gnn_W1", "L0_gnn_W2")):
                    wv = a[n].rearrange("r (p k) n -> r p k n", k=KD)
                    tv = table.rearrange("(r t p) d -> r p t d", t=NT, p=P)
                    if layer:
                        sp.wait_ge(sem("msg_copied"), CH)
                        sp.wait_ge(sem("seg0_tile"), NT)
                    for b in range(2):
                        sp.dma_start(RW[:, b], wv[b]).then_inc(sem(f"rw_in{b}"), 16)

                    def store(i, b):
                        sp.wait_ge(sem(f"xw_copied{b}"), i * 2 + (layer * R + 3))
                        sp.dma_start(tv[bass.ds(i * 2 + b, 1)].rearrange("r p t d -> p (r t) d"),
                                     XW[:, b]).then_inc(sem(f"xw_stored{b}"), 16)

                    with sp.Fori(0, R // 2 - 1) as i:
                        for b in range(2):
                            store(i, b)
                            sp.dma_start(RW[:, b].rearrange("p (r k) n -> p r k n", r=1),
                                         wv[bass.ds(i * 2 + (b + 2), 1)].rearrange("r p k n -> p r k n")).then_inc(sem(f"rw_in{b}"), 16)
                    for b in range(2):
                        store(R // 2 - 1, b)

            def experts(tag, ne, w1, w2):
                w1v = a[w1].rearrange("e (p k) h -> e p k h", k=KD)
                w2v = a[w2].rearrange("e (m p) n -> e p m n", p=128)
                with sp.Fori(0, ne // 2) as i:
                    for b in range(2):
                        sp.wait_ge(sem(tag + f"w_free{b}"), i + 1)
                        sp.dma_start(W1[:, b].rearrange("p (e k) h -> p e k h", e=1),
                                     w1v[bass.ds(i * 2 + b, 1)].rearrange("e p k h -> p e k h")).then_inc(sem(tag + f"w_in{b}"), 16)
                        sp.dma_start(W2[:, b].rearrange("p (e m) h -> p e m h", e=1),
                                     w2v[bass.ds(i * 2 + b, 1)].rearrange("e p m h -> p e m h")).then_inc(sem(tag + f"w_in{b}"), 16)

            if stop > 1:
                experts("moe0_", E0, "L0_ffn_W1", "L0_ffn_W2")
            if stop > 5:
                experts("moe2_", E2, "L2_ffn_w1", "L2_ffn_w2")
            if stop > 7:
                sp.wait_ge(sem("arena_free_for_tree"), 1)
                sp.dma_start(w1r[:, 0, :], a["L3_ffn_w1s"][0:128, :]).then_inc(sem("tree_in"), 16)
                sp.dma_start(w1r[0:127, 1, :], a["L3_ffn_w1s"][128:255, :]).then_inc(sem("tree_in"), 16)
                sp.dma_start(b2s[:, 0, :], a["L3_ffn_b2s"][0:128, :]).then_inc(sem("tree_in"), 16)
                sp.dma_start(b2s[0:127, 1, :], a["L3_ffn_b2s"][128:255, :]).then_inc(sem("tree_in"), 16)
                sp.dma_start(b1s[:, 0:NODES], bc(a["L3_ffn_b1s"])).then_inc(sem("tree_in"), 16)
                tw = a["L3_ffn_w2s"].rearrange("j (p k) n -> j p k n", k=KD)
                sp.wait_ge(sem("tree_lists"), 1)
                done = 0
                for t in range(NT):
                    n = sp.value_load(tcnt[t:t + 1, 0:1], min_val=1, max_val=STEPS // TU)
                    with sp.Fori(0, n) as i:
                        for u in range(TU):
                            node = sp.value_load(tnode[t:t + 1, 0, bass.ds(i * TU + u, 1)], min_val=0, max_val=NODES - 1)
                            sp.wait_ge(sem(f"tree_w_free{u}"), i + done + 1)
                            sp.dma_start(TW[:, u].rearrange("p (j k) n -> p j k n", j=1),
                                         tw[bass.ds(node, 1)].rearrange("j p k n -> p j k n")).then_inc(sem(f"tree_w_in{u}"), 16)
                    done = n + done
            if stop < 8:
              sp.wait_ge(sem("x_final"), 1)
              sp.dma_start(out.rearrange("(t p) d -> p t d", p=P), X[:]).then_inc(sem("out_stored"), 16)
              sp.wait_ge(sem("out_stored"), 16)

        @block.gpsimd
        def _(_p):
            pool.memset(ident[:], 0.0)
            pool.memset(ones[:], 1.0)
            pool.memset(zeros[:], 0.0)
            pool.memset(bd[:], 0.0)
            pool.memset(ones_b[:], 1.0)
            pool.memset(upper_b[:], 1.0)
            for d in range(DEPTH):
                pool.memset(levelk[:, d:d + 1], float(2 ** d - 1))
            pool.drain().then_inc(sem("bd_zeroed"), 1)
            pool.affine_select(out=ident[:], in_=ident[:], compare_op=ALU.not_equal, fill=1.0, base=0,
                               pattern=[[-1, 128]], channel_multiplier=1)
            pool.affine_select(out=upper_b[:], in_=upper_b[:], compare_op=ALU.is_gt, fill=0.0, base=0,
                               pattern=[[1, P]], channel_multiplier=-1)
            pool.iota(pcoli[:], pattern=[[1, 1]], base=0, channel_multiplier=1)
            pool.iota(iot, pattern=[[1, N]], base=0, channel_multiplier=0)
            pool.iota(TH[:, 0].bitcast(I32), pattern=[[P, NT], [0, PAIRS]], base=0, channel_multiplier=0)
            pool.iota(TH[:, 1].bitcast(I32), pattern=[[P, NT], [0, PAIRS]], base=P, channel_multiplier=0)
            pool.iota(TH[:, 2].bitcast(I32), pattern=[[0, NT], [1, PAIRS]], base=0, channel_multiplier=0)
            pool.drain().then_inc(sem("consts"), 1)
            if stop > 0:
                pool.wait_ge(sem("edge_fields"), 1)
                for layer in range(2):
                    for b in range(2):
                        pool.wait_ge(sem(f"xw_stored{b}"), 16 * (R // 2) * (layer + 1) + 16)
                    groups = CH // (2 * SLOTS)
                    with pool.Fori(0, groups) as g:
                        for h in range(2):
                            pool.wait_ge(sem(f"slots_free{h}"), g * SLOTS + (layer * groups + 1) * SLOTS)
                            pool.tensor_copy(gis[:, h, :], GI[:, bass.ds(g * (2 * SLOTS) + h * SLOTS, SLOTS)]).then_inc(sem("idx_staged"), 1)
                            pool.wait_ge(sem("idx_staged"), g * 2 + (layer * groups * 2 + h + 1))
                            pool.sem_inc(sem("idx_seen"), 1)
                            for s in range(SLOTS):
                                pool.indirect_dma_start(
                                    out=RING[:, h, s, :], out_offset=None, in_=table,
                                    in_offset=bass.IndirectOffsetOnAxis(ap=gis[:, h, s:s + 1], axis=0),
                                ).then_inc(sem(f"gathered{h}_{s}"), 16)

            if stop > 7:
                pool.wait_ge(sem("x_final"), 1)
                for t in range(NT):
                    pool.indirect_dma_start(
                        out=out, out_offset=bass.IndirectOffsetOnAxis(ap=sid[:, t:t + 1], axis=0),
                        in_=CXS[:, t, D:2 * D], in_offset=None).then_inc(sem("out_stored"), 16)
                pool.wait_ge(sem("out_stored"), 16 * NT)

        @block.scalar
        def _(_a):
            def stats(li):
                act.wait_ge(sem("var_ready"), li + 1)
                act.activation(std5[:], var5[:], ACT.Sqrt).then_inc(sem("std_ready"), 1)

            def features(fi):
                act.wait_ge(sem("xt_mm"), 3 * fi + 1)
                act.copy(XT[:, 0, 0:500], PS[:, 0, 0:500]).then_inc(sem("xt_ready"), 1)

            def edges():
                for t in range(NT):
                    act.wait_ge(sem("edge_tile_mm"), t + 1)
                    for w, dst in ((0, C), (2, CW)):
                        for b, c0, c1 in bank_pair(w):
                            act.copy(dst[:, t, c0:c1], PS[0:P, b, 0:c1 - c0])
                    act.copy(AE[:, t, :], PS[0:P, 4, 0:FE]).then_inc(sem("edge_tile_copied"), 1)
                for i in range(NT):
                    act.wait_ge(sem("ct_mm"), i + 1)
                    act.copy(CT[:, i, 0:500], PS[0:P, (i % 2) * 2, 0:500])
                    act.copy(CT[:, i, 500:N], PS[0:P, (i % 2) * 2 + 1, 0:P]).then_inc(sem("ct_copied"), 1)
                act.wait_ge(sem("aet_mm"), 1)
                act.copy(AET[:, 0:500], PS[0:FE, 4, 0:500])
                act.copy(AET[:, 500:N], PS[0:FE, 5, 0:P]).then_inc(sem("aet_copied"), 1)
                act.wait_ge(sem("degrees"), 1)
                act.activation(sc5[:, 1:4, :], sc5[:, 1:4, :], ACT.Sqrt).then_inc(sem("degree_roots"), 1)

            def relational(layer):
                with act.Fori(0, R // 2) as i:
                    for b in range(2):
                        act.wait_ge(sem(f"rel_mm{b}"), i + (layer * (R // 2) + 1))
                        act.wait_ge(sem(f"xw_stored{b}"), i * 16 + (layer * (R // 2) + 1) * 16)
                        act.copy(XW[:, b, 0:2, :], PS[0:P, 3 * b, :].rearrange("p (t d) -> p t d", t=2))
                        act.copy(XW[:, b, 2:4, :], PS[0:P, 3 * b + 1, :].rearrange("p (t d) -> p t d", t=2)).then_inc(sem(f"xw_copied{b}"), 1)
                if layer == 0:
                    act.wait_ge(sem("edge_tile_mm"), NT)
                else:
                    act.wait_ge(sem("seg0_tile"), NT)
                groups = CH // (2 * SLOTS)
                with act.Fori(0, groups) as g:
                    for h in range(2):
                        for s in range(SLOTS):
                            act.wait_ge(sem(f"gathered{h}_{s}"), g * 16 + (layer * groups + 1) * 16)
                            act.copy(MSG[:, bass.ds(g * (2 * SLOTS) + (h * SLOTS + s), 1), :], RING[:, h, s:s + 1, :]).then_inc(sem("msg_copied"), 1)
                        act.drain().then_inc(sem(f"slots_free{h}"), SLOTS)

            def experts(tag, ne, func, b1off):
                with act.Fori(0, ne // 2) as i:
                    for b in range(2):
                        act.wait_ge(sem(tag + f"w_free{b}"), i + 1)
                        for m in range(MH):
                            for hf, (bank, c0, c1) in enumerate(bank_pair((m % 2) * 2)):
                                act.wait_ge(sem(tag + "hidden_mm"), i * (4 * MH) + (b * 2 * MH + 2 * m + hf + 1))
                                act.sem_inc(sem(tag + "hidden_seen"), 1)
                                act.activation(HT[:, b, m, c0:c1], PS[:, bank, 0:c1 - c0], func,
                                               bias=b1T[:, bass.ds(i * (2 * MH) + (b1off + b * MH + m), 1)]).then_inc(sem(tag + "hidden"), 1)

            if stop > 0:
                for h in range(2):
                    act.sem_inc(sem(f"slots_free{h}"), SLOTS)
            edges()
            if stop > 0:
                stats(0)
                features(0)
                relational(0)
                features(1)
                relational(1)
            if stop > 1:
                stats(1)
                features(2)
                experts("moe0_", E0, ACT.Gelu, 0)
            if stop > 2:
                stats(2)
                features(3)
            if stop > 3:
                stats(3)
                features(4)
                for t in range(NT):
                    act.wait_ge(sem("slice_shifted"), t + 1)
                    act.activation(SW[:, t, :], SW[:, t, :], ACT.Exp).then_inc(sem("slice_exp"), 1)
                act.wait_ge(sem("attn_shifted"), 1)
                act.activation(AT, AT, ACT.Exp, scale=HD ** -0.5).then_inc(sem("attn_exp"), 1)
            if stop > 4:
                stats(4)
                features(5)
            if stop > 5:
                stats(5)
                features(6)
                act.wait_ge(sem("top2_diff"), 1)
                act.activation(gwt[:, :, 1], gwt[:, :, 0], ACT.Exp).then_inc(sem("top2_exp"), 1)
                experts("moe2_", E2, ACT.Relu, 32)
                stats(6)
            if stop > 6:
                stats(7)
                features(7)
            if stop > 7:
                stats(8)
                features(8)
                act.wait_ge(sem("tree_scores"), 1)
                act.activation(CXI[:, :, 0:NODES], SCO[:, :, 0:NODES], ACT.Abs).then_inc(sem("tree_abs"), 1)
                act.wait_ge(sem("tree_abs"), 1)
                act.activation(CXI[:, :, 0:NODES], CXI[:, :, 0:NODES], ACT.Gelu).then_inc(sem("tree_gelu"), 1)
                act.wait_ge(sem("tree_sorted"), 1)
                for bank, c0, c1 in bank_pair(5):
                    act.copy(XT[:, 0, c0:c1], PS[:, bank, 0:c1 - c0])
                for t in (0, 1):
                    act.copy(CXS[:, t, :], PS[0:P, t, :])
                act.drain().then_inc(sem("tree_sorted_out"), 1)
                act.wait_ge(sem("tree_sorted"), 2)
                for bank, c0, c1 in bank_pair(5):
                    last = act.copy(XT[:, 1, c0:c1], PS[:, bank, 0:c1 - c0])
                last.then_inc(sem("tree_sorted_out"), 1)

        @block.tensor
        def _(_t):
            def rows(j=0):
                return slice(j * P, j * P + P)

            def features(fi):
                for k in range(KD):
                    for t in range(NT - 1):
                        if k == 0:
                            pe.wait_ge(sem("xn_ready"), NT * fi + t + 1)
                        last = pe.transpose(PS[:, k, rows(t)], XNk[:, t, k, :], ident[0:P, 0:P])
                    last.then_inc(sem("xt_mm"), 1)
                pe.wait_ge(sem("xn_ready"), NT * fi + NT)
                for k in range(KD):
                    last = pe.transpose(PS[:, 2, rows(k)], XNk[:, NT - 1, k, :], ident[0:P, 0:P])
                last.then_inc(sem("xt_mm"), 1)
                pe.wait_ge(sem("xt_ready"), 3 * fi + 3)

            def rowprod(dst, w, t, n=None, start=True, stop_=True):
                for k in range(KD):
                    last = pe.matmul(dst, XT[:, k, rows(t)], w[:, k, :] if n is None else w[:, k, n],
                                     start=start and k == 0, stop=stop_ and k == KD - 1, skip_group_check=True)
                return last

            def edges():
                pe.wait_ge(sem("consts"), 1)
                pe.wait_ge(sem("edge_rows"), 1)
                for i in range(4):
                    pe.transpose(PS[0:P, 0, i * CH:i * CH + CH], ef[:, i, :], ident[0:CH, 0:CH])
                for i in range(2):
                    last = pe.transpose(PS[0:1, 1, i * CH:i * CH + CH], red[:, i:i + 1], ident[0:CH, 0:CH])
                last.then_inc(sem("edge_cols"), 1)
                pe.wait_ge(sem("prep_in"), 64)
                pe.transpose(PS[:, 2, 0:32], b1r[0:32, 0, :], ident[0:32, 0:32])
                pe.transpose(PS[:, 2, 32:96], b1r[0:64, 1, :], ident[0:64, 0:64])
                pe.transpose(PS[:, 2, 96:100], bxr, ident[0:HP, 0:HP])
                w2rk = w2r.rearrange("p o (f k) -> p o k f", k=KD)
                for k in range(KD):
                    for o in range(2):
                        last = pe.transpose(PS[:, 3, (k * 2 + o) * 128:(k * 2 + o) * 128 + 128], w2rk[:, o, k, :], ident[:])
                last.then_inc(sem("prep_mm"), 1)
                pe.wait_ge(sem("ranges"), 1)
                pe.wait_ge(sem("prep_out"), 1)
                pe.wait_ge(sem("attr_in"), 16)
                for b in range(2):
                    pe.sem_inc(sem(f"oh_free{b}"), PAIRS + 1)
                for t in range(NT):
                    lo = pe.value_load(rng[0:1, 0, t:t + 1], min_val=0, max_val=PAIRS - 1)
                    hi = pe.value_load(rng[0:1, 1, t:t + 1], min_val=1, max_val=PAIRS)
                    step = pe.value_load(rng[0:1, 2, t:t + 1], min_val=0, max_val=PAIRS * (NT + 1) + 1)
                    if t:
                        pe.wait_ge(sem("edge_tile_copied"), t)
                    for w in (0, 2):
                        for bank, c0, c1 in bank_pair(w):
                            pe.matmul(PS[0:P, bank, 0:c1 - c0], zeros[0:P, 0:P], zeros[0:P, 0:c1 - c0],
                                      start=True, stop=False, skip_group_check=True)
                    pe.matmul(PS[0:P, 4, 0:FE], zeros[0:P, 0:P], zeros[0:P, 0:FE], start=True, stop=False, skip_group_check=True)
                    with pe.Fori(lo, hi) as j:
                        for b in range(2):
                            pe.wait_ge(sem(f"oh_ready{b}"), j + step)
                            for i in range(4):
                                for bank, c0, c1 in bank_pair(0 if i == 0 else 2):
                                    pe.matmul(PS[0:P, bank, 0:c1 - c0], OHB[:, b, i, 0:P], OHS[:, b, c0:c1],
                                              start=False, stop=False, skip_group_check=True)
                            pe.matmul(PS[0:P, 4, 0:FE], OHF[:, b, :], EA[:, bass.ds(j * 2 + b, 1), :],
                                      start=False, stop=False, skip_group_check=True).then_inc(sem(f"oh_free{b}"), 1)
                    for w in (0, 2):
                        for bank, c0, c1 in bank_pair(w):
                            pe.matmul(PS[0:P, bank, 0:c1 - c0], zeros[0:P, 0:P], zeros[0:P, 0:c1 - c0],
                                      start=False, stop=True, skip_group_check=True)
                    pe.matmul(PS[0:P, 4, 0:FE], zeros[0:P, 0:P], zeros[0:P, 0:FE], start=False, stop=True,
                              skip_group_check=True).then_inc(sem("edge_tile_mm"), 1)
                pe.wait_ge(sem("edge_tile_copied"), NT)
                for i in range(NT):
                    if i >= 2:
                        pe.wait_ge(sem("ct_copied"), i - 1)
                    for j in range(NT):
                        last = pe.transpose(PS[0:P, (i % 2) * 2 + j // 4, rows(j % 4)], C[:, j, rows(i)], ident[0:P, 0:P])
                    last.then_inc(sem("ct_mm"), 1)
                for j in range(NT):
                    last = pe.transpose(PS[0:FE, 4 + j // 4, rows(j % 4)], AE[:, j, :], ident[0:P, 0:P])
                last.then_inc(sem("aet_mm"), 1)
                pe.wait_ge(sem("ct_copied"), NT)
                pe.wait_ge(sem("aet_copied"), 1)

            def relational(layer):
                with pe.Fori(0, R // 2) as i:
                    for b in range(2):
                        pe.wait_ge(sem(f"rw_in{b}"), i * 16 + (layer * (R // 2) + 1) * 16)
                        pe.wait_ge(sem(f"xw_copied{b}"), i * 2 + (layer * R + 1))
                        for t in range(NT):
                            last = rowprod(yslot(t, 3 * b), RW[:, b], t)
                        last.then_inc(sem(f"rel_mm{b}"), 1)
                for b in range(2):
                    pe.wait_ge(sem(f"xw_copied{b}"), R * (layer + 1) + 1)
                for b in range(2):
                    pe.sem_inc(sem(f"seg{layer}_free{b}"), PAIRS + 1)
                for t in range(NT):
                    lo = pe.value_load(rng[0:1, 0, t:t + 1], min_val=0, max_val=PAIRS - 1)
                    hi = pe.value_load(rng[0:1, 1, t:t + 1], min_val=1, max_val=PAIRS)
                    step = pe.value_load(rng[0:1, 2, t:t + 1], min_val=0, max_val=PAIRS * (NT + 1) + 1)
                    acc = PS[0:P, t, 0:D]
                    rowprod(acc, selfw[:, layer], t, stop_=False)
                    with pe.Fori(lo, hi) as j:
                        for b in range(2):
                            pe.wait_ge(sem(f"seg{layer}_ready{b}"), j + step)
                            pe.wait_ge(sem("msg_copied"), j * 2 + (layer * CH + b + 1))
                            pe.matmul(acc, OHG[:, b, :], MSG[:, bass.ds(j * 2 + b, 1), :],
                                      start=False, stop=False, skip_group_check=True).then_inc(sem(f"seg{layer}_free{b}"), 1)
                    pe.matmul(acc, zeros[0:P, 0:P], zeros[0:P, 0:D], start=False, stop=True,
                              skip_group_check=True).then_inc(sem(f"seg{layer}_tile"), 1)

            def experts(tag, ne, wg, b2x):
                for t in range(NT):
                    last = rowprod(PS[0:P, 7, t * ne:t * ne + ne], wg, t)
                last.then_inc(sem(tag + "route_mm"), 1)
                pe.wait_ge(sem(tag + "route"), 1)
                for t in range(NT):
                    last = pe.transpose(PS[0:ne, 5 + t // 4, rows(t % 4)], M[:, t, 0:ne], ident[0:P, 0:P])
                last.then_inc(sem(tag + "route_mm"), 1)
                pe.wait_ge(sem(tag + "route"), 2)
                for t in range(NT):
                    last = pe.matmul(yslot(t, 4), MT[0:ne, rows(t)], b2x[:], start=True, stop=True)
                last.then_inc(sem(tag + "route_mm"), 1)
                for b in range(2):
                    pe.sem_inc(sem(tag + f"w_free{b}"), 1)
                with pe.Fori(0, ne // 2) as i:
                    for b in range(2):
                        pe.wait_ge(sem(tag + f"w_in{b}"), i * 32 + 32)
                        for m in range(MH):
                            for hf, (bank, c0, c1) in enumerate(bank_pair((m % 2) * 2)):
                                n = b * 2 * MH + 2 * m + hf - 3
                                if n >= 1:
                                    pe.wait_ge(sem(tag + "hidden"), i * (4 * MH) + n)
                                for k in range(KD):
                                    last = pe.matmul(PS[:, bank, 0:c1 - c0], W1[:, b, k, m * 128:m * 128 + 128], XT[:, k, c0:c1],
                                                     start=(k == 0), stop=(k == KD - 1))
                                last.then_inc(sem(tag + "hidden_mm"), 1)
                        pe.wait_ge(sem(tag + "hidden"), i * (4 * MH) + (b + 1) * 2 * MH)
                        for g, tiles in enumerate(((0, 1), (2, 3), (4,))):
                            pe.wait_ge(sem(tag + "added"), i * 6 + (b * 3 + g + 1))
                            for t in tiles:
                                for m in range(MH):
                                    last = pe.matmul(yslot(t, 4), HT[:, b, m, rows(t)], W2[:, b, m, :],
                                                     start=(m == 0), stop=(m == MH - 1))
                            last.then_inc(sem(tag + "y_mm"), 1)
                        pe.drain().then_inc(sem(tag + f"w_free{b}"), 1)

            def spmm(mat, rhs, i, dst, stop_=True):
                for j in range(NT):
                    last = pe.matmul(dst, mat[:, j, rows(i)], rhs(j), start=(j == 0), stop=stop_ and j == NT - 1,
                                     skip_group_check=True)
                return last

            edges()
            pe.wait_ge(sem("weights_in"), WEIGHTS_IN)
            if stop > 0:
                features(0)
                relational(0)
                features(1)
                relational(1)
            if stop > 1:
                features(2)
                experts("moe0_", E0, wg0, b2x0)
            if stop > 2:
                features(3)
                for w in range(4):
                    if w >= 2:
                        pe.wait_ge(sem("cheb_y"), w - 1)
                    for t in range(NT):
                        last = rowprod(yslot(t, 3 if w % 2 == 0 else 0), cheb[:, w], t)
                    last.then_inc(sem("cheb_mm"), 1)
                for r in range(3):
                    pe.wait_ge(sem("cheb_u"), r + 1)
                    for i in range(NT):
                        last = spmm(C, lambda j: U[:, j, :], i, PS[0:P, i, 0:D])
                    last.then_inc(sem("cheb_spmm"), 1)
            if stop > 3:
                features(4)
                for m in range(HP):
                    for bank, c0, c1 in bank_pair((m % 2) * 2):
                        if m >= 2:
                            pe.wait_ge(sem("xmt"), m - 1)
                        for k in range(KD):
                            last = pe.matmul(PS[:, bank, 0:c1 - c0], wx[:, k, m * 128:m * 128 + 128], XT[:, k, c0:c1],
                                             start=(k == 0), stop=(k == KD - 1))
                    last.then_inc(sem("xmt_mm"), 1)
                for t in range(NT):
                    if t >= 2:
                        pe.wait_ge(sem("fx"), t - 1)
                    rowprod(PS[0:P, 4 + t % 2, :], wfx, t).then_inc(sem("fx_mm"), 1)
                pe.wait_ge(sem("xmt"), HP)
                for t in range(NT):
                    if t >= 2:
                        pe.wait_ge(sem("slice_shifted"), t - 1)
                    for m in range(HP):
                        last = pe.matmul(PS[0:P, 6 + t % 2, m * 128:m * 128 + 128], XMT[:, m, rows(t)], bd[:, 0, :],
                                         start=True, stop=True)
                    last.then_inc(sem("logit_mm"), 1)
                pe.wait_ge(sem("fx"), NT)
                for t in range(NT):
                    pe.wait_ge(sem("slice_w"), t + 1)
                    pe.matmul(PS[:, 1, :], ones[:, :], SW[:, t, :], start=(t == 0), stop=(t == NT - 1), skip_group_check=True)
                for m in range(HP):
                    for t in range(NT):
                        last = pe.matmul(PS[:, 0, m * 128:m * 128 + 128], FX[:, t, m * 128:m * 128 + 128],
                                         SW[:, t, m * 128:m * 128 + 128], start=(t == 0), stop=(t == NT - 1), skip_group_check=True)
                last.then_inc(sem("attn_products"), 1)
                for m in range(HP):
                    if m >= 2:
                        pe.wait_ge(sem("swt"), m - 1)
                    for t in range(NT):
                        last = pe.transpose(PS[:, 2 + (m % 2) * 2 + t // 4, rows(t % 4)], SW[:, t, m * 128:m * 128 + 128], ident[0:P, 0:P])
                    last.then_inc(sem("swt_mm"), 1)
                pe.wait_ge(sem("attn_operands"), 1)
                pe.wait_ge(sem("swt"), HP)
                for w, bank in ((1, 2), (2, 3)):
                    for m in range(HP):
                        last = pe.matmul(PS[:, bank, m * 128:m * 128 + 128], bd[:, w, :], STT[:, m, :], start=True, stop=True)
                for m in range(HP):
                    last = pe.matmul(PS[:, 4, m * 128:m * 128 + 128], STT[:, m, :], bd[:, 3, :], start=True, stop=True)
                last.then_inc(sem("attn_products"), 1)
                pe.wait_ge(sem("attn_operands"), 2)
                for m in range(HP):
                    last = pe.matmul(PS[:, 0, m * 128:m * 128 + 128], QT[:, m, :], KT[:, m, :], start=True, stop=True)
                last.then_inc(sem("attn_products"), 1)
                pe.wait_ge(sem("attn_operands"), 3)
                for m in range(HP):
                    last = pe.transpose(PS[:, 1, m * 128:m * 128 + 128], ABD[:, m, :], ident[:])
                last.then_inc(sem("attn_products"), 1)
                pe.wait_ge(sem("attn_operands"), 4)
                for m in range(HP):
                    last = pe.matmul(PS[:, 2, m * 128:m * 128 + 128], ATT[:, m, :], VV[:, m, :], start=True, stop=True)
                last.then_inc(sem("attn_products"), 1)
                pe.wait_ge(sem("attn_operands"), 5)
                for m in range(HP):
                    for bank, c0, c1 in bank_pair(4 if m % 2 == 0 else 0):
                        if m >= 2:
                            pe.wait_ge(sem("oxt"), m - 1)
                        last = pe.matmul(PS[:, bank, 0:c1 - c0], OS[:, m, :], SWT[:, m, c0:c1], start=True, stop=True)
                    last.then_inc(sem("oxt_mm"), 1)
                pe.wait_ge(sem("oxt"), HP)
                for t in range(NT):
                    for m in range(HP):
                        last = pe.matmul(PS[0:P, t, 0:D], OXT[:, m, rows(t)], wout[:, m, :], start=(m == 0), stop=(m == HP - 1))
                    last.then_inc(sem("attn_out_mm"), 1)
            if stop > 4:
                features(5)
                for t in range(NT):
                    last = rowprod(yslot(t, 3), w2T, t)
                last.then_inc(sem("wg_y_mm"), 1)
                pe.wait_ge(sem("wg_y"), 1)
                for i in range(NT):
                    spmm(CW, lambda j: U[:, j, :], i, PS[0:P, i, 0:D]).then_inc(sem("wg_mm"), 1)
            if stop > 5:
                features(6)
                experts("moe2_", E2, wg2, b2x2)
            if stop > 6:
                features(7)
                for t in range(NT):
                    last = rowprod(yslot(t, 3), l3w, t)
                last.then_inc(sem("ng_y_mm"), 1)
                pe.wait_ge(sem("ng_y"), 1)
                for i in range(NT):
                    spmm(CT, lambda j: U[:, j, :], i, PS[0:P, i, 0:D], stop_=False)
                    pe.matmul(PS[0:P, i, 0:D], AET[:, rows(i)], l3we[:], start=False, stop=True,
                              skip_group_check=True).then_inc(sem("ng_mm"), 1)
            if stop > 7:
                features(8)
                pe.wait_ge(sem("tree_in"), 16 * 5)
                w1rk = w1r.rearrange("p o (f k) -> p o k f", k=KD)
                for k in range(KD):
                    pe.transpose(PS[:, 3, k * 256:k * 256 + 128], w1rk[:, 0, k, :], ident[:])
                    last = pe.transpose(PS[:, 3, k * 256 + 128:k * 256 + 255], w1rk[0:127, 1, k, :], ident[0:127, 0:127])
                last.then_inc(sem("tree_products"), 1)
                pe.wait_ge(sem("tree_operands"), 1)
                for t in range(NT):
                    last = rowprod(yslot(t, 4)[:, 0:NODES], w1T, t, n=slice(0, NODES))
                last.then_inc(sem("tree_products"), 1)
                pe.wait_ge(sem("tree_operands"), 2)
                for o in range(2):
                    for t in range(NT):
                        last = pe.transpose(PS[0:128 - o, 2 * o + t // 4, rows(t % 4)], CXI[:, t, o * 128:o * 128 + 128 - o], ident[0:P, 0:P])
                last.then_inc(sem("tree_products"), 1)
                pe.wait_ge(sem("tree_leaves"), 1)
                for t in range(NT):
                    pe.matmul(PS[0:P, 4, 0:LEAVES], ones_b[:], LB[:, t, :], start=(t == 0), stop=False, skip_group_check=True)
                    pe.matmul(PS[0:P, 4, 0:LEAVES], ones_b[:], GB[:, t, :], start=False, stop=(t == NT - 1), skip_group_check=True)
                for t in range(NT):
                    place = PS[0:P, 5 + t // 4, (t % 4) * LEAVES:(t % 4) * LEAVES + LEAVES]
                    for u in range(NT):
                        pe.matmul(place, ones_b[:], GB[:, u, :], start=(u == 0), stop=False, skip_group_check=True)
                    for u in range(t):
                        pe.matmul(place, ones_b[:], LB[:, u, :], start=False, stop=False, skip_group_check=True)
                    last = pe.matmul(place, upper_b[:], LB[:, t, :], start=False, stop=True, skip_group_check=True)
                last.then_inc(sem("tree_places"), 1)
                pe.wait_ge(sem("tree_operands"), 3)
                for t in range(NT):
                    for o in range(2):
                        last = pe.matmul(yslot(t, 0), COT[0:128 - o, o, rows(t)], b2s[0:128 - o, o, :], start=(o == 0), stop=(o == 1))
                last.then_inc(sem("tree_products"), 1)
                pe.wait_ge(sem("tree_operands"), 4)
                for r in range(NT):
                    for t in range(NT):
                        pe.matmul(PS[0:P, r, :], PM[:, t, rows(r)], CXI[:, t, :], start=(t == 0), stop=(t == NT - 1))
                for k in range(KD):
                    if k:
                        pe.wait_ge(sem("tree_sorted_out"), 1)
                    for bank, c0, c1 in bank_pair(5):
                        for t in range(NT):
                            last = pe.matmul(PS[:, bank, 0:c1 - c0], XNk[:, t, k, :], PM[:, t, c0:c1], start=(t == 0), stop=(t == NT - 1))
                    last.then_inc(sem("tree_sorted"), 1)
                pe.wait_ge(sem("tree_sorted_out"), 2)
                pe.wait_ge(sem("tree_rows_out"), 1)
                for u in range(TU):
                    pe.sem_inc(sem(f"tree_added{u}"), 1)
                    pe.sem_inc(sem(f"tree_w_free{u}"), 1)
                done = 0
                for t in range(NT):
                    n = pe.value_load(tcnt[t:t + 1, 0:1], min_val=1, max_val=STEPS // TU)
                    with pe.Fori(0, n) as i:
                        for u in range(TU):
                            pe.wait_ge(sem(f"tree_w_in{u}"), (i + done) * 16 + 16)
                            pe.wait_ge(sem(f"tree_added{u}"), i + done + 1)
                            rowprod(PS[0:P, u, 0:D], TW[:, u], t).then_inc(sem(f"tree_w_free{u}"), 1)
                    done = n + done

        @block.vector
        def _(_v):
            def layer_norm(li, src, dst, signal=True):
                for t in range(NT):
                    v.bn_stats(out=bst[:, t, :], in_=src[:, t, :])
                v.drain()
                for t in range(NT):
                    v.bn_aggr(out=mv[:, t, :], in_=bst[:, t, :])
                v.drain()
                v.tensor_scalar(var5[:], mv[:, :, 1], EPS, None, ALU.add).then_inc(sem("var_ready"), 1)
                v.wait_ge(sem("std_ready"), li + 1)
                v.reciprocal(rstd[:], std5[:])
                v.drain()
                for t in range(NT):
                    i = v.tensor_scalar(dst[:, t, :], src[:, t, :], mv[:, t, 0:1], rstd[:, t:t + 1], ALU.subtract, ALU.mult)
                    if signal:
                        i.then_inc(sem("xn_ready"), 1)

            def features(fi):
                v.wait_ge(sem("xt_mm"), 3 * fi + 2)
                v.tensor_copy(XT[:, 1, 0:500], PS[:, 1, 0:500]).then_inc(sem("xt_ready"), 1)
                v.wait_ge(sem("xt_mm"), 3 * fi + 3)
                v.tensor_copy(XT[:, :, 500:N], PS[:, 2, 0:2 * P].rearrange("p (k n) -> p k n", k=2)).then_inc(sem("xt_ready"), 1)

            def load_range(t):
                return (v.value_load(rng[0:1, 0, t:t + 1], min_val=0, max_val=PAIRS - 1),
                        v.value_load(rng[0:1, 1, t:t + 1], min_val=1, max_val=PAIRS),
                        v.value_load(rng[0:1, 2, t:t + 1], min_val=0, max_val=PAIRS * (NT + 1) + 1))

            def edges():
                v.wait_ge(sem("edges_in"), 64)
                for i in range(2):
                    v.tensor_copy(ef[:, i, :], ei[:, i, :])
                v.tensor_copy(ef[:, 2, :], ei[:, 2, :])
                v.drain()
                v.scalar_tensor_tensor(out=ef[:, 2, :], in0=ef[:, 2, :], scalar=float(N), in1=ef[:, 0, :], op0=ALU.mult, op1=ALU.add)
                v.tensor_reduce(red[:, 0:1], ef[:, 1, :], AX.X, ALU.min)
                v.tensor_reduce(red[:, 1:2], ef[:, 1, :], AX.X, ALU.max)
                v.drain().then_inc(sem("edge_rows"), 1)
                v.wait_ge(sem("consts"), 1)
                v.tensor_copy(io16[:], iot)
                v.tensor_copy(ioe[:], iot[:, 0:E2])
                v.tensor_copy(ioleaf[:], iot[:, 0:STEPS])
                v.tensor_copy(pcol[:, 0:1], pcoli[:])
                v.drain()
                v.tensor_scalar(pcol[:, 1:2], pcol[:, 0:1], float(P), None, ALU.mult)
                THi = TH.bitcast(I32)
                v.tensor_copy(TH, THi)
                v.wait_ge(sem("edge_cols"), 1)
                v.tensor_copy(EF[:], PS[0:P, 0, 0:4 * CH].rearrange("p (i c) -> p i c", i=4))
                v.tensor_reduce(mm_[:, 0, :], PS[0:1, 1, 0:CH].rearrange("p (j b) -> p j b", b=2), AX.X, ALU.min)
                v.tensor_reduce(mm_[:, 1, :], PS[0:1, 1, CH:2 * CH].rearrange("p (j b) -> p j b", b=2), AX.X, ALU.max)
                v.drain()
                v.tensor_copy(GI[:], EF[:, 2, :])
                v.drain().then_inc(sem("edge_fields"), 1)
                w = EF[:, 3, :]
                v.tensor_copy(wtb, w)
                v.drain()
                v.tensor_copy(WP3[:, 0, :], wtb)
                v.drain()
                v.tensor_tensor(wtmp[:, 0, :], w, WP3[:, 0, :], ALU.subtract)
                v.drain()
                v.tensor_copy(wtb, wtmp[:, 0, :])
                v.drain()
                v.tensor_copy(WP3[:, 1, :], wtb)
                v.drain()
                v.tensor_tensor(WP3[:, 2, :], wtmp[:, 0, :], WP3[:, 1, :], ALU.subtract)
                def over_tiles(x):
                    return x.unsqueeze(1).to_broadcast([1, NT, PAIRS])
                v.tensor_tensor(tou[:, 0], over_tiles(mm_[:, 0, :]), TH[:, 1], ALU.is_lt)
                v.tensor_tensor(tou[:, 1], over_tiles(mm_[:, 1, :]), TH[:, 0], ALU.is_ge)
                v.drain()
                v.tensor_tensor(tou[:, 0], tou[:, 0], tou[:, 1], ALU.mult)
                v.drain()
                v.tensor_scalar(tou[:, 1], tou[:, 0], -1000.0, 1000.0, ALU.mult, ALU.add)
                v.drain()
                v.tensor_tensor(tou[:, 1], tou[:, 1], TH[:, 2], ALU.add)
                v.scalar_tensor_tensor(out=tou[:, 2], in0=TH[:, 2], scalar=1.0, in1=tou[:, 0], op0=ALU.add, op1=ALU.mult)
                v.drain()
                v.tensor_reduce(lh[:, 0, :], tou[:, 1], AX.X, ALU.min)
                v.tensor_reduce(lh[:, 1, :], tou[:, 2], AX.X, ALU.max)
                v.drain()
                v.tensor_scalar(lh[:, 0, :], lh[:, 0, :], float(PAIRS - 1), None, ALU.min)
                v.memset(lh[:, 2, :], 0.0)
                v.drain()
                v.scalar_tensor_tensor(out=lh[:, 1, :], in0=lh[:, 0, :], scalar=1.0, in1=lh[:, 1, :], op0=ALU.add, op1=ALU.max)
                v.drain()
                v.tensor_tensor(lh[:, 3, :], lh[:, 1, :], lh[:, 0, :], ALU.subtract)
                for t in range(NT - 1):
                    v.drain()
                    v.tensor_tensor(lh[:, 2, t + 1:t + 2], lh[:, 2, t:t + 1], lh[:, 3, t:t + 1], ALU.add)
                v.drain()
                v.tensor_tensor(lh[:, 2, :], lh[:, 2, :], lh[:, 0, :], ALU.subtract)
                v.drain()
                v.tensor_scalar(lh[:, 2, :], lh[:, 2, :], float(PAIRS + 1), None, ALU.add)
                v.drain()
                v.tensor_copy(rng[:], lh[:, 0:3, :])
                v.drain().then_inc(sem("ranges"), 1)
                v.wait_ge(sem("prep_mm"), 1)
                v.tensor_copy(b1T[:], PS[:, 2, 0:96])
                v.tensor_copy(bxT[:], PS[:, 2, 96:100])
                v.tensor_copy(w2T[:], PS[:, 3, :].rearrange("p (k o) -> p k o", k=KD))
                v.drain().then_inc(sem("prep_out"), 1)
                for b in range(2):
                    v.sem_inc(sem(f"oh_ready{b}"), PAIRS)
                for t in range(NT):
                    lo, hi, step = load_range(t)
                    own = io16[:, t * P:t * P + P]
                    with v.Fori(lo, hi) as j:
                        for b in range(2):
                            v.wait_ge(sem(f"oh_free{b}"), j + step)
                            col = bass.ds(j * 2 + b, 1)
                            v.tensor_scalar(OHS[:, b, 0:N], io16[:], EF[:, 0, col], None, ALU.is_equal)
                            v.tensor_scalar(OHB[:, b, 0, 0:P], own, EF[:, 1, col], None, ALU.is_equal)
                            for i in range(3):
                                v.tensor_scalar(OHB[:, b, i + 1, 0:P], own, EF[:, 1, col], WP3[:, i, col], ALU.is_equal, ALU.mult)
                            v.tensor_scalar(OHF[:, b, :], own, EF[:, 1, col], None, ALU.is_equal).then_inc(sem(f"oh_ready{b}"), 1)
                v.wait_ge(sem("edge_tile_copied"), NT)
                v.tensor_reduce(sc5[:, 0, :], C[:], AX.X, ALU.add)
                for t in range(NT):
                    v.tensor_tensor(OHF[:, 0, :], C[:, t, t * P:t * P + P], ident[0:P, 0:P], ALU.mult)
                    v.drain()
                    v.tensor_reduce(dg5[:, t:t + 1], OHF[:, 0, :], AX.X, ALU.add)
                    v.drain()
                v.wait_ge(sem("ct_copied"), NT)
                v.tensor_reduce(dis[:], CT[:], AX.X, ALU.add)
                v.drain()
                v.tensor_scalar(sc5[:, 1, :], dis[:], 1.0, None, ALU.add)
                v.tensor_scalar(sc5[:, 2, :], dis[:], 1.0, None, ALU.max)
                v.tensor_scalar(sc5[:, 3, :], sc5[:, 0, :], 1.0, None, ALU.max)
                v.drain().then_inc(sem("degrees"), 1)
                v.wait_ge(sem("degree_roots"), 1)
                v.reciprocal(dis[:], sc5[:, 1, :])
                v.reciprocal(nout[:], sc5[:, 2, :])
                v.reciprocal(nin[:], sc5[:, 3, :])
                v.drain()
                v.tensor_tensor(q5[:], dis[:], dis[:], ALU.mult)
                v.drain()
                v.scalar_tensor_tensor(out=q5[:], in0=dg5[:], scalar=1.0, in1=q5[:], op0=ALU.add, op1=ALU.subtract)
                v.drain()

            def relational(layer):
                with v.Fori(0, R // 2) as i:
                    for b in range(2):
                        v.wait_ge(sem(f"rel_mm{b}"), i + (layer * (R // 2) + 1))
                        v.wait_ge(sem(f"xw_stored{b}"), i * 16 + (layer * (R // 2) + 1) * 16)
                        v.tensor_copy(XW[:, b, 4, :], PS[0:P, 3 * b + 2, 0:D]).then_inc(sem(f"xw_copied{b}"), 1)

                for b in range(2):
                    v.sem_inc(sem(f"seg{layer}_ready{b}"), PAIRS)

                def finish(t):
                    v.wait_ge(sem(f"seg{layer}_tile"), t + 1)
                    if layer == 0:
                        v.tensor_tensor(XN[:, t, :], PS[0:P, t, 0:D], bias[:, 0, :], ALU.add)
                        v.drain()
                        v.tensor_scalar(XN[:, t, :], XN[:, t, :], 0.0, None, ALU.max).then_inc(sem("xn_ready"), 1)
                    else:
                        v.tensor_tensor(XN[:, t, :], PS[0:P, t, 0:D], bias[:, 1, :], ALU.add)
                        v.drain()
                        v.tensor_tensor(X[:, t, :], X[:, t, :], XN[:, t, :], ALU.add)
                for t in range(NT):
                    lo, hi, step = load_range(t)
                    with v.Fori(lo, hi) as j:
                        for b in range(2):
                            v.wait_ge(sem(f"seg{layer}_free{b}"), j + step)
                            v.tensor_scalar(OHG[:, b, :], io16[:, t * P:t * P + P], EF[:, 1, bass.ds(j * 2 + b, 1)], None,
                                            ALU.is_equal).then_inc(sem(f"seg{layer}_ready{b}"), 1)
                    if t:
                        finish(t - 1)
                finish(NT - 1)
                v.drain()

            def experts(tag, ne, bg, soft, acc):
                v.wait_ge(sem(tag + "route_mm"), 1)
                v.tensor_tensor(gate[:, :, 0:ne], PS[0:P, 7, 0:NT * ne].rearrange("p (t e) -> p t e", e=ne),
                                bg[:].unsqueeze(1).to_broadcast([P, NT, ne]), ALU.add)
                v.drain()
                for t in range(NT):
                    v.max(gmax[:, t, :], gate[:, t, 0:ne])
                v.drain()
                for t in range(NT):
                    v.max_index(gidx[:, t, :], gmax[:, t, :], gate[:, t, 0:ne])
                v.drain()
                v.tensor_copy(gidf[:], gidx[:, :, 0:2])
                if soft:
                    v.tensor_tensor(gwt[:, :, 0], gmax[:, :, 1], gmax[:, :, 0], ALU.subtract).then_inc(sem("top2_diff"), 1)
                    v.wait_ge(sem("top2_exp"), 1)
                    v.tensor_scalar(gwt[:, :, 2], gwt[:, :, 1], 1.0, None, ALU.add)
                    v.drain()
                    v.reciprocal(gwt[:, :, 2], gwt[:, :, 2])
                    v.drain()
                    v.tensor_tensor(gwt[:, :, 3], gwt[:, :, 1], gwt[:, :, 2], ALU.mult)
                else:
                    v.memset(gwt[:], 1.0)
                v.drain()
                for t in range(NT):
                    v.tensor_scalar(M[:, t, 0:ne], ioe[:, 0:ne], gidf[:, t, 0:1], gwt[:, t, 2:3], ALU.is_equal, ALU.mult)
                    v.tensor_scalar(gate[:, t, 0:ne], ioe[:, 0:ne], gidf[:, t, 1:2], gwt[:, t, 3:4], ALU.is_equal, ALU.mult)
                v.drain()
                v.tensor_tensor(M[:, :, 0:ne], M[:, :, 0:ne], gate[:, :, 0:ne], ALU.add).then_inc(sem(tag + "route"), 1)
                v.wait_ge(sem(tag + "route_mm"), 2)
                v.tensor_copy(MT[0:ne, 0:500], PS[0:ne, 5, 0:500])
                v.tensor_copy(MT[0:ne, 500:N], PS[0:ne, 6, 0:P])
                v.drain().then_inc(sem(tag + "route"), 1)
                v.wait_ge(sem(tag + "route_mm"), 3)
                for g, tiles in enumerate(((0, 1), (2, 3), (4,))):
                    for t in tiles:
                        last = v.tensor_tensor(acc[:, t, :], yslot(t, 4), acc[:, t, :], ALU.add)
                    last.then_inc(sem(tag + "added"), 1)
                with v.Fori(0, ne // 2) as i:
                    for b in range(2):
                        for g, tiles in enumerate(((0, 1), (2, 3), (4,))):
                            v.drain()
                            v.wait_ge(sem(tag + "y_mm"), i * 6 + (b * 3 + g + 1))
                            for t in tiles:
                                last = v.scalar_tensor_tensor(out=acc[:, t, :], in0=yslot(t, 4), scalar=M[:, t, bass.ds(i * 2 + b, 1)],
                                                              in1=acc[:, t, :], op0=ALU.mult, op1=ALU.add)
                            last.then_inc(sem(tag + "added"), 1)
                v.drain()

            def bank_tiles(base, n=D):
                for g, (t0, t1) in enumerate(((0, 2), (2, 4), (4, 5))):
                    yield t0, t1, PS[0:P, base + g, 0:(t1 - t0) * D].rearrange("p (t d) -> p t d", d=D)[:, :, 0:n]

            edges()
            v.wait_ge(sem("x_in"), 16)
            v.wait_ge(sem("weights_in"), WEIGHTS_IN)
            if stop > 0:
                layer_norm(0, X, XN)
                features(0)
                relational(0)
                features(1)
                relational(1)
            if stop > 1:
                layer_norm(1, X, XN)
                features(2)
                experts("moe0_", E0, bg0, False, X)
            if stop > 2:
                layer_norm(2, X, XN)
                features(3)
                for w in range(4):
                    v.wait_ge(sem("cheb_mm"), w + 1)
                    for t0, t1, src in bank_tiles(3 if w % 2 == 0 else 0):
                        last = v.tensor_copy(Y[:, w, t0:t1, :], src)
                    last.then_inc(sem("cheb_y"), 1)
                terms = [(Y[:, 3], Y[:, 2], None, 2.0, S1), (S1, Y[:, 1], Y[:, 3], 2.0, S2), (S2, Y[:, 0], S1, 1.0, U)]
                v.drain()
                for r, (x, y, z, f, dst) in enumerate(terms):
                    for t in range(NT):
                        last = v.tensor_scalar(U[:, t, :], x[:, t, :], dis[:, t:t + 1], None, ALU.mult)
                    last.then_inc(sem("cheb_u"), 1)
                    v.tensor_scalar(sc5[:, 0, :], q5[:], f, None, ALU.mult)
                    v.tensor_scalar(sc5[:, 1, :], dis[:], -f, None, ALU.mult)
                    if z is not None:
                        v.tensor_tensor(y, y, z, ALU.subtract)
                    v.drain()
                    for t in range(NT):
                        v.scalar_tensor_tensor(out=y[:, t, :], in0=x[:, t, :], scalar=sc5[:, 0, t:t + 1], in1=y[:, t, :], op0=ALU.mult, op1=ALU.add)
                    v.drain()
                    v.wait_ge(sem("cheb_spmm"), r + 1)
                    for t in range(NT):
                        v.scalar_tensor_tensor(out=dst[:, t, :], in0=PS[0:P, t, 0:D], scalar=sc5[:, 1, t:t + 1], in1=y[:, t, :], op0=ALU.mult, op1=ALU.add)
                    v.drain()
                v.tensor_tensor(X[:], X[:], U, ALU.add)
                v.drain()
                v.tensor_tensor(X[:], X[:], bias[:, 2, :].unsqueeze(1).to_broadcast([P, NT, D]), ALU.add)
                v.drain()
            if stop > 3:
                layer_norm(3, X, XN)
                features(4)
                v.tensor_scalar(rtemp[:], temp[:], 0.1, 5.0, ALU.max, ALU.min)
                v.drain()
                v.reciprocal(rtemp[:], rtemp[:])
                v.memset(blk, 0.0)
                v.drain()
                for h in range(2):
                    v.memset(blk[h * HD:h * HD + HD, h * HD:h * HD + HD], 1.0)
                v.memset(ABD, 0.0)
                for m in range(HP):
                    v.wait_ge(sem("xmt_mm"), m + 1)
                    for bank, c0, c1 in bank_pair((m % 2) * 2):
                        last = v.tensor_scalar(XMT[:, m, c0:c1], PS[:, bank, 0:c1 - c0], bxT[:, m:m + 1], None, ALU.add)
                    last.then_inc(sem("xmt"), 1)
                for t in range(NT):
                    v.wait_ge(sem("fx_mm"), t + 1)
                    v.tensor_tensor(FX[:, t, :], PS[0:P, 4 + t % 2, :], bfx[:], ALU.add).then_inc(sem("fx"), 1)
                for t in range(NT):
                    v.wait_ge(sem("logit_mm"), t + 1)
                    sw = SW[:, t, :].rearrange("p (h g) -> p h g", h=8)
                    v.tensor_tensor(sw, PS[0:P, 6 + t % 2, :].rearrange("p (h g) -> p h g", h=8),
                                    bsl[:].unsqueeze(1).to_broadcast([P, 8, HD]), ALU.add)
                    v.drain()
                    v.tensor_tensor(sw, sw, rtemp[:].unsqueeze(2).to_broadcast([P, 8, HD]), ALU.mult)
                    v.drain()
                    v.tensor_reduce(hm[:, t, :], sw, AX.X, ALU.max)
                    v.drain()
                    v.tensor_tensor(sw, sw, hm[:, t, :].unsqueeze(2).to_broadcast([P, 8, HD]), ALU.subtract).then_inc(sem("slice_shifted"), 1)
                for t in range(NT):
                    sw = SW[:, t, :].rearrange("p (h g) -> p h g", h=8)
                    v.wait_ge(sem("slice_exp"), t + 1)
                    v.tensor_reduce(hs[:, t, :], sw, AX.X, ALU.add)
                    v.drain()
                    v.reciprocal(hr[:, t, :], hs[:, t, :])
                    v.drain()
                    v.tensor_tensor(sw, sw, hr[:, t, :].unsqueeze(2).to_broadcast([P, 8, HD]), ALU.mult).then_inc(sem("slice_w"), 1)
                v.wait_ge(sem("attn_products"), 1)
                v.tensor_scalar(rn, PS[:, 1, :], 1e-5, None, ALU.add)
                v.drain()
                v.reciprocal(rn, rn)
                v.drain()
                blk4 = blk.unsqueeze(1).to_broadcast([128, HP, 128])
                rn4 = rn.rearrange("p (m g) -> p m g", m=HP)
                v.tensor_tensor(rn4, rn4, blk4, ALU.mult)
                v.drain()
                v.tensor_tensor(STT, PS[:, 0, :].rearrange("p (m g) -> p m g", m=HP), rn4, ALU.mult).then_inc(sem("attn_operands"), 1)
                for m in range(HP):
                    v.wait_ge(sem("swt_mm"), m + 1)
                    b0 = 2 + (m % 2) * 2
                    v.tensor_copy(SWT[:, m, 0:500], PS[:, b0, 0:500])
                    v.tensor_copy(SWT[:, m, 500:N], PS[:, b0 + 1, 0:P]).then_inc(sem("swt"), 1)
                v.wait_ge(sem("attn_products"), 2)
                for dst, bank in ((QT, 2), (KT, 3), (VV, 4)):
                    last = v.tensor_copy(dst, PS[:, bank, :].rearrange("p (m g) -> p m g", m=HP))
                last.then_inc(sem("attn_operands"), 1)
                v.wait_ge(sem("attn_products"), 3)
                for h in range(2):
                    hr_ = slice(h * HD, h * HD + HD)
                    v.tensor_copy(AT[hr_], PS[hr_, 0, :].rearrange("p (m g) -> p m g", m=HP)[:, :, hr_])
                v.drain()
                v.tensor_reduce(am[:, 0, :], AT, AX.X, ALU.max)
                v.drain()
                v.tensor_tensor(AT, AT, am[:, 0, :].unsqueeze(2).to_broadcast([128, HP, HD]), ALU.subtract).then_inc(sem("attn_shifted"), 1)
                v.wait_ge(sem("attn_exp"), 1)
                v.tensor_reduce(am[:, 1, :], AT, AX.X, ALU.add)
                v.drain()
                v.reciprocal(am[:, 2, :], am[:, 1, :])
                v.drain()
                for h in range(2):
                    hr_ = slice(h * HD, h * HD + HD)
                    last = v.tensor_tensor(ABD[hr_, :, hr_], AT[hr_], am[hr_, 2, :].unsqueeze(2).to_broadcast([HD, HP, HD]), ALU.mult)
                last.then_inc(sem("attn_operands"), 1)
                v.wait_ge(sem("attn_products"), 4)
                v.tensor_copy(ATT, PS[:, 1, :].rearrange("p (m g) -> p m g", m=HP)).then_inc(sem("attn_operands"), 1)
                v.wait_ge(sem("attn_products"), 5)
                v.tensor_copy(OS, PS[:, 2, :].rearrange("p (m g) -> p m g", m=HP)).then_inc(sem("attn_operands"), 1)
                for m in range(HP):
                    v.wait_ge(sem("oxt_mm"), m + 1)
                    for bank, c0, c1 in bank_pair(4 if m % 2 == 0 else 0):
                        last = v.tensor_copy(OXT[:, m, c0:c1], PS[:, bank, 0:c1 - c0])
                    last.then_inc(sem("oxt"), 1)
                v.tensor_tensor(X[:], X[:], bias[:, 3, :].unsqueeze(1).to_broadcast([P, NT, D]), ALU.add)
                v.drain()
                for t in range(NT):
                    v.wait_ge(sem("attn_out_mm"), t + 1)
                    v.tensor_tensor(X[:, t, :], PS[0:P, t, 0:D], X[:, t, :], ALU.add)
                v.drain()
            if stop > 4:
                layer_norm(4, X, XN)
                features(5)
                v.wait_ge(sem("wg_y_mm"), 1)
                for t0, t1, src in bank_tiles(3):
                    last = v.tensor_copy(U[:, t0:t1, :], src)
                last.then_inc(sem("wg_y"), 1)
                v.tensor_tensor(X[:], X[:], bias[:, 4, :].unsqueeze(1).to_broadcast([P, NT, D]), ALU.add)
                v.drain()
                for t in range(NT):
                    v.wait_ge(sem("wg_mm"), t + 1)
                    v.tensor_tensor(X[:, t, :], PS[0:P, t, 0:D], X[:, t, :], ALU.add)
                v.drain()
            if stop > 5:
                layer_norm(5, X, XN)
                features(6)
                experts("moe2_", E2, bg2, True, XN)
                layer_norm(6, XN, XN, signal=False)
                v.drain()
                v.tensor_tensor(XN[:], XN[:], bias[:, 5, :].unsqueeze(1).to_broadcast([P, NT, D]), ALU.mult)
                v.tensor_tensor(X[:], X[:], bias[:, 6, :].unsqueeze(1).to_broadcast([P, NT, D]), ALU.add)
                v.drain()
                v.tensor_tensor(X[:], X[:], XN[:], ALU.add)
                v.drain()
            if stop > 6:
                layer_norm(7, X, XN)
                features(7)
                v.wait_ge(sem("ng_y_mm"), 1)
                for t in range(NT):
                    last = v.tensor_scalar(U[:, t, :], yslot(t, 3), nout[:, t:t + 1], None, ALU.mult)
                last.then_inc(sem("ng_y"), 1)
                for t in range(NT):
                    v.wait_ge(sem("ng_mm"), t + 1)
                    v.scalar_tensor_tensor(out=S1[:, t, :], in0=PS[0:P, t, 0:D], scalar=nin[:, t:t + 1], in1=bias[:, 7, :], op0=ALU.mult, op1=ALU.add)
                v.drain()
                v.scalar_tensor_tensor(out=X[:], in0=S1, scalar=0.0, in1=X[:], op0=ALU.max, op1=ALU.add)
                v.drain().then_inc(sem("arena_free_for_tree"), 1)
            if stop > 7:
                layer_norm(8, X, XN)
                features(8)
                v.wait_ge(sem("tree_products"), 1)
                v.tensor_copy(w1T[:, :, 0:NODES], PS[:, 3, :].rearrange("p (k j) -> p k j", k=KD)[:, :, 0:NODES]).then_inc(sem("tree_operands"), 1)
                v.wait_ge(sem("tree_products"), 2)
                for t0, t1, src in bank_tiles(4, NODES):
                    v.tensor_tensor(SCO[:, t0:t1, 0:NODES], src, b1s[:, 0:NODES].unsqueeze(1).to_broadcast([P, t1 - t0, NODES]), ALU.add)
                v.drain().then_inc(sem("tree_scores"), 1)
                v.memset(TM[:, :, 0:1], 1.0)
                for d in range(DEPTH - 1):
                    n0, n1 = 2 ** d - 1, 2 ** (d + 1) - 1
                    kids = TM[:, :, n1:2 * n1 + 1].rearrange("p t (j c) -> p t j c", c=2)
                    v.drain()
                    for t in range(NT):
                        v.scalar_tensor_tensor(out=kids[:, t, :, 1], in0=SCO[:, t, n0:n1], scalar=0.0, in1=TM[:, t, n0:n1], op0=ALU.is_gt, op1=ALU.mult)
                        v.scalar_tensor_tensor(out=kids[:, t, :, 0], in0=SCO[:, t, n0:n1], scalar=0.0, in1=TM[:, t, n0:n1], op0=ALU.is_le, op1=ALU.mult)
                v.drain()
                v.wait_ge(sem("tree_gelu"), 1)
                v.tensor_tensor(CXI[:, :, 0:NODES], CXI[:, :, 0:NODES], TM[:, :, 0:NODES], ALU.mult).then_inc(sem("tree_operands"), 1)
                leaf = TM[:, :, LEAVES - 1:NODES]
                v.tensor_copy(LB, leaf)
                v.tensor_tensor(tl, leaf, ioleaf[:, 0:LEAVES].unsqueeze(1).to_broadcast([P, NT, LEAVES]), ALU.mult)
                v.drain()
                v.tensor_reduce(lid[:, 0, :], tl, AX.X, ALU.add)
                v.drain()
                for t in range(NT):
                    v.tensor_scalar(GB[:, t, :], ioleaf[:, 0:LEAVES], lid[:, 0, t:t + 1], None, ALU.is_gt)
                v.drain().then_inc(sem("tree_leaves"), 1)
                v.wait_ge(sem("tree_products"), 3)
                for o in range(2):
                    v.tensor_copy(COT[0:128 - o, o, 0:500], PS[0:128 - o, 2 * o, 0:500])
                    last = v.tensor_copy(COT[0:128 - o, o, 500:N], PS[0:128 - o, 2 * o + 1, 0:P])
                last.then_inc(sem("tree_operands"), 1)
                v.wait_ge(sem("tree_places"), 1)
                for i in range(2):
                    v.tensor_scalar(tls[:, i, :], PS[0:NT, 4, 0:LEAVES], pcol[0:NT, 1:2], float(i * (P - 1)), ALU.subtract, ALU.is_le)
                for t in range(NT):
                    v.tensor_tensor(tl[:, t, :], PS[0:P, 5 + t // 4, (t % 4) * LEAVES:(t % 4) * LEAVES + LEAVES], leaf[:, t, :], ALU.mult)
                v.drain()
                v.tensor_reduce(lid[:, 1, :], tl, AX.X, ALU.add)
                v.drain()
                for t in range(NT):
                    v.tensor_scalar(PM[:, t, :], io16[:], lid[:, 1, t:t + 1], None, ALU.is_equal)
                    v.tensor_scalar(CXI[:, t, NODES:D], pcol[:, 0:1], float(t * P), None, ALU.add)
                v.wait_ge(sem("tree_products"), 4)
                for t in range(NT):
                    last = v.tensor_tensor(CXI[:, t, D:2 * D], yslot(t, 0), X[:, t, :], ALU.add)
                last.then_inc(sem("tree_operands"), 1)
                v.tensor_reduce(tb[:, 0, 0:2], tls, AX.X, ALU.add)
                v.drain()
                for d in range(DEPTH):
                    v.tensor_copy(tbi[:, 0, d, :], tb[:, 0, 0:2])
                v.drain()
                for d in range(DEPTH):
                    v.tensor_scalar(tbi[:, 1, d, :], tbi[:, 0, d, :], DEPTH - 1 - d, None, ALU.arith_shift_right)
                v.drain()
                v.tensor_copy(tb[:, 1, 0:8], tbi[:, 1, :, 0])
                v.tensor_copy(tb[:, 2, 0:8], tbi[:, 1, :, 1])
                v.memset(tb[:, 4, 0:1], 0.0)
                v.drain()
                v.scalar_tensor_tensor(out=tb[:, 3, 0:8], in0=tb[:, 2, 0:8], scalar=1.0, in1=tb[:, 1, 0:8], op0=ALU.add, op1=ALU.subtract)
                for d in range(DEPTH):
                    v.drain()
                    v.tensor_tensor(tb[:, 4, d + 1:d + 2], tb[:, 4, d:d + 1], tb[:, 3, d:d + 1], ALU.add)
                v.drain()
                v.tensor_tensor(tb[:, 5, 0:8], tb[:, 1, 0:8], tb[:, 4, 0:8], ALU.subtract)
                v.drain()
                v.tensor_tensor(tb[:, 5, 0:8], tb[:, 5, 0:8], levelk[:], ALU.add)
                v.drain()
                v.tensor_tensor(tb[:, 6, 1:8], tb[:, 5, 1:8], tb[:, 5, 0:7], ALU.subtract)
                v.tensor_copy(tb[:, 6, 0:1], tb[:, 5, 0:1])
                v.memset(tb[:, 6, 8:9], 1000.0)
                v.drain()
                for d in range(9):
                    v.tensor_scalar(tn[:, d, :], ioleaf[0:NT, :], tb[:, 4, d:d + 1], tb[:, 6, d:d + 1], ALU.is_ge, ALU.mult)
                v.tensor_scalar(tls[:, 0, 0:STEPS // TU], ioleaf[0:NT, 0:STEPS // TU], float(TU), tb[:, 4, 8:9], ALU.mult, ALU.is_lt)
                v.drain()
                v.tensor_reduce(tb[:, 7, 0:1], tls[:, 0, 0:STEPS // TU], AX.X, ALU.add)
                for d in range(1, 9):
                    v.tensor_tensor(tn[:, 0, :], tn[:, 0, :], tn[:, d, :], ALU.add)
                    v.drain()
                v.tensor_tensor(tn[:, 0, :], tn[:, 0, :], ioleaf[0:NT, :], ALU.add)
                v.drain()
                v.tensor_copy(tcnt[:, 0:1], tb[:, 7, 0:1])
                v.tensor_scalar(tn[:, 1, :], tn[:, 0, :], float(NODES - 1), None, ALU.min)
                v.tensor_scalar(tn[:, 2, :], tn[:, 0, :], float(NODES), None, ALU.min)
                v.drain()
                v.tensor_copy(tnode, tn[:, 1:3, :])
                v.drain().then_inc(sem("tree_lists"), 1)
                v.wait_ge(sem("tree_sorted"), 1)
                for t in (2, 3, 4):
                    v.tensor_copy(CXS[:, t, :], PS[0:P, t, :])
                v.drain().then_inc(sem("tree_rows_out"), 1)
                v.wait_ge(sem("tree_sorted_out"), 2)
                v.tensor_copy(CS[:, :, 0:NODES], CXS[:, :, 0:NODES])
                v.memset(CS[:, :, NODES:D], 0.0)
                v.tensor_copy(sid, CXS[:, :, NODES])
                v.drain()
                done = 0
                for t in range(NT):
                    n = v.value_load(tcnt[t:t + 1, 0:1], min_val=1, max_val=STEPS // TU)
                    own = CXS[:, t, D:2 * D]
                    with v.Fori(0, n) as i:
                        for u in range(TU):
                            node = v.value_load(tnode[t:t + 1, 1, bass.ds(i * TU + u, 1)], min_val=0, max_val=NODES)
                            v.drain()
                            v.wait_ge(sem(f"tree_w_free{u}"), i + done + 2)
                            v.scalar_tensor_tensor(out=own, in0=PS[0:P, u, 0:D], scalar=CS[:, t, bass.ds(node, 1)],
                                                   in1=own, op0=ALU.mult, op1=ALU.add).then_inc(sem(f"tree_added{u}"), 1)
                    done = n + done
            v.drain().then_inc(sem("x_final"), 1)


_INS = ['x', 'src', 'dst', 'edge_attr_64', 'edge_type_8', 'edge_weight', 'L0_gnn_W1', 'L0_gnn_self_w1', 'L0_gnn_b1',
        'L0_gnn_W2', 'L0_gnn_self_w2', 'L0_gnn_b2', 'L0_ffn_Wg', 'L0_ffn_bg', 'L0_ffn_W1', 'L0_ffn_b1', 'L0_ffn_W2',
        'L0_ffn_b2', 'L1_gnn_weight', 'L1_gnn_bias', 'L1_ffn_W_fx', 'L1_ffn_b_fx', 'L1_ffn_W_x', 'L1_ffn_b_x',
        'L1_ffn_W_slice', 'L1_ffn_b_slice', 'L1_ffn_W_q', 'L1_ffn_W_k', 'L1_ffn_W_v', 'L1_ffn_W_out', 'L1_ffn_b_out',
        'L1_ffn_temperature', 'L2_gnn_W', 'L2_gnn_b', 'L2_ffn_gate_w', 'L2_ffn_gate_b', 'L2_ffn_w1', 'L2_ffn_b1',
        'L2_ffn_w2', 'L2_ffn_b2', 'L2_ffn_gamma', 'L2_ffn_beta', 'L3_gnn_weight', 'L3_gnn_bias', 'L3_ffn_w1s',
        'L3_ffn_b1s', 'L3_ffn_w2s', 'L3_ffn_b2s']


def kernel(**inputs):
    import numpy as _np
    import concourse.bacc as _bacc
    from concourse import mybir as _mybir
    from concourse.bass_utils import run_bass_kernel_spmd as _run

    nc = _bacc.Bacc("TRN2", target_bir_lowering=False, num_devices=1)
    arrays, args = {}, {}
    for name in _INS:
        x = _np.ascontiguousarray(inputs[name])
        arrays[f"in_{name}"] = x
        args[name] = nc.dram_tensor(f"in_{name}", x.shape, _mybir.dt.from_np(x.dtype), kind="ExternalInput").ap()
    out = nc.dram_tensor("out_x", (N, D), F32, kind="ExternalOutput").ap()
    build(nc, args, out)
    r = _run(nc, [arrays], core_ids=[0])
    return r.results[0]["out_x"]
```

```python
from contextlib import ExitStack

import concourse.bass as bass
from concourse import mybir

F32 = mybir.dt.float32
BF16 = mybir.dt.bfloat16
F16 = mybir.dt.float16
I32 = mybir.dt.int32
U32 = mybir.dt.uint32
ALU = mybir.AluOpType
ACT = mybir.ActivationFunctionType
AX = mybir.AxisListType

N = 625
D = 256
P = 125
NT = N // P
KD = D // 128
E = 10000
CH = E // P
G = 4
GROUPS = CH // G
R = 8
FE = 64
HD = 64
HP = 4
HID = 512
MH = HID // 128
E0, E2 = 8, 16
BS = 128
UB = 3
MAXB = 27
NODES = 255
DEPTH = 8
LEAVES = 2 ** (DEPTH - 1)
TU = 6
STEPS = 252 + 12
SLOTS = 4
EPS = 1e-5
HALF = (313, 312)


def build(nc, a, out, stop=99):
    v, pe, act, pool, sp = nc.vector, nc.tensor, nc.scalar, nc.gpsimd, nc.sync
    table = nc.dram_tensor("relation_table", (R * N, D), F32).ap()
    slots = {tag: nc.dram_tensor(tag + "slots", (MAXB * BS, D), F32).ap() for tag in ("moe0_", "moe2_")}

    with ExitStack() as ctx:
        def sb(name, shape, dt=F32):
            return ctx.enter_context(nc.sbuf_tensor(name, shape, dt))

        sems = {}

        def sem(name):
            if name not in sems:
                sems[name] = ctx.enter_context(nc.semaphore(name))
            return sems[name]

        PS = ctx.enter_context(nc.psum_tensor("PS", [128, 8, 512], F32))

        X = sb("X", [P, NT, D])
        XN = sb("XN", [P, NT, D])
        XT = sb("XT", [128, KD, N])
        XNk = XN[:].rearrange("p t (f k) -> p t k f", k=KD)
        graph = sb("graph", [P, 3 * NT * N])

        def matrix(i):
            return graph[:, i * NT * N:(i + 1) * NT * N].rearrange("p (t n) -> p t n", t=NT)

        C, CW, CT = matrix(0), matrix(1), matrix(2)
        EA = graph[:, NT * N:NT * N + CH * FE].rearrange("p (c f) -> p c f", c=CH)
        AE = graph[:, NT * N + CH * FE:NT * N + CH * FE + NT * FE].rearrange("p (t f) -> p t f", t=NT)
        AET = sb("AET", [FE, N])
        ident = sb("ident", [128, 128])
        zeros = sb("zeros", [128, 320], BF16)
        ones = sb("ones", [P, 128])
        io16 = sb("io16", [P, N], F16)
        ioe = sb("ioe", [P, E2])
        EF = sb("EF", [P, 4, CH])
        GI = sb("GI", [P, CH], I32)
        WP3 = sb("WP3", [P, 3, CH])
        gis = sb("gis", [P, 2, SLOTS], I32)
        rng = sb("rng", [1, 6, NT], I32)
        bst = sb("bst", [P, NT, 6])
        mv = sb("mv", [P, NT, 2])
        var5 = sb("var5", [P, NT])
        std5 = sb("std5", [P, NT])
        rstd = sb("rstd", [P, NT])
        dis = sb("dis", [P, NT])
        q5 = sb("q5", [P, NT])
        dg5 = sb("dg5", [P, NT])
        nout = sb("nout", [P, NT])
        nin = sb("nin", [P, NT])
        sc5 = sb("sc5", [P, 4, NT])
        selfw = sb("selfw", [128, 2, KD, D])
        wg0 = sb("wg0", [128, KD, E0])
        wg2 = sb("wg2", [128, KD, E2])
        cheb = sb("cheb", [128, 4, KD, D])
        wfx = sb("wfx", [128, KD, 512])
        wx = sb("wx", [128, KD, 512])
        wout = sb("wout", [128, HP, D])
        bd = sb("bd", [128, 4, 128])
        w2T = sb("w2T", [128, KD, D])
        l3w = sb("l3w", [128, KD, D])
        l3we = sb("l3we", [FE, D])
        b1T = sb("b1T", [128, 32 + 64])
        bxT = sb("bxT", [128, HP])
        bias = sb("bias", [P, 8, D])
        bfx = sb("bfx", [P, 512])
        bsl = sb("bsl", [P, HD])
        temp = sb("temp", [P, 8])
        rtemp = sb("rtemp", [P, 8])
        bg0 = sb("bg0", [P, E0])
        bg2 = sb("bg2", [P, E2])
        gate = sb("gate", [P, NT, E2])
        gmax = sb("gmax", [P, NT, 8])
        gidx = sb("gidx", [P, NT, 8], U32)
        gidf = sb("gidf", [P, NT, 2])
        gwt = sb("gwt", [P, NT, 4])
        one_hot = sb("one_hot", [P, 2, NT, E2])
        chosen = sb("chosen", [P, NT, E2], BF16)
        place = sb("place", [P, 2, NT, E2])
        blocks = sb("blocks", [P, 4, E2])
        blocksi = sb("blocksi", [P, E2], I32)
        slotf = sb("slotf", [P, 2, NT])
        slot = sb("slot", [P, 2, NT], I32)
        bexi = sb("bexi", [1, MAXB + 2], I32)
        zrow = sb("zrow", [128, D])
        ARENA = 25040
        arena = sb("arena", [128, ARENA])

        def view(off, shape, dt=F32):
            n = 1
            for s in shape[1:]:
                n *= s
            words = n if dt in (F32, I32) else (n + 1) // 2
            assert off + words <= ARENA, (off, words)
            w = arena[0:shape[0], off:off + words]
            if dt != F32:
                w = w.bitcast(dt)
            names = "abcdef"[:len(shape) - 1]
            if len(shape) > 2:
                w = w.rearrange("p (" + " ".join(names) + ") -> p " + " ".join(names),
                                **{k: s for k, s in zip(names, shape[1:])})
            return w

        MSG = view(0, [P, CH, D])
        RING = view(20480, [P, 2, SLOTS, D])
        ei = view(5500, [CH, 3, P], I32)
        ef = view(6000, [CH, 4, P])
        red = view(6600, [CH, 2])
        TH = view(6700, [1, 3, NT, GROUPS])
        mm_ = view(7400, [1, 2, GROUPS])
        tou = view(7500, [1, 3, NT, GROUPS])
        lh = view(8200, [1, 8, NT])
        wtmp = view(8300, [P, 2, CH])
        wtb = view(8500, [P, CH], BF16)
        b1r = view(8600, [64, 2, 128])
        bxr = view(8900, [HP, 128])
        w2r = view(9200, [128, 2, D])
        OHS = view(22528, [P, G, 626], BF16)
        OHB = view(23780, [P, G, 3, 126], BF16)
        OHF = view(24536, [P, G, P])
        iot = view(12000, [P, N], I32)
        RW = view(13000, [128, 2, KD, D])
        XW = view(14100, [P, 2, NT, D])
        W1 = view(0, [128, UB, KD, HID])
        W2 = view(3072, [128, UB, MH, D])
        HT = view(6144, [128, UB, MH, BS])
        XB = view(7680, [BS, UB, D])
        XBT = view(8448, [128, UB, KD, BS])
        YB = view(9216, [BS, UB, D])
        B2 = view(9984, [BS, UB, D])
        YG = view(10752, [P, 2, NT, D])
        bexp = view(13320, [1, MAXB, E2])
        bex = view(13760, [1, MAXB + 2])
        bodies = view(13800, [1, MAXB // UB])
        Y = view(0, [P, 4, NT, D])
        U = view(5120, [P, NT, D])
        S1 = view(6400, [P, NT, D])
        S2 = view(7680, [P, NT, D])
        XMT = view(0, [128, HP, N])
        FX = view(2500, [P, NT, 512])
        SW = view(5060, [P, NT, 512])
        SWT = view(7620, [128, HP, N])
        OXT = view(10120, [128, HP, N])
        hm = view(12620, [P, NT, 8])
        hs = view(12660, [P, NT, 8])
        hr = view(12700, [P, NT, 8])
        rn = view(12740, [128, 512])
        STT = view(13252, [128, HP, 128])
        QT = view(13764, [128, HP, 128])
        KT = view(14276, [128, HP, 128])
        VV = view(14788, [128, HP, 128])
        AT = view(15300, [128, HP, HD])
        am = view(15560, [128, 3, HP])
        ABD = view(15600, [128, HP, 128])
        ATT = view(16112, [128, HP, 128])
        OS = view(16624, [128, HP, 128])
        blk = view(17140, [128, 128])
        w1r = view(0, [128, 2, D])
        w1T = view(512, [128, KD, D])
        b1s = view(1024, [P, D])
        b2s = view(1280, [128, 2, D])
        SCO = view(1792, [P, NT, D])
        TM = view(3072, [P, NT, D])
        COT = view(4352, [128, 2, N])
        CXI = view(5632, [P, NT, 512])
        CXS = view(8192, [P, NT, 512])
        PM = view(10752, [P, NT, N])
        LB = view(13900, [P, NT, LEAVES], BF16)
        GB = view(14220, [P, NT, LEAVES], BF16)
        CS = view(14540, [P, NT, D])
        tl = view(15820, [P, NT, LEAVES])
        lid = view(16460, [P, 2, NT])
        tn = view(16480, [NT, 9, STEPS])
        tls = view(18860, [NT, 2, LEAVES])
        tb = view(19120, [NT, 12, 16])
        tbi = view(19320, [NT, 2, 8, 2], I32)
        tcnt = view(19360, [NT, 2], I32)
        tnode = view(19364, [NT, 2, STEPS], I32)
        sid = view(19893, [P, NT], I32)
        TW = view(19900, [128, TU, KD, D])

        WEIGHTS_IN = 16 * (12 + 4 + 6 + 8)


        ones_b = sb("ones_b", [P, P], BF16)
        upper_b = sb("upper_b", [P, P], BF16)
        ioleaf = sb("ioleaf", [P, STEPS])
        pcol = sb("pcol", [P, 2])
        pcoli = sb("pcoli", [P, 1], I32)
        levelk = sb("levelk", [NT, 8])

        block = ctx.enter_context(nc.Block())

        def bank_pair(w):
            return [(w, 0, HALF[0]), (w + 1, HALF[0], N)]

        def hidden_slot(b, m):
            return PS[:, 2 + b, m * BS:m * BS + BS]

        def mixture_bodies(eng, second):
            n = eng.value_load(bexi[0:1, MAXB:MAXB + 1], min_val=1, max_val=MAXB // UB)
            before = eng.value_load(bexi[0:1, MAXB + 1:MAXB + 2], min_val=1, max_val=MAXB // UB) if second else 0
            return n, before

        def block_expert(eng, i, b, second):
            return eng.value_load(bexi[0:1, bass.ds(i * UB + b, 1)], min_val=0, max_val=(E2 if second else E0) - 1)

        def yslot(t, base):
            return PS[0:P, base + t // 2, (t % 2) * D:(t % 2) * D + D]

        def tree_weights(eng, half):
            tw = a["L3_ffn_w2s"].rearrange("j (p k) n -> j p k n", k=KD)
            eng.wait_ge(sem("tree_lists"), 1)
            done = 0
            for t in range(NT):
                n = eng.value_load(tcnt[t:t + 1, 0:1], min_val=1, max_val=STEPS // TU)
                with eng.Fori(0, n) as i:
                    for u in range(half, TU, 2):
                        node = eng.value_load(tnode[t:t + 1, 0, bass.ds(i * TU + u, 1)], min_val=0, max_val=NODES - 1)
                        eng.wait_ge(sem(f"tree_w_free{u}"), i + done + 1)
                        eng.dma_start(TW[:, u].rearrange("p (j k) n -> p j k n", j=1),
                                      tw[bass.ds(node, 1)].rearrange("j p k n -> p j k n")).then_inc(sem(f"tree_w_in{u}"), 16)
                done = n + done

        @block.sync
        def _(_sp):
            def bc(x, n=P):
                return x.partition_broadcast(n)

            def feat(w):
                return w.rearrange("(p k) n -> p k n", k=KD)

            for i, n in enumerate(("src", "dst", "edge_type_8")):
                sp.dma_start(ei[:, i, :], a[n].rearrange("(c p) -> c p", p=P)).then_inc(sem("edges_in"), 16)
            sp.dma_start(ef[:, 3, :], a["edge_weight"].rearrange("(c p) -> c p", p=P)).then_inc(sem("edges_in"), 16)
            sp.dma_start(X[:], a["x"].rearrange("(t p) d -> p t d", p=P)).then_inc(sem("x_in"), 16)
            sp.dma_start(b1r[0:32, 0, :], a["L0_ffn_b1"].rearrange("e (m p) -> (e m) p", p=128)).then_inc(sem("prep_in"), 16)
            sp.dma_start(b1r[0:64, 1, :], a["L2_ffn_b1"].rearrange("e (m p) -> (e m) p", p=128)).then_inc(sem("prep_in"), 16)
            sp.dma_start(bxr, a["L1_ffn_b_x"].rearrange("(m p) -> m p", p=128)).then_inc(sem("prep_in"), 16)
            sp.dma_start(w2r, a["L2_gnn_W"].rearrange("(o p) f -> p o f", p=128)).then_inc(sem("prep_in"), 16)
            if stop > 0:
                for b in range(2):
                    sp.dma_start(RW[:, b], a["L0_gnn_W1"].rearrange("r (p k) n -> r p k n", k=KD)[b]).then_inc(sem(f"rw_in{b}"), 16)
            for dst, src in [(selfw[:, 0], feat(a["L0_gnn_self_w1"])), (selfw[:, 1], feat(a["L0_gnn_self_w2"])),
                             (bias[:, 0, :], bc(a["L0_gnn_b1"])), (bias[:, 1, :], bc(a["L0_gnn_b2"]))]:
                sp.dma_start(dst, src).then_inc(sem("layer_weights_in"), 16)
            sp.dma_start(EA, a["edge_attr_64"].rearrange("(c p) f -> p c f", p=P)).then_inc(sem("attr_in"), 16)

            def later_weights():
                loads = [
                    (wg0[:], feat(a["L0_ffn_Wg"])), (wg2[:], feat(a["L2_ffn_gate_w"])),
                    (wfx[:], feat(a["L1_ffn_W_fx"])), (wx[:], feat(a["L1_ffn_W_x"])),
                    (wout[:], a["L1_ffn_W_out"].rearrange("(m p) n -> p m n", p=128)),
                    (l3w[:], feat(a["L3_gnn_weight"][0:D, :])), (l3we[:], a["L3_gnn_weight"][D:D + FE, :]),
                    (bfx[:], bc(a["L1_ffn_b_fx"])), (bsl[:], bc(a["L1_ffn_b_slice"])),
                    (temp[:], bc(a["L1_ffn_temperature"].rearrange("a h b c -> (a h b c)"))),
                    (bg0[:], bc(a["L0_ffn_bg"])), (bg2[:], bc(a["L2_ffn_gate_b"])),
                ]
                loads += [(cheb[:, k], feat(a["L1_gnn_weight"][k])) for k in range(4)]
                loads += [(bias[:, 2 + i, :], bc(a[n])) for i, n in enumerate(
                    ("L1_gnn_bias", "L1_ffn_b_out", "L2_gnn_b", "L2_ffn_gamma", "L2_ffn_beta", "L3_gnn_bias"))]
                for dst, src in loads:
                    sp.dma_start(dst, src).then_inc(sem("weights_in"), 16)
                sp.wait_ge(sem("bd_zeroed"), 1)
                for i, n in enumerate(("L1_ffn_W_slice", "L1_ffn_W_q", "L1_ffn_W_k", "L1_ffn_W_v")):
                    for h in range(2):
                        sp.dma_start(bd[h * HD:h * HD + HD, i, h * HD:h * HD + HD], a[n]).then_inc(sem("weights_in"), 16)
                assert 16 * (len(loads) + 8) == WEIGHTS_IN
                for tag in ("moe0_", "moe2_"):
                    sp.dma_start(slots[tag].rearrange("(b p) d -> p b d", p=BS),
                                 zrow[:].unsqueeze(1).to_broadcast([BS, MAXB, D])).then_inc(sem("slots_zeroed"), 16)

            if stop > 0:
                for b in range(2):
                    sp.sem_inc(sem(f"xw_stored{b}"), 16)
                    sp.sem_inc(sem(f"xw_copied{b}"), 1)
                for layer, n in enumerate(("L0_gnn_W1", "L0_gnn_W2")):
                    wv = a[n].rearrange("r (p k) n -> r p k n", k=KD)
                    tv = table.rearrange("(r t p) d -> r p t d", t=NT, p=P)
                    if layer:
                        later_weights()
                        sp.wait_ge(sem("msg_copied"), CH)
                        sp.wait_ge(sem("seg0_tile"), NT)
                        for b in range(2):
                            sp.dma_start(RW[:, b], wv[b]).then_inc(sem(f"rw_in{b}"), 16)

                    def store(i, b):
                        sp.wait_ge(sem(f"xw_copied{b}"), i * 2 + (layer * R + 3))
                        sp.dma_start(tv[bass.ds(i * 2 + b, 1)].rearrange("r p t d -> p (r t) d"),
                                     XW[:, b]).then_inc(sem(f"xw_stored{b}"), 16)

                    with sp.Fori(0, R // 2 - 1) as i:
                        for b in range(2):
                            store(i, b)
                            sp.dma_start(RW[:, b].rearrange("p (r k) n -> p r k n", r=1),
                                         wv[bass.ds(i * 2 + (b + 2), 1)].rearrange("r p k n -> p r k n")).then_inc(sem(f"rw_in{b}"), 16)
                    for b in range(2):
                        store(R // 2 - 1, b)

            def experts(tag, second, w1, w2, b2):
                w2v = a[w2].rearrange("e (m p) n -> e p m n", p=128)
                w1v = a[w1].rearrange("e (p k) h -> e p k h", k=KD)
                xv = slots[tag].rearrange("(b p) d -> b p d", p=BS)
                sp.wait_ge(sem("routed"), second + 1)
                n, before = mixture_bodies(sp, second)
                with sp.Fori(0, n) as i:
                    expert = [block_expert(sp, i, b, second) for b in range(UB)]

                    def load_w1(b):
                        sp.wait_ge(sem(f"w1_free{b}"), i + before + 1)
                        sp.dma_start(W1[:, b].rearrange("p (e k) h -> p e k h", e=1),
                                     w1v[bass.ds(expert[b], 1)].rearrange("e p k h -> p e k h")).then_inc(sem(f"w1_in{b}"), 16)

                    def load_tokens(b):
                        sp.wait_ge(sem(f"xb_free{b}"), i + before + 1)
                        sp.wait_ge(sem("dispatched"), 16 * 2 * NT * (second + 1))
                        sp.dma_start(XB[:, b].rearrange("p (e d) -> p e d", e=1),
                                     xv[bass.ds(i * UB + b, 1)].rearrange("e p d -> p e d")).then_inc(sem(f"x_block_in{b}"), 16)

                    def load_w2(b):
                        sp.wait_ge(sem(f"w2_free{b}"), i + before + 1)
                        sp.dma_start(W2[:, b].rearrange("p (e m) h -> p e m h", e=1),
                                     w2v[bass.ds(expert[b], 1)].rearrange("e p m h -> p e m h")).then_inc(sem(f"w2_in{b}"), 16)

                    def load_b2(b):
                        sp.wait_ge(sem(f"y_out{b}"), i + before + 1)
                        sp.dma_start(B2[:, b].rearrange("p (e d) -> p e d", e=1),
                                     a[b2][bass.ds(expert[b], 1), :].partition_broadcast(BS)).then_inc(sem(f"b2_in{b}"), 16)

                    load_w1(0)
                    load_w1(1)
                    load_w2(0)
                    load_tokens(0)
                    load_tokens(1)
                    load_tokens(2)
                    load_b2(0)
                    load_w1(2)
                    load_w2(1)
                    load_b2(1)
                    load_w2(2)
                    load_b2(2)

            if stop > 1:
                experts("moe0_", 0, "L0_ffn_W1", "L0_ffn_W2", "L0_ffn_b2")
            if stop > 5:
                experts("moe2_", 1, "L2_ffn_w1", "L2_ffn_w2", "L2_ffn_b2")
            if stop > 7:
                sp.wait_ge(sem("arena_free_for_tree"), 1)
                sp.dma_start(w1r[:, 0, :], a["L3_ffn_w1s"][0:128, :]).then_inc(sem("tree_in"), 16)
                sp.dma_start(w1r[0:127, 1, :], a["L3_ffn_w1s"][128:255, :]).then_inc(sem("tree_in"), 16)
                sp.dma_start(b2s[:, 0, :], a["L3_ffn_b2s"][0:128, :]).then_inc(sem("tree_in"), 16)
                sp.dma_start(b2s[0:127, 1, :], a["L3_ffn_b2s"][128:255, :]).then_inc(sem("tree_in"), 16)
                sp.dma_start(b1s[:, 0:NODES], bc(a["L3_ffn_b1s"])).then_inc(sem("tree_in"), 16)
                tree_weights(sp, 0)
            if stop < 8:
              sp.wait_ge(sem("x_final"), 1)
              sp.dma_start(out.rearrange("(t p) d -> p t d", p=P), X[:]).then_inc(sem("out_stored"), 16)
              sp.wait_ge(sem("out_stored"), 16)

        @block.gpsimd
        def _(_p):
            pool.memset(ident[:], 0.0)
            pool.memset(ones[:], 1.0)
            pool.memset(zeros[:], 0.0)
            pool.memset(bd[:], 0.0)
            pool.memset(zrow[:], 0.0)
            pool.memset(ones_b[:], 1.0)
            pool.memset(upper_b[:], 1.0)
            for d in range(DEPTH):
                pool.memset(levelk[:, d:d + 1], float(2 ** d - 1))
            pool.drain().then_inc(sem("bd_zeroed"), 1)
            pool.affine_select(out=ident[:], in_=ident[:], compare_op=ALU.not_equal, fill=1.0, base=0,
                               pattern=[[-1, 128]], channel_multiplier=1)
            pool.affine_select(out=upper_b[:], in_=upper_b[:], compare_op=ALU.is_gt, fill=0.0, base=0,
                               pattern=[[1, P]], channel_multiplier=-1)
            pool.iota(pcoli[:], pattern=[[1, 1]], base=0, channel_multiplier=1)
            pool.iota(iot, pattern=[[1, N]], base=0, channel_multiplier=0)
            pool.iota(TH[:, 0].bitcast(I32), pattern=[[P, NT], [0, GROUPS]], base=0, channel_multiplier=0)
            pool.iota(TH[:, 1].bitcast(I32), pattern=[[P, NT], [0, GROUPS]], base=P, channel_multiplier=0)
            pool.iota(TH[:, 2].bitcast(I32), pattern=[[0, NT], [1, GROUPS]], base=0, channel_multiplier=0)
            pool.drain().then_inc(sem("consts"), 1)
            def experts(tag, second):
                pool.wait_ge(sem("slots_zeroed"), 32)
                pool.wait_ge(sem("routed"), second + 1)
                for k in range(2):
                    for t in range(NT):
                        pool.indirect_dma_start(
                            out=slots[tag], out_offset=bass.IndirectOffsetOnAxis(ap=slot[:, k, t:t + 1], axis=0),
                            in_=XN[:, t, :], in_offset=None).then_inc(sem("dispatched"), 16)
                n, before = mixture_bodies(pool, second)
                for b in range(UB):
                    pool.wait_ge(sem(f"y_stored{b}"), (n + before) * 16 + 16)
                pool.sem_inc(sem("seen"), 1)
                for t in range(NT):
                    for k in range(2):
                        pool.indirect_dma_start(
                            out=YG[:, k, t, :], out_offset=None, in_=slots[tag],
                            in_offset=bass.IndirectOffsetOnAxis(ap=slot[:, k, t:t + 1], axis=0)).then_inc(sem(f"collected{t}"), 16)

            if stop > 0:
                pool.wait_ge(sem("edge_fields"), 1)
                for layer in range(2):
                    for b in range(2):
                        pool.wait_ge(sem(f"xw_stored{b}"), 16 * (R // 2) * (layer + 1) + 16)
                    groups = CH // (2 * SLOTS)
                    with pool.Fori(0, groups) as g:
                        for h in range(2):
                            pool.wait_ge(sem(f"slots_free{h}"), g * SLOTS + (layer * groups + 1) * SLOTS)
                            pool.tensor_copy(gis[:, h, :], GI[:, bass.ds(g * (2 * SLOTS) + h * SLOTS, SLOTS)]).then_inc(sem("idx_staged"), 1)
                            pool.wait_ge(sem("idx_staged"), g * 2 + (layer * groups * 2 + h + 1))
                            pool.sem_inc(sem("seen"), 1)
                            for s in range(SLOTS):
                                pool.indirect_dma_start(
                                    out=RING[:, h, s, :], out_offset=None, in_=table,
                                    in_offset=bass.IndirectOffsetOnAxis(ap=gis[:, h, s:s + 1], axis=0),
                                ).then_inc(sem(f"gathered{h}_{s}"), 16)

            if stop > 1:
                experts("moe0_", 0)
            if stop > 5:
                experts("moe2_", 1)
            if stop > 7:
                pool.wait_ge(sem("x_final"), 1)
                for t in range(NT):
                    pool.indirect_dma_start(
                        out=out, out_offset=bass.IndirectOffsetOnAxis(ap=sid[:, t:t + 1], axis=0),
                        in_=CXS[:, t, D:2 * D], in_offset=None).then_inc(sem("out_stored"), 16)
                pool.wait_ge(sem("out_stored"), 16 * NT)

        @block.scalar
        def _(_a):
            def stats(li):
                for t in range(NT):
                    act.wait_ge(sem("var_ready"), NT * li + t + 1)
                    act.activation(std5[:, t:t + 1], var5[:, t:t + 1], ACT.Sqrt).then_inc(sem("std_ready"), 1)

            def features(fi):
                act.wait_ge(sem("xt_mm"), 2 * fi + 1)
                act.copy(XT[:, 0, 0:500], PS[:, 0, 0:500]).then_inc(sem("xt_ready_act"), 1)
                act.wait_ge(sem("xt_mm"), 2 * fi + 2)
                act.copy(XT[:, :, 500:N], PS[:, 2, 0:2 * P].rearrange("p (k n) -> p k n", k=2)).then_inc(sem("xt_ready_act"), 1)

            def degrees():
                act.wait_ge(sem("degrees"), 1)
                act.activation(sc5[:, 1:4, :], sc5[:, 1:4, :], ACT.Sqrt).then_inc(sem("degree_roots"), 1)

            def relational(layer):
                with act.Fori(0, R // 2) as i:
                    for b in range(2):
                        act.wait_ge(sem(f"rel_mm{b}"), i + (layer * (R // 2) + 1))
                        act.wait_ge(sem(f"xw_stored{b}"), i * 16 + (layer * (R // 2) + 1) * 16)
                        act.copy(XW[:, b, 0:2, :], PS[0:P, 3 * b, :].rearrange("p (t d) -> p t d", t=2))
                        act.copy(XW[:, b, 2:4, :], PS[0:P, 3 * b + 1, :].rearrange("p (t d) -> p t d", t=2)).then_inc(sem(f"xw_copied{b}"), 1)
                if layer:
                    act.wait_ge(sem("seg0_tile"), NT)
                groups = CH // (2 * SLOTS)
                with act.Fori(0, groups) as g:
                    for h in range(2):
                        for s in range(SLOTS):
                            act.wait_ge(sem(f"gathered{h}_{s}"), g * 16 + (layer * groups + 1) * 16)
                            act.copy(MSG[:, bass.ds(g * (2 * SLOTS) + (h * SLOTS + s), 1), :], RING[:, h, s:s + 1, :]).then_inc(sem("msg_copied"), 1)
                        act.drain().then_inc(sem(f"slots_free{h}"), SLOTS)

            def experts(tag, second, func, b1off):
                yv = slots[tag].rearrange("(b p) d -> b p d", p=BS)
                act.wait_ge(sem("routed"), second + 1)
                n, before = mixture_bodies(act, second)
                if not second:
                    degrees()
                with act.Fori(0, n) as i:
                    experts_of = [block_expert(act, i, b, second) for b in range(UB)]
                    for b, e in enumerate(experts_of):
                        act.wait_ge(sem(f"w2_free{b}"), i + before + 1)
                        act.wait_ge(sem(f"w1_free{b}"), i + before + 2)
                        act.sem_inc(sem("seen"), 1)
                        for m in range(MH):
                            act.activation(HT[:, b, m, :], hidden_slot(b, m), func,
                                           bias=b1T[:, bass.ds(e * MH + (b1off + m), 1)]).then_inc(sem("hidden"), 1)
                    for b in range(UB):
                        act.wait_ge(sem(f"y_out{b}"), i + before + 2)
                        act.dma_start(yv[bass.ds(i * UB + b, 1)].rearrange("e p d -> p e d"),
                                      YB[:, b].rearrange("p (e d) -> p e d", e=1)).then_inc(sem(f"y_stored{b}"), 16)

            if stop > 0:
                for h in range(2):
                    act.sem_inc(sem(f"slots_free{h}"), SLOTS)
            if stop > 0:
                stats(0)
                features(0)
                relational(0)
                features(1)
                relational(1)
                stats(1)
            if stop > 1:
                features(2)
                experts("moe0_", 0, ACT.Gelu, 0)
                stats(2)
            if stop > 2:
                features(3)
                stats(3)
            if stop > 3:
                features(4)
                for t in range(NT):
                    act.wait_ge(sem("slice_shifted"), t + 1)
                    act.activation(SW[:, t, :], SW[:, t, :], ACT.Exp).then_inc(sem("slice_exp"), 1)
                act.wait_ge(sem("attn_shifted"), 1)
                act.activation(AT, AT, ACT.Exp, scale=HD ** -0.5).then_inc(sem("attn_exp"), 1)
                stats(4)
            if stop > 4:
                features(5)
                stats(5)
            if stop > 5:
                features(6)
                act.wait_ge(sem("top2_diff"), 1)
                act.activation(gwt[:, :, 1], gwt[:, :, 0], ACT.Exp).then_inc(sem("top2_exp"), 1)
                experts("moe2_", 1, ACT.Relu, 32)
                stats(6)
                stats(7)
            if stop > 6:
                features(7)
                stats(8)
            if stop > 7:
                features(8)
                act.wait_ge(sem("tree_scores"), 1)
                act.activation(CXI[:, :, 0:NODES], SCO[:, :, 0:NODES], ACT.Abs).then_inc(sem("tree_abs"), 1)
                act.wait_ge(sem("tree_abs"), 1)
                act.activation(CXI[:, :, 0:NODES], CXI[:, :, 0:NODES], ACT.Gelu).then_inc(sem("tree_gelu"), 1)
                act.wait_ge(sem("tree_sorted"), 1)
                for bank, c0, c1 in bank_pair(5):
                    act.copy(XT[:, 0, c0:c1], PS[:, bank, 0:c1 - c0])
                for t in (0, 1):
                    act.copy(CXS[:, t, :], PS[0:P, t, :])
                act.drain().then_inc(sem("tree_sorted_out"), 1)
                act.wait_ge(sem("tree_sorted"), 2)
                for bank, c0, c1 in bank_pair(5):
                    last = act.copy(XT[:, 1, c0:c1], PS[:, bank, 0:c1 - c0])
                last.then_inc(sem("tree_sorted_out"), 1)
                tree_weights(act, 1)

        @block.tensor
        def _(_t):
            def rows(j=0):
                return slice(j * P, j * P + P)

            def features(fi):
                for t in range(NT - 1):
                    pe.wait_ge(sem("xn_ready"), NT * fi + t + 1)
                    for k in range(KD):
                        last = pe.transpose(PS[:, k, rows(t)], XNk[:, t, k, :], ident[0:P, 0:P])
                last.then_inc(sem("xt_mm"), 1)
                pe.wait_ge(sem("xn_ready"), NT * fi + NT)
                for k in range(KD):
                    last = pe.transpose(PS[:, 2, rows(k)], XNk[:, NT - 1, k, :], ident[0:P, 0:P])
                last.then_inc(sem("xt_mm"), 1)
                pe.wait_ge(sem("xt_ready"), fi + 1)
                pe.wait_ge(sem("xt_ready_act"), 2 * fi + 2)

            def rowprod(dst, w, t, n=None, start=True, stop_=True):
                for k in range(KD):
                    last = pe.matmul(dst, XT[:, k, rows(t)], w[:, k, :] if n is None else w[:, k, n],
                                     start=start and k == 0, stop=stop_ and k == KD - 1, skip_group_check=True)
                return last

            def edge_fields():
                pe.wait_ge(sem("edge_rows"), 1)
                for i in range(4):
                    pe.transpose(PS[0:P, 3, i * CH:i * CH + CH], ef[:, i, :], ident[0:CH, 0:CH])
                for i in range(2):
                    last = pe.transpose(PS[0:1, 4, i * CH:i * CH + CH], red[:, i:i + 1], ident[0:CH, 0:CH])
                last.then_inc(sem("edge_cols"), 1)
                pe.wait_ge(sem("prep_in"), 64)
                pe.transpose(PS[:, 6, 0:32], b1r[0:32, 0, :], ident[0:32, 0:32])
                pe.transpose(PS[:, 6, 32:96], b1r[0:64, 1, :], ident[0:64, 0:64])
                pe.transpose(PS[:, 6, 96:100], bxr, ident[0:HP, 0:HP])
                w2rk = w2r.rearrange("p o (f k) -> p o k f", k=KD)
                for k in range(KD):
                    for o in range(2):
                        last = pe.transpose(PS[:, 7, (k * 2 + o) * 128:(k * 2 + o) * 128 + 128], w2rk[:, o, k, :], ident[:])
                last.then_inc(sem("prep_mm"), 1)

            def over_groups(t, p, opening, step_of_chunk, closing):
                lo = pe.value_load(rng[0:1, 0, t:t + 1], min_val=0, max_val=GROUPS - 1)
                hi = pe.value_load(rng[0:1, 1, t:t + 1], min_val=1, max_val=GROUPS)
                step = pe.value_load(rng[0:1, 2 + p, t:t + 1], min_val=0, max_val=G * GROUPS * (4 * NT + 1))
                opening()
                with pe.Fori(lo, hi) as j:
                    for b in range(G):
                        pe.wait_ge(sem("oh_ready"), j * G + step + (b + 1))
                        step_of_chunk(j, b).then_inc(sem("oh_free"), 1)
                return closing()

            def zero_products(banks, start):
                for bank, n in banks:
                    last = pe.matmul(PS[0:P, bank, 0:n], zeros[0:P, 0:P], zeros[0:P, 0:n],
                                     start=start, stop=not start, skip_group_check=True)
                return last

            def counts():
                pe.wait_ge(sem("attr_in"), 16)
                for t in range(NT):
                    b0 = 3 * (t % 2)
                    banks = [(b0, HALF[0]), (b0 + 1, HALF[1]), (b0 + 2, FE)]
                    if t >= 2:
                        pe.wait_ge(sem("edge_tile_copied"), t - 1)

                    def chunk(j, b):
                        for bank, c0, c1 in bank_pair(b0):
                            pe.matmul(PS[0:P, bank, 0:c1 - c0], OHB[:, b, 0, 0:P], OHS[:, b, c0:c1],
                                      start=False, stop=False, skip_group_check=True)
                        return pe.matmul(PS[0:P, b0 + 2, 0:FE], OHF[:, b, :], EA[:, bass.ds(j * G + b, 1), :],
                                         start=False, stop=False, skip_group_check=True)

                    over_groups(t, 0, lambda: zero_products(banks, True), chunk,
                               lambda: zero_products(banks, False)).then_inc(sem("edge_tile_mm"), 1)
                pe.wait_ge(sem("edge_tile_copied"), NT)
                for j in range(NT):
                    last = pe.transpose(PS[0:FE, 4 + j // 4, rows(j % 4)], AE[:, j, :], ident[0:P, 0:P])
                last.then_inc(sem("ct_mm"), 1)
                for i in range(NT):
                    if i >= 2:
                        pe.wait_ge(sem("ct_copied"), i)
                    for j in range(NT):
                        last = pe.transpose(PS[0:P, (6 if i % 2 == 0 else 0) + j // 4, rows(j % 4)], C[:, j, rows(i)], ident[0:P, 0:P])
                    last.then_inc(sem("ct_mm"), 1)
                pe.wait_ge(sem("ct_copied"), NT + 1)

            def weighted():
                for t in range(NT):
                    b0 = 2 * (t % 2)
                    banks = [(b0, HALF[0]), (b0 + 1, HALF[1])]
                    if t >= 2:
                        pe.wait_ge(sem("edge_tile_copied"), NT + t - 1)

                    def chunk(j, b):
                        for i in range(3):
                            for bank, c0, c1 in bank_pair(b0):
                                last = pe.matmul(PS[0:P, bank, 0:c1 - c0], OHB[:, b, i, 0:P], OHS[:, b, c0:c1],
                                                 start=False, stop=False, skip_group_check=True)
                        return last

                    over_groups(t, 2, lambda: zero_products(banks, True), chunk,
                               lambda: zero_products(banks, False)).then_inc(sem("edge_tile_mm"), 1)
                pe.wait_ge(sem("edge_tile_copied"), 2 * NT)

            def relational(layer):
                with pe.Fori(0, R // 2) as i:
                    for b in range(2):
                        pe.wait_ge(sem(f"rw_in{b}"), i * 16 + (layer * (R // 2) + 1) * 16)
                        pe.wait_ge(sem(f"xw_copied{b}"), i * 2 + (layer * R + 1))
                        for t in range(NT):
                            last = rowprod(yslot(t, 3 * b), RW[:, b], t)
                        last.then_inc(sem(f"rel_mm{b}"), 1)
                for b in range(2):
                    pe.wait_ge(sem(f"xw_copied{b}"), R * (layer + 1) + 1)
                if layer == 0:
                    pe.wait_ge(sem("ranges"), 1)
                    pe.sem_inc(sem("oh_free"), CH + G)
                    counts()
                else:
                    weighted()
                pe.wait_ge(sem("layer_weights_in"), 64)
                for t in range(NT):
                    acc = PS[0:P, 3 + t, 0:D]

                    def chunk(j, b):
                        pe.wait_ge(sem("msg_copied"), j * G + (layer * CH + b + 1))
                        return pe.matmul(acc, OHF[:, b, :], MSG[:, bass.ds(j * G + b, 1), :],
                                         start=False, stop=False, skip_group_check=True)

                    over_groups(t, 1 + 2 * layer, lambda: rowprod(acc, selfw[:, layer], t, stop_=False), chunk,
                               lambda: pe.matmul(acc, zeros[0:P, 0:P], zeros[0:P, 0:D], start=False, stop=True,
                                                 skip_group_check=True)).then_inc(sem(f"seg{layer}_tile"), 1)

            def experts(second, ne, wg):
                for t in range(NT):
                    last = rowprod(PS[0:P, 7, t * ne:t * ne + ne], wg, t)
                last.then_inc(sem("route_mm"), 1)
                pe.wait_ge(sem("chosen"), second + 1)
                for t in range(NT):
                    dst = PS[0:P, 6, t * ne:t * ne + ne]
                    for u in range(t):
                        pe.matmul(dst, ones_b[:], chosen[:, u, 0:ne], start=(u == 0), stop=False, skip_group_check=True)
                    pe.matmul(dst, upper_b[:], chosen[:, t, 0:ne], start=(t == 0), stop=True, skip_group_check=True)
                for t in range(NT):
                    last = pe.matmul(PS[0:P, 5, 0:ne], ones_b[:], chosen[:, t, 0:ne], start=(t == 0), stop=(t == NT - 1), skip_group_check=True)
                last.then_inc(sem("route_mm"), 1)
                pe.wait_ge(sem("routed"), second + 1)
                n, before = mixture_bodies(pe, second)
                if not second:
                    for b in range(UB):
                        for name in ("w1_free", "w2_free", "xb_free", "y_out"):
                            pe.sem_inc(sem(f"{name}{b}"), 1)
                    pe.sem_inc(sem("hidden"), UB * MH)

                def tokens(i, b):
                    pe.wait_ge(sem(f"x_block_in{b}"), (i + before) * 16 + 16)
                    for k in range(KD):
                        last = pe.transpose(PS[:, b % 2, k * BS:k * BS + BS],
                                            XB[:, b, :].rearrange("p (f k) -> p k f", k=KD)[:, k, :], ident[:])
                    last.then_inc(sem(f"xb_free{b}"), 1)

                def hidden(i, b):
                    pe.wait_ge(sem(f"w1_in{b}"), (i + before) * 16 + 16)
                    pe.wait_ge(sem("xbt"), (i + before) * UB + b + 1)
                    pe.wait_ge(sem("hidden"), (i + before) * (UB * MH) + (b + 1) * MH)
                    for m in range(MH):
                        for k in range(KD):
                            last = pe.matmul(hidden_slot(b, m), W1[:, b, k, m * 128:m * 128 + 128], XBT[:, b, k, :],
                                             start=(k == 0), stop=(k == KD - 1), skip_group_check=True)
                    last.then_inc(sem(f"w1_free{b}"), 1)

                def outputs(i, b):
                    pe.wait_ge(sem(f"w2_in{b}"), (i + before) * 16 + 16)
                    pe.wait_ge(sem(f"y_out{b}"), i + before + 1)
                    for m in range(MH):
                        pe.wait_ge(sem("hidden"), (i + before) * (UB * MH) + (UB * MH + b * MH + m + 1))
                        last = pe.matmul(PS[:, 5 + b, 0:D], HT[:, b, m, :], W2[:, b, m, :], start=(m == 0), stop=(m == MH - 1))
                    last.then_inc(sem(f"w2_free{b}"), 1)

                with pe.Fori(0, n) as i:
                    tokens(i, 0)
                    tokens(i, 1)
                    hidden(i, 0)
                    tokens(i, 2)
                    hidden(i, 1)
                    outputs(i, 0)
                    hidden(i, 2)
                    outputs(i, 1)
                    outputs(i, 2)

            def spmm(mat, rhs, i, dst, stop_=True):
                for j in range(NT):
                    last = pe.matmul(dst, mat[:, j, rows(i)], rhs(j), start=(j == 0), stop=stop_ and j == NT - 1,
                                     skip_group_check=True)
                return last

            pe.wait_ge(sem("consts"), 1)
            if stop > 0:
                features(0)
                edge_fields()
                pe.wait_ge(sem("edge_fields"), 1)
                relational(0)
                features(1)
                relational(1)
            pe.wait_ge(sem("weights_in"), WEIGHTS_IN)
            if stop > 1:
                features(2)
                experts(0, E0, wg0)
            if stop > 2:
                features(3)
                for w in range(4):
                    if w >= 2:
                        pe.wait_ge(sem("cheb_y"), w - 1)
                    for t in range(NT):
                        last = rowprod(yslot(t, 3 if w % 2 == 0 else 0), cheb[:, w], t)
                    last.then_inc(sem("cheb_mm"), 1)
                for r in range(3):
                    pe.wait_ge(sem("cheb_u"), NT * (r + 1))
                    for i in range(NT):
                        spmm(C, lambda j: (U, S1, U)[r][:, j, :], i, PS[0:P, 3 + i, 0:D]).then_inc(sem("cheb_spmm"), 1)
            if stop > 3:
                features(4)
                for m in range(HP):
                    for bank, c0, c1 in bank_pair((m % 2) * 2):
                        if m >= 2:
                            pe.wait_ge(sem("xmt"), m - 1)
                        for k in range(KD):
                            last = pe.matmul(PS[:, bank, 0:c1 - c0], wx[:, k, m * 128:m * 128 + 128], XT[:, k, c0:c1],
                                             start=(k == 0), stop=(k == KD - 1))
                    last.then_inc(sem("xmt_mm"), 1)
                for t in range(NT):
                    if t >= 2:
                        pe.wait_ge(sem("fx"), t - 1)
                    rowprod(PS[0:P, 4 + t % 2, :], wfx, t).then_inc(sem("fx_mm"), 1)
                pe.wait_ge(sem("xmt"), HP)
                for t in range(NT):
                    if t >= 2:
                        pe.wait_ge(sem("slice_shifted"), t - 1)
                    for m in range(HP):
                        last = pe.matmul(PS[0:P, 6 + t % 2, m * 128:m * 128 + 128], XMT[:, m, rows(t)], bd[:, 0, :],
                                         start=True, stop=True)
                    last.then_inc(sem("logit_mm"), 1)
                pe.wait_ge(sem("fx"), NT)
                for t in range(NT):
                    pe.wait_ge(sem("slice_w"), t + 1)
                    pe.matmul(PS[:, 1, :], ones[:, :], SW[:, t, :], start=(t == 0), stop=(t == NT - 1), skip_group_check=True)
                for m in range(HP):
                    for t in range(NT):
                        last = pe.matmul(PS[:, 0, m * 128:m * 128 + 128], FX[:, t, m * 128:m * 128 + 128],
                                         SW[:, t, m * 128:m * 128 + 128], start=(t == 0), stop=(t == NT - 1), skip_group_check=True)
                last.then_inc(sem("attn_products"), 1)
                for m in range(HP):
                    if m >= 2:
                        pe.wait_ge(sem("swt"), m - 1)
                    for t in range(NT):
                        last = pe.transpose(PS[:, 2 + (m % 2) * 2 + t // 4, rows(t % 4)], SW[:, t, m * 128:m * 128 + 128], ident[0:P, 0:P])
                    last.then_inc(sem("swt_mm"), 1)
                pe.wait_ge(sem("attn_operands"), 1)
                pe.wait_ge(sem("swt"), HP)
                for w, bank in ((1, 2), (2, 3)):
                    for m in range(HP):
                        last = pe.matmul(PS[:, bank, m * 128:m * 128 + 128], bd[:, w, :], STT[:, m, :], start=True, stop=True)
                for m in range(HP):
                    last = pe.matmul(PS[:, 4, m * 128:m * 128 + 128], STT[:, m, :], bd[:, 3, :], start=True, stop=True)
                last.then_inc(sem("attn_products"), 1)
                pe.wait_ge(sem("attn_operands"), 2)
                for m in range(HP):
                    last = pe.matmul(PS[:, 0, m * 128:m * 128 + 128], QT[:, m, :], KT[:, m, :], start=True, stop=True)
                last.then_inc(sem("attn_products"), 1)
                pe.wait_ge(sem("attn_operands"), 3)
                for m in range(HP):
                    last = pe.transpose(PS[:, 1, m * 128:m * 128 + 128], ABD[:, m, :], ident[:])
                last.then_inc(sem("attn_products"), 1)
                pe.wait_ge(sem("attn_operands"), 4)
                for m in range(HP):
                    last = pe.matmul(PS[:, 2, m * 128:m * 128 + 128], ATT[:, m, :], VV[:, m, :], start=True, stop=True)
                last.then_inc(sem("attn_products"), 1)
                pe.wait_ge(sem("attn_operands"), 5)
                for m in range(HP):
                    for bank, c0, c1 in bank_pair(4 if m % 2 == 0 else 0):
                        if m >= 2:
                            pe.wait_ge(sem("oxt"), m - 1)
                        last = pe.matmul(PS[:, bank, 0:c1 - c0], OS[:, m, :], SWT[:, m, c0:c1], start=True, stop=True)
                    last.then_inc(sem("oxt_mm"), 1)
                pe.wait_ge(sem("oxt"), HP)
                for t in range(NT):
                    for m in range(HP):
                        last = pe.matmul(PS[0:P, 3 + t, 0:D], OXT[:, m, rows(t)], wout[:, m, :], start=(m == 0), stop=(m == HP - 1))
                    last.then_inc(sem("attn_out_mm"), 1)
            if stop > 4:
                features(5)
                for t in range(NT):
                    last = rowprod(yslot(t, 3), w2T, t)
                last.then_inc(sem("wg_y_mm"), 1)
                pe.wait_ge(sem("wg_y"), 1)
                for i in range(NT):
                    spmm(CW, lambda j: U[:, j, :], i, PS[0:P, 3 + i, 0:D]).then_inc(sem("wg_mm"), 1)
            if stop > 5:
                features(6)
                experts(1, E2, wg2)
            if stop > 6:
                features(7)
                for t in range(NT):
                    last = rowprod(yslot(t, 3), l3w, t)
                last.then_inc(sem("ng_y_mm"), 1)
                pe.wait_ge(sem("ng_y"), 1)
                for i in range(NT):
                    spmm(CT, lambda j: U[:, j, :], i, PS[0:P, 3 + i, 0:D], stop_=False)
                    pe.matmul(PS[0:P, 3 + i, 0:D], AET[:, rows(i)], l3we[:], start=False, stop=True,
                              skip_group_check=True).then_inc(sem("ng_mm"), 1)
            if stop > 7:
                features(8)
                pe.wait_ge(sem("tree_in"), 16 * 5)
                w1rk = w1r.rearrange("p o (f k) -> p o k f", k=KD)
                for k in range(KD):
                    pe.transpose(PS[:, 3, k * 256:k * 256 + 128], w1rk[:, 0, k, :], ident[:])
                    last = pe.transpose(PS[:, 3, k * 256 + 128:k * 256 + 255], w1rk[0:127, 1, k, :], ident[0:127, 0:127])
                last.then_inc(sem("tree_products"), 1)
                pe.wait_ge(sem("tree_operands"), 1)
                for t in range(NT):
                    last = rowprod(yslot(t, 4)[:, 0:NODES], w1T, t, n=slice(0, NODES))
                last.then_inc(sem("tree_products"), 1)
                pe.wait_ge(sem("tree_operands"), 2)
                for o in range(2):
                    for t in range(NT):
                        last = pe.transpose(PS[0:128 - o, 2 * o + t // 4, rows(t % 4)], CXI[:, t, o * 128:o * 128 + 128 - o], ident[0:P, 0:P])
                last.then_inc(sem("tree_products"), 1)
                pe.wait_ge(sem("tree_leaves"), 1)
                for t in range(NT):
                    pe.matmul(PS[0:P, 4, 0:LEAVES], ones_b[:], LB[:, t, :], start=(t == 0), stop=False, skip_group_check=True)
                    pe.matmul(PS[0:P, 4, 0:LEAVES], ones_b[:], GB[:, t, :], start=False, stop=(t == NT - 1), skip_group_check=True)
                for t in range(NT):
                    place = PS[0:P, 5 + t // 4, (t % 4) * LEAVES:(t % 4) * LEAVES + LEAVES]
                    for u in range(NT):
                        pe.matmul(place, ones_b[:], GB[:, u, :], start=(u == 0), stop=False, skip_group_check=True)
                    for u in range(t):
                        pe.matmul(place, ones_b[:], LB[:, u, :], start=False, stop=False, skip_group_check=True)
                    last = pe.matmul(place, upper_b[:], LB[:, t, :], start=False, stop=True, skip_group_check=True)
                last.then_inc(sem("tree_places"), 1)
                pe.wait_ge(sem("tree_operands"), 3)
                for t in range(NT):
                    for o in range(2):
                        last = pe.matmul(yslot(t, 0), COT[0:128 - o, o, rows(t)], b2s[0:128 - o, o, :], start=(o == 0), stop=(o == 1))
                last.then_inc(sem("tree_products"), 1)
                pe.wait_ge(sem("tree_operands"), 4)
                for r in range(NT):
                    for t in range(NT):
                        pe.matmul(PS[0:P, r, :], PM[:, t, rows(r)], CXI[:, t, :], start=(t == 0), stop=(t == NT - 1))
                for k in range(KD):
                    if k:
                        pe.wait_ge(sem("tree_sorted_out"), 1)
                    for bank, c0, c1 in bank_pair(5):
                        for t in range(NT):
                            last = pe.matmul(PS[:, bank, 0:c1 - c0], XNk[:, t, k, :], PM[:, t, c0:c1], start=(t == 0), stop=(t == NT - 1))
                    last.then_inc(sem("tree_sorted"), 1)
                pe.wait_ge(sem("tree_sorted_out"), 2)
                pe.wait_ge(sem("tree_rows_out"), 1)
                for u in range(TU):
                    pe.sem_inc(sem(f"tree_added{u}"), 1)
                    pe.sem_inc(sem(f"tree_w_free{u}"), 1)
                done = 0
                for t in range(NT):
                    n = pe.value_load(tcnt[t:t + 1, 0:1], min_val=1, max_val=STEPS // TU)
                    with pe.Fori(0, n) as i:
                        for u in range(TU):
                            pe.wait_ge(sem(f"tree_w_in{u}"), (i + done) * 16 + 16)
                            pe.wait_ge(sem(f"tree_added{u}"), i + done + 1)
                            rowprod(PS[0:P, u, 0:D], TW[:, u], t).then_inc(sem(f"tree_w_free{u}"), 1)
                    done = n + done

        @block.vector
        def _(_v):
            def layer_norm(li, src, dst, produce=None, signal=True):
                def normalise(t):
                    v.wait_ge(sem("std_ready"), NT * li + t + 1)
                    v.reciprocal(rstd[:, t:t + 1], std5[:, t:t + 1])
                    v.drain()
                    i = v.tensor_scalar(dst[:, t, :], src[:, t, :], mv[:, t, 0:1], rstd[:, t:t + 1], ALU.subtract, ALU.mult)
                    if signal:
                        i.then_inc(sem("xn_ready"), 1)

                for t in range(NT):
                    if produce:
                        produce(t)
                        v.drain()
                    v.bn_stats(out=bst[:, t, :], in_=src[:, t, :])
                    v.drain()
                    v.bn_aggr(out=mv[:, t, :], in_=bst[:, t, :])
                    v.drain()
                    v.tensor_scalar(var5[:, t:t + 1], mv[:, t, 1:2], EPS, None, ALU.add).then_inc(sem("var_ready"), 1)
                    if t:
                        normalise(t - 1)
                normalise(NT - 1)

            def features(fi):
                v.wait_ge(sem("xt_mm"), 2 * fi + 1)
                v.tensor_copy(XT[:, 1, 0:500], PS[:, 1, 0:500]).then_inc(sem("xt_ready"), 1)

            def over_groups(t, p, one_hots):
                lo = v.value_load(rng[0:1, 0, t:t + 1], min_val=0, max_val=GROUPS - 1)
                hi = v.value_load(rng[0:1, 1, t:t + 1], min_val=1, max_val=GROUPS)
                step = v.value_load(rng[0:1, 2 + p, t:t + 1], min_val=0, max_val=G * GROUPS * (4 * NT + 1))
                with v.Fori(lo, hi) as j:
                    for b in range(G):
                        v.wait_ge(sem("oh_free"), j * G + step + (b + 1))
                        one_hots(b, bass.ds(j * G + b, 1), io16[:, t * P:t * P + P]).then_inc(sem("oh_ready"), 1)

            def edge_rows():
                v.wait_ge(sem("edges_in"), 64)
                for i in range(2):
                    v.tensor_copy(ef[:, i, :], ei[:, i, :])
                v.tensor_copy(ef[:, 2, :], ei[:, 2, :])
                v.drain()
                v.scalar_tensor_tensor(out=ef[:, 2, :], in0=ef[:, 2, :], scalar=float(N), in1=ef[:, 0, :], op0=ALU.mult, op1=ALU.add)
                v.tensor_reduce(red[:, 0:1], ef[:, 1, :], AX.X, ALU.min)
                v.tensor_reduce(red[:, 1:2], ef[:, 1, :], AX.X, ALU.max)
                v.drain().then_inc(sem("edge_rows"), 1)

            def edge_fields():
                v.wait_ge(sem("consts"), 1)
                v.tensor_copy(io16[:], iot)
                v.tensor_copy(ioe[:], iot[:, 0:E2])
                v.tensor_copy(ioleaf[:], iot[:, 0:STEPS])
                v.tensor_copy(pcol[:, 0:1], pcoli[:])
                v.drain()
                v.tensor_scalar(pcol[:, 1:2], pcol[:, 0:1], float(P), None, ALU.mult)
                THi = TH.bitcast(I32)
                v.tensor_copy(TH, THi)
                v.wait_ge(sem("edge_cols"), 1)
                v.tensor_copy(EF[:], PS[0:P, 3, 0:4 * CH].rearrange("p (i c) -> p i c", i=4))
                v.tensor_reduce(mm_[:, 0, :], PS[0:1, 4, 0:CH].rearrange("p (j b) -> p j b", b=G), AX.X, ALU.min)
                v.tensor_reduce(mm_[:, 1, :], PS[0:1, 4, CH:2 * CH].rearrange("p (j b) -> p j b", b=G), AX.X, ALU.max)
                v.drain()
                v.tensor_copy(GI[:], EF[:, 2, :])
                v.drain().then_inc(sem("edge_fields"), 1)
                w = EF[:, 3, :]
                v.tensor_copy(wtb, w)
                v.drain()
                v.tensor_copy(WP3[:, 0, :], wtb)
                v.drain()
                v.tensor_tensor(wtmp[:, 0, :], w, WP3[:, 0, :], ALU.subtract)
                v.drain()
                v.tensor_copy(wtb, wtmp[:, 0, :])
                v.drain()
                v.tensor_copy(WP3[:, 1, :], wtb)
                v.drain()
                v.tensor_tensor(WP3[:, 2, :], wtmp[:, 0, :], WP3[:, 1, :], ALU.subtract)
                def over_tiles(x):
                    return x.unsqueeze(1).to_broadcast([1, NT, GROUPS])
                v.tensor_tensor(tou[:, 0], over_tiles(mm_[:, 0, :]), TH[:, 1], ALU.is_lt)
                v.tensor_tensor(tou[:, 1], over_tiles(mm_[:, 1, :]), TH[:, 0], ALU.is_ge)
                v.drain()
                v.tensor_tensor(tou[:, 0], tou[:, 0], tou[:, 1], ALU.mult)
                v.drain()
                v.tensor_scalar(tou[:, 1], tou[:, 0], -1000.0, 1000.0, ALU.mult, ALU.add)
                v.drain()
                v.tensor_tensor(tou[:, 1], tou[:, 1], TH[:, 2], ALU.add)
                v.scalar_tensor_tensor(out=tou[:, 2], in0=TH[:, 2], scalar=1.0, in1=tou[:, 0], op0=ALU.add, op1=ALU.mult)
                v.drain()
                v.tensor_reduce(lh[:, 0, :], tou[:, 1], AX.X, ALU.min)
                v.tensor_reduce(lh[:, 1, :], tou[:, 2], AX.X, ALU.max)
                v.drain()
                v.tensor_scalar(lh[:, 0, :], lh[:, 0, :], float(GROUPS - 1), None, ALU.min)
                v.memset(lh[:, 2, :], 0.0)
                v.drain()
                v.scalar_tensor_tensor(out=lh[:, 1, :], in0=lh[:, 0, :], scalar=1.0, in1=lh[:, 1, :], op0=ALU.add, op1=ALU.max)
                v.drain()
                v.tensor_tensor(lh[:, 3, :], lh[:, 1, :], lh[:, 0, :], ALU.subtract)
                for t in range(NT - 1):
                    v.drain()
                    v.tensor_tensor(lh[:, 2, t + 1:t + 2], lh[:, 2, t:t + 1], lh[:, 3, t:t + 1], ALU.add)
                v.drain()
                v.tensor_tensor(lh[:, 4, 0:1], lh[:, 2, NT - 1:NT], lh[:, 3, NT - 1:NT], ALU.add)
                v.drain()
                v.tensor_tensor(lh[:, 2, :], lh[:, 2, :], lh[:, 0, :], ALU.subtract)
                v.drain()
                v.tensor_scalar(lh[:, 2, :], lh[:, 2, :], float(GROUPS), float(G), ALU.add, ALU.mult)
                v.tensor_scalar(lh[:, 4, 0:1], lh[:, 4, 0:1], float(G), None, ALU.mult)
                v.tensor_copy(rng[:, 0:2, :], lh[:, 0:2, :])
                v.drain()
                v.tensor_copy(rng[:, 2, :], lh[:, 2, :])
                for p in range(1, 4):
                    v.tensor_scalar(lh[:, 2, :], lh[:, 2, :], lh[:, 4, 0:1], None, ALU.add)
                    v.drain()
                    v.tensor_copy(rng[:, 2 + p, :], lh[:, 2, :])
                v.drain().then_inc(sem("ranges"), 1)
                v.wait_ge(sem("prep_mm"), 1)
                v.tensor_copy(b1T[:], PS[:, 6, 0:96])
                v.tensor_copy(bxT[:], PS[:, 6, 96:100])
                v.tensor_copy(w2T[:], PS[:, 7, :].rearrange("p (k o) -> p k o", k=KD))
                v.drain()

            def counts():
                v.sem_inc(sem("oh_ready"), CH)

                def one_hots(b, col, own):
                    v.tensor_scalar(OHS[:, b, 0:N], io16[:], EF[:, 0, col], None, ALU.is_equal)
                    v.tensor_scalar(OHB[:, b, 0, 0:P], own, EF[:, 1, col], None, ALU.is_equal)
                    return v.tensor_scalar(OHF[:, b, :], own, EF[:, 1, col], None, ALU.is_equal)

                def out(t):
                    v.wait_ge(sem("edge_tile_mm"), t + 1)
                    b0 = 3 * (t % 2)
                    for bank, c0, c1 in bank_pair(b0):
                        v.tensor_copy(C[:, t, c0:c1], PS[0:P, bank, 0:c1 - c0])
                    v.tensor_copy(AE[:, t, :], PS[0:P, b0 + 2, 0:FE]).then_inc(sem("edge_tile_copied"), 1)

                for t in range(NT):
                    over_groups(t, 0, one_hots)
                    if t:
                        out(t - 1)
                out(NT - 1)
                v.wait_ge(sem("ct_mm"), 1)
                v.tensor_copy(AET[:, 0:500], PS[0:FE, 4, 0:500])
                v.tensor_copy(AET[:, 500:N], PS[0:FE, 5, 0:P]).then_inc(sem("ct_copied"), 1)
                for i in range(NT):
                    v.wait_ge(sem("ct_mm"), i + 2)
                    bank = 6 if i % 2 == 0 else 0
                    v.tensor_copy(CT[:, i, 0:500], PS[0:P, bank, 0:500])
                    v.tensor_copy(CT[:, i, 500:N], PS[0:P, bank + 1, 0:P]).then_inc(sem("ct_copied"), 1)

            def weighted():
                def one_hots(b, col, own):
                    v.tensor_scalar(OHS[:, b, 0:N], io16[:], EF[:, 0, col], None, ALU.is_equal)
                    for i in range(3):
                        last = v.tensor_scalar(OHB[:, b, i, 0:P], own, EF[:, 1, col], WP3[:, i, col], ALU.is_equal, ALU.mult)
                    return last

                def out(t):
                    v.wait_ge(sem("edge_tile_mm"), NT + t + 1)
                    for bank, c0, c1 in bank_pair(2 * (t % 2)):
                        last = v.tensor_copy(CW[:, t, c0:c1], PS[0:P, bank, 0:c1 - c0])
                    last.then_inc(sem("edge_tile_copied"), 1)

                for t in range(NT):
                    over_groups(t, 2, one_hots)
                    if t:
                        out(t - 1)
                out(NT - 1)

            def degrees():
                v.tensor_reduce(sc5[:, 0, :], C, AX.X, ALU.add)
                for t in range(NT):
                    v.tensor_tensor(OHF[:, 0, :], C[:, t, t * P:t * P + P], ident[0:P, 0:P], ALU.mult)
                    v.drain()
                    v.tensor_reduce(dg5[:, t:t + 1], OHF[:, 0, :], AX.X, ALU.add)
                    v.drain()
                v.tensor_reduce(dis[:], CT, AX.X, ALU.add)
                v.drain()
                v.tensor_scalar(sc5[:, 1, :], dis[:], 1.0, None, ALU.add)
                v.tensor_scalar(sc5[:, 2, :], dis[:], 1.0, None, ALU.max)
                v.tensor_scalar(sc5[:, 3, :], sc5[:, 0, :], 1.0, None, ALU.max)
                v.drain().then_inc(sem("degrees"), 1)
                v.wait_ge(sem("degree_roots"), 1)
                v.reciprocal(dis[:], sc5[:, 1, :])
                v.reciprocal(nout[:], sc5[:, 2, :])
                v.reciprocal(nin[:], sc5[:, 3, :])
                v.drain()
                v.tensor_tensor(q5[:], dis[:], dis[:], ALU.mult)
                v.drain()
                v.scalar_tensor_tensor(out=q5[:], in0=dg5[:], scalar=1.0, in1=q5[:], op0=ALU.add, op1=ALU.subtract)
                v.drain()

            def relational(layer):
                with v.Fori(0, R // 2) as i:
                    for b in range(2):
                        v.wait_ge(sem(f"rel_mm{b}"), i + (layer * (R // 2) + 1))
                        v.wait_ge(sem(f"xw_stored{b}"), i * 16 + (layer * (R // 2) + 1) * 16)
                        v.tensor_copy(XW[:, b, 4, :], PS[0:P, 3 * b + 2, 0:D]).then_inc(sem(f"xw_copied{b}"), 1)

                if layer == 0:
                    counts()
                else:
                    weighted()
                v.wait_ge(sem("layer_weights_in"), 64)

                def finish(t):
                    v.wait_ge(sem(f"seg{layer}_tile"), t + 1)
                    if layer == 0:
                        v.tensor_tensor(XN[:, t, :], PS[0:P, 3 + t, 0:D], bias[:, 0, :], ALU.add)
                        v.drain()
                        v.tensor_scalar(XN[:, t, :], XN[:, t, :], 0.0, None, ALU.max).then_inc(sem("xn_ready"), 1)
                    else:
                        v.tensor_tensor(XN[:, t, :], PS[0:P, 3 + t, 0:D], bias[:, 1, :], ALU.add)
                        v.drain()
                        v.tensor_tensor(X[:, t, :], X[:, t, :], XN[:, t, :], ALU.add)
                def one_hots(b, col, own):
                    return v.tensor_scalar(OHF[:, b, :], own, EF[:, 1, col], None, ALU.is_equal)

                def produce(t):
                    if t == 0:
                        over_groups(0, 1 + 2 * layer, one_hots)
                    if t + 1 < NT:
                        over_groups(t + 1, 1 + 2 * layer, one_hots)
                    finish(t)

                if layer == 0:
                    for t in range(NT):
                        produce(t)
                else:
                    layer_norm(1, X, XN, produce)

            def experts(second, ne, bg, soft):
                v.wait_ge(sem("route_mm"), 2 * second + 1)
                v.tensor_tensor(gate[:, :, 0:ne], PS[0:P, 7, 0:NT * ne].rearrange("p (t e) -> p t e", e=ne),
                                bg[:].unsqueeze(1).to_broadcast([P, NT, ne]), ALU.add)
                v.drain()
                for t in range(NT):
                    v.max(gmax[:, t, :], gate[:, t, 0:ne])
                v.drain()
                for t in range(NT):
                    v.max_index(gidx[:, t, :], gmax[:, t, :], gate[:, t, 0:ne])
                v.drain()
                v.tensor_copy(gidf[:], gidx[:, :, 0:2])
                if soft:
                    v.tensor_tensor(gwt[:, :, 0], gmax[:, :, 1], gmax[:, :, 0], ALU.subtract).then_inc(sem("top2_diff"), 1)
                    v.wait_ge(sem("top2_exp"), 1)
                    v.tensor_scalar(gwt[:, :, 2], gwt[:, :, 1], 1.0, None, ALU.add)
                    v.drain()
                    v.reciprocal(gwt[:, :, 2], gwt[:, :, 2])
                    v.drain()
                    v.tensor_tensor(gwt[:, :, 3], gwt[:, :, 1], gwt[:, :, 2], ALU.mult)
                else:
                    v.memset(gwt[:], 1.0)
                v.drain()
                for k in range(2):
                    for t in range(NT):
                        v.tensor_scalar(one_hot[:, k, t, 0:ne], ioleaf[:, 0:ne], gidf[:, t, k:k + 1], None, ALU.is_equal)
                v.drain()
                v.tensor_tensor(chosen[:, :, 0:ne], one_hot[:, 0, :, 0:ne], one_hot[:, 1, :, 0:ne], ALU.add).then_inc(sem("chosen"), 1)
                v.wait_ge(sem("route_mm"), 2 * second + 2)
                v.tensor_scalar(blocksi[:, 0:ne], PS[0:P, 5, 0:ne], float(BS - 1), None, ALU.add)
                v.drain()
                v.tensor_scalar(blocksi[:, 0:ne], blocksi[:, 0:ne], 7, None, ALU.arith_shift_right)
                v.drain()
                v.tensor_scalar(blocks[:, 0, 0:ne], blocksi[:, 0:ne], 1.0, None, ALU.max)
                v.drain()
                src, n = 0, 1
                if second:
                    v.tensor_copy(bexi[:, MAXB + 1:MAXB + 2], bexi[:, MAXB:MAXB + 1])
                while n < ne:
                    dst = 1 + src % 2
                    v.tensor_copy(blocks[:, dst, 0:n], blocks[:, src, 0:n])
                    v.tensor_tensor(blocks[:, dst, n:ne], blocks[:, src, n:ne], blocks[:, src, 0:ne - n], ALU.add)
                    v.drain()
                    src, n = dst, 2 * n
                ends = blocks[:, src, 0:ne]
                v.tensor_tensor(blocks[:, 3, 0:ne], ends, blocks[:, 0, 0:ne], ALU.subtract)
                v.tensor_tensor(bexp[:, :, 0:ne], ioleaf[0:1, 0:MAXB].unsqueeze(2).to_broadcast([1, MAXB, ne]),
                                blocks[0:1, src, 0:ne].unsqueeze(1).to_broadcast([1, MAXB, ne]), ALU.is_ge)
                v.tensor_scalar(bodies, ioleaf[0:1, 0:MAXB // UB], float(UB), blocks[0:1, src, ne - 1:ne], ALU.mult, ALU.is_lt)
                v.drain()
                v.tensor_reduce(bex[:, 0:MAXB], bexp[:, :, 0:ne], AX.X, ALU.add)
                v.tensor_reduce(bex[:, MAXB:MAXB + 1], bodies, AX.X, ALU.add)
                v.tensor_scalar(blocks[:, 3, 0:ne], blocks[:, 3, 0:ne], float(BS), None, ALU.mult)
                v.drain()
                v.tensor_scalar(bex[:, 0:MAXB], bex[:, 0:MAXB], float(ne - 1), None, ALU.min)
                v.tensor_tensor(place[:, 0, :, 0:ne], PS[0:P, 6, 0:NT * ne].rearrange("p (t e) -> p t e", e=ne),
                                blocks[:, 3, 0:ne].unsqueeze(1).to_broadcast([P, NT, ne]), ALU.add)
                v.drain()
                v.tensor_copy(bexi[:, 0:MAXB], bex[:, 0:MAXB])
                v.tensor_copy(bexi[:, MAXB:MAXB + 1], bex[:, MAXB:MAXB + 1])
                v.tensor_tensor(place[:, 1, :, 0:ne], place[:, 0, :, 0:ne], one_hot[:, 1, :, 0:ne], ALU.mult)
                v.drain()
                v.tensor_tensor(place[:, 0, :, 0:ne], place[:, 0, :, 0:ne], one_hot[:, 0, :, 0:ne], ALU.mult)
                v.drain()
                for k in range(2):
                    v.tensor_reduce(slotf[:, k, :], place[:, k, :, 0:ne], AX.X, ALU.add)
                v.drain()
                v.tensor_copy(slot[:], slotf[:])
                v.drain().then_inc(sem("routed"), 1)
                if not second:
                    degrees()
                n, before = mixture_bodies(v, second)
                if not second:
                    for b in range(UB):
                        v.sem_inc(sem(f"y_stored{b}"), 16)

                def tokens(i, b):
                    v.wait_ge(sem(f"xb_free{b}"), i + before + 2)
                    v.tensor_copy(XBT[:, b], PS[:, b % 2, 0:2 * BS].rearrange("p (k n) -> p k n", k=KD)).then_inc(sem("xbt"), 1)

                def outputs(i, b):
                    v.wait_ge(sem(f"w2_free{b}"), i + before + 2)
                    v.wait_ge(sem(f"b2_in{b}"), (i + before) * 16 + 16)
                    v.wait_ge(sem(f"y_stored{b}"), (i + before) * 16 + 16)
                    v.tensor_tensor(YB[:, b, :], PS[:, 5 + b, 0:D], B2[:, b, :], ALU.add).then_inc(sem(f"y_out{b}"), 1)

                with v.Fori(0, n) as i:
                    tokens(i, 0)
                    tokens(i, 1)
                    tokens(i, 2)
                    outputs(i, 0)
                    outputs(i, 1)
                    outputs(i, 2)
            def collect(t, second, acc):
                v.wait_ge(sem(f"collected{t}"), 32 * (second + 1))
                for k in range(2):
                    v.scalar_tensor_tensor(out=acc[:, t, :], in0=YG[:, k, t, :], scalar=gwt[:, t, 2 + k:3 + k],
                                           in1=acc[:, t, :], op0=ALU.mult, op1=ALU.add)
                    v.drain()

            def bank_tiles(base, n=D):
                for g, (t0, t1) in enumerate(((0, 2), (2, 4), (4, 5))):
                    yield t0, t1, PS[0:P, base + g, 0:(t1 - t0) * D].rearrange("p (t d) -> p t d", d=D)[:, :, 0:n]

            if stop > 0:
                edge_rows()
                v.wait_ge(sem("x_in"), 16)
                layer_norm(0, X, XN)
                features(0)
                edge_fields()
                relational(0)
                features(1)
                relational(1)
            v.wait_ge(sem("weights_in"), WEIGHTS_IN)
            if stop > 1:
                features(2)
                experts(0, E0, bg0, False)
                layer_norm(2, X, XN, lambda t: collect(t, 0, X))
            if stop > 2:
                features(3)
                for w in range(4):
                    v.wait_ge(sem("cheb_mm"), w + 1)
                    for t0, t1, src in bank_tiles(3 if w % 2 == 0 else 0):
                        last = v.tensor_copy(Y[:, w, t0:t1, :], src)
                    last.then_inc(sem("cheb_y"), 1)
                b3, b2, b1 = Y[:, 3], Y[:, 2], Y[:, 1]
                v.drain()
                for t in range(NT):
                    v.tensor_scalar(U[:, t, :], b3[:, t, :], dis[:, t:t + 1], None, ALU.mult).then_inc(sem("cheb_u"), 1)
                v.tensor_scalar(sc5[:, 0, :], q5[:], 2.0, None, ALU.mult)
                v.tensor_scalar(sc5[:, 1, :], dis[:], -2.0, None, ALU.mult)
                v.tensor_scalar(sc5[:, 2, :], dis[:], -1.0, None, ALU.mult)
                v.tensor_tensor(b1, b1, b3, ALU.subtract)
                v.drain()
                for t in range(NT):
                    v.scalar_tensor_tensor(out=b2[:, t, :], in0=b3[:, t, :], scalar=sc5[:, 0, t:t + 1], in1=b2[:, t, :], op0=ALU.mult, op1=ALU.add)
                v.tensor_tensor(X[:], X[:], bias[:, 2, :].unsqueeze(1).to_broadcast([P, NT, D]), ALU.add)
                v.drain()
                v.tensor_tensor(X[:], X[:], Y[:, 0], ALU.add)
                v.drain()
                for r, (b, bn, u) in enumerate(((b2, b1, S1), (b1, None, U))):
                    for t in range(NT):
                        v.wait_ge(sem("cheb_spmm"), NT * r + t + 1)
                        v.scalar_tensor_tensor(out=b[:, t, :], in0=PS[0:P, 3 + t, 0:D], scalar=sc5[:, 1, t:t + 1], in1=b[:, t, :], op0=ALU.mult, op1=ALU.add)
                        v.drain()
                        v.tensor_scalar(u[:, t, :], b[:, t, :], dis[:, t:t + 1], None, ALU.mult).then_inc(sem("cheb_u"), 1)
                        if r == 0:
                            v.scalar_tensor_tensor(out=bn[:, t, :], in0=b[:, t, :], scalar=sc5[:, 0, t:t + 1], in1=bn[:, t, :], op0=ALU.mult, op1=ALU.add)
                            v.tensor_tensor(X[:, t, :], X[:, t, :], b[:, t, :], ALU.subtract)
                        else:
                            v.scalar_tensor_tensor(out=X[:, t, :], in0=b[:, t, :], scalar=q5[:, t:t + 1], in1=X[:, t, :], op0=ALU.mult, op1=ALU.add)
                    v.drain()

                def cheb_out(t):
                    v.wait_ge(sem("cheb_spmm"), NT * 2 + t + 1)
                    v.scalar_tensor_tensor(out=X[:, t, :], in0=PS[0:P, 3 + t, 0:D], scalar=sc5[:, 2, t:t + 1], in1=X[:, t, :], op0=ALU.mult, op1=ALU.add)

                layer_norm(3, X, XN, cheb_out)
            if stop > 3:
                features(4)
                v.tensor_scalar(rtemp[:], temp[:], 0.1, 5.0, ALU.max, ALU.min)
                v.drain()
                v.reciprocal(rtemp[:], rtemp[:])
                v.memset(blk, 0.0)
                v.drain()
                for h in range(2):
                    v.memset(blk[h * HD:h * HD + HD, h * HD:h * HD + HD], 1.0)
                v.memset(ABD, 0.0)
                for m in range(HP):
                    v.wait_ge(sem("xmt_mm"), m + 1)
                    for bank, c0, c1 in bank_pair((m % 2) * 2):
                        last = v.tensor_scalar(XMT[:, m, c0:c1], PS[:, bank, 0:c1 - c0], bxT[:, m:m + 1], None, ALU.add)
                    last.then_inc(sem("xmt"), 1)
                for t in range(NT):
                    v.wait_ge(sem("fx_mm"), t + 1)
                    v.tensor_tensor(FX[:, t, :], PS[0:P, 4 + t % 2, :], bfx[:], ALU.add).then_inc(sem("fx"), 1)
                for t in range(NT):
                    v.wait_ge(sem("logit_mm"), t + 1)
                    sw = SW[:, t, :].rearrange("p (h g) -> p h g", h=8)
                    v.tensor_tensor(sw, PS[0:P, 6 + t % 2, :].rearrange("p (h g) -> p h g", h=8),
                                    bsl[:].unsqueeze(1).to_broadcast([P, 8, HD]), ALU.add)
                    v.drain()
                    v.tensor_tensor(sw, sw, rtemp[:].unsqueeze(2).to_broadcast([P, 8, HD]), ALU.mult)
                    v.drain()
                    v.tensor_reduce(hm[:, t, :], sw, AX.X, ALU.max)
                    v.drain()
                    v.tensor_tensor(sw, sw, hm[:, t, :].unsqueeze(2).to_broadcast([P, 8, HD]), ALU.subtract).then_inc(sem("slice_shifted"), 1)
                for t in range(NT):
                    sw = SW[:, t, :].rearrange("p (h g) -> p h g", h=8)
                    v.wait_ge(sem("slice_exp"), t + 1)
                    v.tensor_reduce(hs[:, t, :], sw, AX.X, ALU.add)
                    v.drain()
                    v.reciprocal(hr[:, t, :], hs[:, t, :])
                    v.drain()
                    v.tensor_tensor(sw, sw, hr[:, t, :].unsqueeze(2).to_broadcast([P, 8, HD]), ALU.mult).then_inc(sem("slice_w"), 1)
                v.wait_ge(sem("attn_products"), 1)
                v.tensor_scalar(rn, PS[:, 1, :], 1e-5, None, ALU.add)
                v.drain()
                v.reciprocal(rn, rn)
                v.drain()
                blk4 = blk.unsqueeze(1).to_broadcast([128, HP, 128])
                rn4 = rn.rearrange("p (m g) -> p m g", m=HP)
                v.tensor_tensor(rn4, rn4, blk4, ALU.mult)
                v.drain()
                v.tensor_tensor(STT, PS[:, 0, :].rearrange("p (m g) -> p m g", m=HP), rn4, ALU.mult).then_inc(sem("attn_operands"), 1)
                for m in range(HP):
                    v.wait_ge(sem("swt_mm"), m + 1)
                    b0 = 2 + (m % 2) * 2
                    v.tensor_copy(SWT[:, m, 0:500], PS[:, b0, 0:500])
                    v.tensor_copy(SWT[:, m, 500:N], PS[:, b0 + 1, 0:P]).then_inc(sem("swt"), 1)
                v.wait_ge(sem("attn_products"), 2)
                for dst, bank in ((QT, 2), (KT, 3), (VV, 4)):
                    last = v.tensor_copy(dst, PS[:, bank, :].rearrange("p (m g) -> p m g", m=HP))
                last.then_inc(sem("attn_operands"), 1)
                v.wait_ge(sem("attn_products"), 3)
                for h in range(2):
                    hr_ = slice(h * HD, h * HD + HD)
                    v.tensor_copy(AT[hr_], PS[hr_, 0, :].rearrange("p (m g) -> p m g", m=HP)[:, :, hr_])
                v.drain()
                v.tensor_reduce(am[:, 0, :], AT, AX.X, ALU.max)
                v.drain()
                v.tensor_tensor(AT, AT, am[:, 0, :].unsqueeze(2).to_broadcast([128, HP, HD]), ALU.subtract).then_inc(sem("attn_shifted"), 1)
                v.wait_ge(sem("attn_exp"), 1)
                v.tensor_reduce(am[:, 1, :], AT, AX.X, ALU.add)
                v.drain()
                v.reciprocal(am[:, 2, :], am[:, 1, :])
                v.drain()
                for h in range(2):
                    hr_ = slice(h * HD, h * HD + HD)
                    last = v.tensor_tensor(ABD[hr_, :, hr_], AT[hr_], am[hr_, 2, :].unsqueeze(2).to_broadcast([HD, HP, HD]), ALU.mult)
                last.then_inc(sem("attn_operands"), 1)
                v.wait_ge(sem("attn_products"), 4)
                v.tensor_copy(ATT, PS[:, 1, :].rearrange("p (m g) -> p m g", m=HP)).then_inc(sem("attn_operands"), 1)
                v.wait_ge(sem("attn_products"), 5)
                v.tensor_copy(OS, PS[:, 2, :].rearrange("p (m g) -> p m g", m=HP)).then_inc(sem("attn_operands"), 1)
                for m in range(HP):
                    v.wait_ge(sem("oxt_mm"), m + 1)
                    for bank, c0, c1 in bank_pair(4 if m % 2 == 0 else 0):
                        last = v.tensor_copy(OXT[:, m, c0:c1], PS[:, bank, 0:c1 - c0])
                    last.then_inc(sem("oxt"), 1)
                v.tensor_tensor(X[:], X[:], bias[:, 3, :].unsqueeze(1).to_broadcast([P, NT, D]), ALU.add)
                v.drain()

                def attn_out(t):
                    v.wait_ge(sem("attn_out_mm"), t + 1)
                    v.tensor_tensor(X[:, t, :], PS[0:P, 3 + t, 0:D], X[:, t, :], ALU.add)

                layer_norm(4, X, XN, attn_out)
            if stop > 4:
                features(5)
                v.wait_ge(sem("wg_y_mm"), 1)
                for t0, t1, src in bank_tiles(3):
                    last = v.tensor_copy(U[:, t0:t1, :], src)
                last.then_inc(sem("wg_y"), 1)
                v.tensor_tensor(X[:], X[:], bias[:, 4, :].unsqueeze(1).to_broadcast([P, NT, D]), ALU.add)
                v.drain()

                def wg_out(t):
                    v.wait_ge(sem("wg_mm"), t + 1)
                    v.tensor_tensor(X[:, t, :], PS[0:P, 3 + t, 0:D], X[:, t, :], ALU.add)

                layer_norm(5, X, XN, wg_out)
            if stop > 5:
                features(6)
                experts(1, E2, bg2, True)
                v.tensor_tensor(X[:], X[:], bias[:, 6, :].unsqueeze(1).to_broadcast([P, NT, D]), ALU.add)
                layer_norm(6, XN, XN, lambda t: collect(t, 1, XN), signal=False)
                v.drain()

                def moe_out(t):
                    v.tensor_tensor(XN[:, t, :], XN[:, t, :], bias[:, 5, :], ALU.mult)
                    v.drain()
                    v.tensor_tensor(X[:, t, :], X[:, t, :], XN[:, t, :], ALU.add)

                layer_norm(7, X, XN, moe_out)
            if stop > 6:
                features(7)
                v.wait_ge(sem("ng_y_mm"), 1)
                for t in range(NT):
                    last = v.tensor_scalar(U[:, t, :], yslot(t, 3), nout[:, t:t + 1], None, ALU.mult)
                last.then_inc(sem("ng_y"), 1)

                def ng_out(t):
                    v.wait_ge(sem("ng_mm"), t + 1)
                    v.scalar_tensor_tensor(out=S1[:, t, :], in0=PS[0:P, 3 + t, 0:D], scalar=nin[:, t:t + 1], in1=bias[:, 7, :], op0=ALU.mult, op1=ALU.add)
                    v.drain()
                    v.scalar_tensor_tensor(out=X[:, t, :], in0=S1[:, t, :], scalar=0.0, in1=X[:, t, :], op0=ALU.max, op1=ALU.add)
                    if t == NT - 1:
                        v.drain().then_inc(sem("arena_free_for_tree"), 1)

                layer_norm(8, X, XN, ng_out)
            if stop > 7:
                features(8)
                v.wait_ge(sem("tree_products"), 1)
                v.tensor_copy(w1T[:, :, 0:NODES], PS[:, 3, :].rearrange("p (k j) -> p k j", k=KD)[:, :, 0:NODES]).then_inc(sem("tree_operands"), 1)
                v.wait_ge(sem("tree_products"), 2)
                for t0, t1, src in bank_tiles(4, NODES):
                    v.tensor_tensor(SCO[:, t0:t1, 0:NODES], src, b1s[:, 0:NODES].unsqueeze(1).to_broadcast([P, t1 - t0, NODES]), ALU.add)
                v.drain().then_inc(sem("tree_scores"), 1)
                v.memset(TM[:, :, 0:1], 1.0)
                for d in range(DEPTH - 1):
                    n0, n1 = 2 ** d - 1, 2 ** (d + 1) - 1
                    kids = TM[:, :, n1:2 * n1 + 1].rearrange("p t (j c) -> p t j c", c=2)
                    v.drain()
                    for t in range(NT):
                        v.scalar_tensor_tensor(out=kids[:, t, :, 1], in0=SCO[:, t, n0:n1], scalar=0.0, in1=TM[:, t, n0:n1], op0=ALU.is_gt, op1=ALU.mult)
                        v.scalar_tensor_tensor(out=kids[:, t, :, 0], in0=SCO[:, t, n0:n1], scalar=0.0, in1=TM[:, t, n0:n1], op0=ALU.is_le, op1=ALU.mult)
                v.drain()
                v.wait_ge(sem("tree_gelu"), 1)
                v.tensor_tensor(CXI[:, :, 0:NODES], CXI[:, :, 0:NODES], TM[:, :, 0:NODES], ALU.mult).then_inc(sem("tree_operands"), 1)
                leaf = TM[:, :, LEAVES - 1:NODES]
                v.tensor_copy(LB, leaf)
                v.tensor_tensor(tl, leaf, ioleaf[:, 0:LEAVES].unsqueeze(1).to_broadcast([P, NT, LEAVES]), ALU.mult)
                v.drain()
                v.tensor_reduce(lid[:, 0, :], tl, AX.X, ALU.add)
                v.drain()
                for t in range(NT):
                    v.tensor_scalar(GB[:, t, :], ioleaf[:, 0:LEAVES], lid[:, 0, t:t + 1], None, ALU.is_gt)
                v.drain().then_inc(sem("tree_leaves"), 1)
                v.wait_ge(sem("tree_products"), 3)
                for o in range(2):
                    v.tensor_copy(COT[0:128 - o, o, 0:500], PS[0:128 - o, 2 * o, 0:500])
                    last = v.tensor_copy(COT[0:128 - o, o, 500:N], PS[0:128 - o, 2 * o + 1, 0:P])
                last.then_inc(sem("tree_operands"), 1)
                v.wait_ge(sem("tree_places"), 1)
                for i in range(2):
                    v.tensor_scalar(tls[:, i, :], PS[0:NT, 4, 0:LEAVES], pcol[0:NT, 1:2], float(i * (P - 1)), ALU.subtract, ALU.is_le)
                for t in range(NT):
                    v.tensor_tensor(tl[:, t, :], PS[0:P, 5 + t // 4, (t % 4) * LEAVES:(t % 4) * LEAVES + LEAVES], leaf[:, t, :], ALU.mult)
                v.drain()
                v.tensor_reduce(lid[:, 1, :], tl, AX.X, ALU.add)
                v.drain()
                for t in range(NT):
                    v.tensor_scalar(PM[:, t, :], io16[:], lid[:, 1, t:t + 1], None, ALU.is_equal)
                    v.tensor_scalar(CXI[:, t, NODES:D], pcol[:, 0:1], float(t * P), None, ALU.add)
                v.wait_ge(sem("tree_products"), 4)
                for t in range(NT):
                    last = v.tensor_tensor(CXI[:, t, D:2 * D], yslot(t, 0), X[:, t, :], ALU.add)
                last.then_inc(sem("tree_operands"), 1)
                v.tensor_reduce(tb[:, 0, 0:2], tls, AX.X, ALU.add)
                v.drain()
                for d in range(DEPTH):
                    v.tensor_copy(tbi[:, 0, d, :], tb[:, 0, 0:2])
                v.drain()
                for d in range(DEPTH):
                    v.tensor_scalar(tbi[:, 1, d, :], tbi[:, 0, d, :], DEPTH - 1 - d, None, ALU.arith_shift_right)
                v.drain()
                v.tensor_copy(tb[:, 1, 0:8], tbi[:, 1, :, 0])
                v.tensor_copy(tb[:, 2, 0:8], tbi[:, 1, :, 1])
                v.memset(tb[:, 4, 0:1], 0.0)
                v.drain()
                v.scalar_tensor_tensor(out=tb[:, 3, 0:8], in0=tb[:, 2, 0:8], scalar=1.0, in1=tb[:, 1, 0:8], op0=ALU.add, op1=ALU.subtract)
                for d in range(DEPTH):
                    v.drain()
                    v.tensor_tensor(tb[:, 4, d + 1:d + 2], tb[:, 4, d:d + 1], tb[:, 3, d:d + 1], ALU.add)
                v.drain()
                v.tensor_tensor(tb[:, 5, 0:8], tb[:, 1, 0:8], tb[:, 4, 0:8], ALU.subtract)
                v.drain()
                v.tensor_tensor(tb[:, 5, 0:8], tb[:, 5, 0:8], levelk[:], ALU.add)
                v.drain()
                v.tensor_tensor(tb[:, 6, 1:8], tb[:, 5, 1:8], tb[:, 5, 0:7], ALU.subtract)
                v.tensor_copy(tb[:, 6, 0:1], tb[:, 5, 0:1])
                v.memset(tb[:, 6, 8:9], 1000.0)
                v.drain()
                for d in range(9):
                    v.tensor_scalar(tn[:, d, :], ioleaf[0:NT, :], tb[:, 4, d:d + 1], tb[:, 6, d:d + 1], ALU.is_ge, ALU.mult)
                v.tensor_scalar(tls[:, 0, 0:STEPS // TU], ioleaf[0:NT, 0:STEPS // TU], float(TU), tb[:, 4, 8:9], ALU.mult, ALU.is_lt)
                v.drain()
                v.tensor_reduce(tb[:, 7, 0:1], tls[:, 0, 0:STEPS // TU], AX.X, ALU.add)
                for d in range(1, 9):
                    v.tensor_tensor(tn[:, 0, :], tn[:, 0, :], tn[:, d, :], ALU.add)
                    v.drain()
                v.tensor_tensor(tn[:, 0, :], tn[:, 0, :], ioleaf[0:NT, :], ALU.add)
                v.drain()
                v.tensor_copy(tcnt[:, 0:1], tb[:, 7, 0:1])
                v.tensor_scalar(tn[:, 1, :], tn[:, 0, :], float(NODES - 1), None, ALU.min)
                v.tensor_scalar(tn[:, 2, :], tn[:, 0, :], float(NODES), None, ALU.min)
                v.drain()
                v.tensor_copy(tnode, tn[:, 1:3, :])
                v.drain().then_inc(sem("tree_lists"), 1)
                v.wait_ge(sem("tree_sorted"), 1)
                for t in (2, 3, 4):
                    v.tensor_copy(CXS[:, t, :], PS[0:P, t, :])
                v.drain().then_inc(sem("tree_rows_out"), 1)
                v.wait_ge(sem("tree_sorted_out"), 2)
                v.tensor_copy(CS[:, :, 0:NODES], CXS[:, :, 0:NODES])
                v.memset(CS[:, :, NODES:D], 0.0)
                v.tensor_copy(sid, CXS[:, :, NODES])
                v.drain()
                done = 0
                for t in range(NT):
                    n = v.value_load(tcnt[t:t + 1, 0:1], min_val=1, max_val=STEPS // TU)
                    own = CXS[:, t, D:2 * D]
                    with v.Fori(0, n) as i:
                        for u in range(TU):
                            node = v.value_load(tnode[t:t + 1, 1, bass.ds(i * TU + u, 1)], min_val=0, max_val=NODES)
                            v.drain()
                            v.wait_ge(sem(f"tree_w_free{u}"), i + done + 2)
                            v.scalar_tensor_tensor(out=own, in0=PS[0:P, u, 0:D], scalar=CS[:, t, bass.ds(node, 1)],
                                                   in1=own, op0=ALU.mult, op1=ALU.add).then_inc(sem(f"tree_added{u}"), 1)
                    done = n + done
            v.drain().then_inc(sem("x_final"), 1)


_INS = ['x', 'src', 'dst', 'edge_attr_64', 'edge_type_8', 'edge_weight', 'L0_gnn_W1', 'L0_gnn_self_w1', 'L0_gnn_b1',
        'L0_gnn_W2', 'L0_gnn_self_w2', 'L0_gnn_b2', 'L0_ffn_Wg', 'L0_ffn_bg', 'L0_ffn_W1', 'L0_ffn_b1', 'L0_ffn_W2',
        'L0_ffn_b2', 'L1_gnn_weight', 'L1_gnn_bias', 'L1_ffn_W_fx', 'L1_ffn_b_fx', 'L1_ffn_W_x', 'L1_ffn_b_x',
        'L1_ffn_W_slice', 'L1_ffn_b_slice', 'L1_ffn_W_q', 'L1_ffn_W_k', 'L1_ffn_W_v', 'L1_ffn_W_out', 'L1_ffn_b_out',
        'L1_ffn_temperature', 'L2_gnn_W', 'L2_gnn_b', 'L2_ffn_gate_w', 'L2_ffn_gate_b', 'L2_ffn_w1', 'L2_ffn_b1',
        'L2_ffn_w2', 'L2_ffn_b2', 'L2_ffn_gamma', 'L2_ffn_beta', 'L3_gnn_weight', 'L3_gnn_bias', 'L3_ffn_w1s',
        'L3_ffn_b1s', 'L3_ffn_w2s', 'L3_ffn_b2s']


def kernel(**inputs):
    import numpy as _np
    import concourse.bacc as _bacc
    from concourse import mybir as _mybir
    from concourse.bass_utils import run_bass_kernel_spmd as _run

    nc = _bacc.Bacc("TRN2", target_bir_lowering=False, num_devices=1)
    arrays, args = {}, {}
    for name in _INS:
        x = _np.ascontiguousarray(inputs[name])
        arrays[f"in_{name}"] = x
        args[name] = nc.dram_tensor(f"in_{name}", x.shape, _mybir.dt.from_np(x.dtype), kind="ExternalInput").ap()
    out = nc.dram_tensor("out_x", (N, D), F32, kind="ExternalOutput").ap()
    build(nc, args, out)
    r = _run(nc, [arrays], core_ids=[0])
    return r.results[0]["out_x"]
```

```python
from contextlib import ExitStack

import concourse.bass as bass
from concourse import mybir

F32 = mybir.dt.float32
BF16 = mybir.dt.bfloat16
F16 = mybir.dt.float16
I32 = mybir.dt.int32
U32 = mybir.dt.uint32
ALU = mybir.AluOpType
ACT = mybir.ActivationFunctionType
AX = mybir.AxisListType

N = 625
D = 256
P = 125
NT = N // P
KD = D // 128
E = 10000
CH = E // P
G = 3
BODIES = -(-CH // G)
CHP = BODIES * G
R = 8
FE = 64
HD = 64
HP = 4
HID = 512
MH = HID // 128
E0, E2 = 8, 16
BS = 128
UB = 3
MAXB = 27
NODES = 255
DEPTH = 8
LEAVES = 2 ** (DEPTH - 1)
TU = 6
STEPS = 252 + 12
SLOTS = 4
EPS = 1e-5
HALF = (313, 312)


class EdgePasses:
    all = 0
    done = 0

    def __init__(self):
        self.ranges = {}


def build(nc, a, out, stop=99):
    v, pe, act, pool, sp = nc.vector, nc.tensor, nc.scalar, nc.gpsimd, nc.sync
    table = nc.dram_tensor("relation_table", (R * N, D), F32).ap()
    slots = {tag: nc.dram_tensor(tag + "slots", (MAXB * BS, D), F32).ap() for tag in ("moe0_", "moe2_")}

    features_by_leaf = nc.dram_tensor("features_by_leaf", (N, D), F32).ap()
    rows_by_leaf = nc.dram_tensor("rows_by_leaf", (N, 2 * D), F32).ap()

    with ExitStack() as ctx:
        def sb(name, shape, dt=F32):
            return ctx.enter_context(nc.sbuf_tensor(name, shape, dt))

        sems = {}

        def sem(name):
            if name not in sems:
                sems[name] = ctx.enter_context(nc.semaphore(name))
            return sems[name]

        PS = ctx.enter_context(nc.psum_tensor("PS", [128, 8, 512], F32))

        X = sb("X", [P, NT, D])
        XN = sb("XN", [P, NT, D])
        XT = sb("XT", [128, KD, N])
        XNk = XN[:].rearrange("p t (f k) -> p t k f", k=KD)
        graph = sb("graph", [P, 3 * NT * N])

        def matrix(i):
            return graph[:, i * NT * N:(i + 1) * NT * N].rearrange("p (t n) -> p t n", t=NT)

        C, CW, CT = matrix(0), matrix(1), matrix(2)
        EA = graph[:, NT * N:NT * N + CHP * FE].rearrange("p (c f) -> p c f", c=CHP)
        AE = graph[:, NT * N + CHP * FE:NT * N + CHP * FE + NT * FE].rearrange("p (t f) -> p t f", t=NT)
        AET = sb("AET", [FE, N])
        ident = sb("ident", [128, 128])
        zeros = sb("zeros", [128, 320], BF16)
        ones = sb("ones", [P, 128])
        io16 = sb("io16", [P, N], F16)
        ioe = sb("ioe", [P, E2])
        EF = sb("EF", [P, 4, CHP])
        GI = sb("GI", [P, CH], I32)
        WP3 = sb("WP3", [P, 3, CHP])
        gis = sb("gis", [P, 2, SLOTS], I32)
        rng = sb("rng", [1, 4, NT], I32)
        bst = sb("bst", [P, NT, 6])
        mv = sb("mv", [P, NT, 2])
        eps = sb("eps", [P, 1])
        std5 = sb("std5", [P, NT])
        rstd = sb("rstd", [P, NT])
        dis = sb("dis", [P, NT])
        q5 = sb("q5", [P, NT])
        dg5 = sb("dg5", [P, NT])
        nout = sb("nout", [P, NT])
        nin = sb("nin", [P, NT])
        sc5 = sb("sc5", [P, 4, NT])
        selfw = sb("selfw", [128, 2, KD, D])
        wg0 = sb("wg0", [128, KD, E0])
        wg2 = sb("wg2", [128, KD, E2])
        cheb = sb("cheb", [128, 4, KD, D])
        wfx = sb("wfx", [128, KD, 512])
        wx = sb("wx", [128, KD, 512])
        wout = sb("wout", [128, HP, D])
        bd = sb("bd", [128, 4, 128])
        w2T = sb("w2T", [128, KD, D])
        l3w = sb("l3w", [128, KD, D])
        l3we = sb("l3we", [FE, D])
        b1T = sb("b1T", [128, 32 + 64])
        bxT = sb("bxT", [128, HP])
        bias = sb("bias", [P, 8, D])
        bfx = sb("bfx", [P, 512])
        bsl = sb("bsl", [P, HD])
        temp = sb("temp", [P, 8])
        rtemp = sb("rtemp", [P, 8])
        bg0 = sb("bg0", [P, E0])
        bg2 = sb("bg2", [P, E2])
        gate = sb("gate", [P, NT, E2])
        gmax = sb("gmax", [P, NT, 8])
        gidx = sb("gidx", [P, NT, 8], U32)
        gidf = sb("gidf", [P, NT, 2])
        gwt = sb("gwt", [P, NT, 4])
        one_hot = sb("one_hot", [P, 2, NT, E2])
        chosen = sb("chosen", [P, NT, E2], BF16)
        place = sb("place", [P, 2, NT, E2])
        blocks = sb("blocks", [P, 4, E2])
        blocksi = sb("blocksi", [P, E2], I32)
        slotf = sb("slotf", [P, 2, NT])
        slot = sb("slot", [P, 2, NT], I32)
        bexi = sb("bexi", [1, MAXB + 2], I32)
        zrow = sb("zrow", [128, D])
        ARENA = 25040
        arena = sb("arena", [128, ARENA])

        def view(off, shape, dt=F32):
            n = 1
            for s in shape[1:]:
                n *= s
            words = n if dt in (F32, I32) else (n + 1) // 2
            assert off + words <= ARENA, (off, words)
            w = arena[0:shape[0], off:off + words]
            if dt != F32:
                w = w.bitcast(dt)
            names = "abcdef"[:len(shape) - 1]
            if len(shape) > 2:
                w = w.rearrange("p (" + " ".join(names) + ") -> p " + " ".join(names),
                                **{k: s for k, s in zip(names, shape[1:])})
            return w

        MSG = view(0, [P, CHP, D])
        RING = view(20736, [P, 2, SLOTS, D])
        ei = view(5500, [CH, 3, P], I32)
        ef = view(6000, [CH, 4, P])
        red = view(6600, [CH, 2])
        TH = view(6700, [1, 3, NT, CH])
        mm_ = view(7900, [1, 2, CH])
        tou = view(8060, [1, 3, NT, CH])
        lh = view(9260, [1, 8, NT])
        wtmp = view(9300, [P, 2, CH])
        wtb = view(9460, [P, CH], BF16)
        b1r = view(9500, [64, 2, 128])
        bxr = view(9756, [HP, 128])
        w2r = view(9900, [128, 2, D])
        nmul = view(10420, [1, NT, BODIES])
        OHS = view(22784, [P, G, 626], BF16)
        OHB = view(23724, [P, G, 3, 126], BF16)
        OHF = view(24292, [P, G, P])
        iot = view(12000, [P, N], I32)
        DG = view(22784, [P, NT, P])
        RW = view(13000, [128, 2, KD, D])
        XW = view(14100, [P, 2, NT, D])
        W1 = view(0, [128, UB, KD, HID])
        W2 = view(3072, [128, UB, MH, D])
        HT = view(6144, [128, UB, MH, BS])
        XB = view(7680, [BS, UB, D])
        XBT = view(8448, [128, UB, KD, BS])
        YB = view(9216, [BS, UB, D])
        YG = view(10752, [P, 2, NT, D])
        bexp = view(13320, [1, MAXB, E2])
        MO = view(14500, [P, NT, D])
        GW = view(15800, [P, NT, E2])
        GWT = view(15900, [E2, N])
        B2 = view(16600, [E2, D])
        bex = view(13760, [1, MAXB + 2])
        bodies = view(13800, [1, MAXB // UB])
        Y = view(0, [P, 4, NT, D])
        U = view(5120, [P, NT, D])
        S1 = view(6400, [P, NT, D])
        S2 = view(7680, [P, NT, D])
        XMT = view(0, [128, HP, N])
        FX = view(2500, [P, NT, 512])
        SW = view(5060, [P, NT, 512])
        SWT = view(7620, [128, HP, N])
        OXT = view(10120, [128, HP, N])
        hm = view(12620, [P, NT, 8])
        hs = view(12660, [P, NT, 8])
        hr = view(12700, [P, NT, 8])
        rn = view(12740, [128, 512])
        STT = view(13252, [128, HP, 128])
        QT = view(13764, [128, HP, 128])
        KT = view(14276, [128, HP, 128])
        VV = view(14788, [128, HP, 128])
        AT = view(15300, [128, HP, HD])
        am = view(15560, [128, 3, HP])
        ABD = view(15600, [128, HP, 128])
        ATT = view(16112, [128, HP, 128])
        OS = view(16624, [128, HP, 128])
        blk = view(17140, [128, 128])
        w1r = view(0, [128, 2, D])
        w1T = view(512, [128, KD, D])
        b1s = view(1024, [P, D])
        b2s = view(1280, [128, 2, D])
        SCO = view(1792, [P, NT, D])
        TM = view(3072, [P, NT, D])
        COT = view(4352, [128, 2, N])
        CXI = view(5632, [P, NT, 512])
        CXS = view(8192, [P, NT, 512])
        placei = view(13500, [P, NT], I32)
        LB = view(13900, [P, NT, LEAVES], BF16)
        GB = view(14220, [P, NT, LEAVES], BF16)
        COS = view(14540, [128, NT, 2, P])
        SO = view(10752, [128, NT, 2, STEPS])
        CL = view(1792, [P, NT, STEPS])
        tl = view(15820, [P, NT, LEAVES])
        lid = view(16460, [P, 2, NT])
        tn = view(16480, [NT, 9, STEPS])
        tls = view(18860, [NT, 2, LEAVES])
        tb = view(19120, [NT, 12, 16])
        tbi = view(19320, [NT, 2, 8, 2], I32)
        tcnt = view(19360, [NT, 2], I32)
        tnode = view(19364, [NT, STEPS], I32)
        sid = view(19893, [P, NT], I32)
        TW = view(19900, [128, TU, KD, D])

        WEIGHTS_IN = 16 * (12 + 4 + 6 + 8)


        ones_b = sb("ones_b", [P, P], BF16)
        upper_b = sb("upper_b", [P, P], BF16)
        ioleaf = sb("ioleaf", [P, STEPS])
        pcol = sb("pcol", [P, 2])
        pcoli = sb("pcoli", [128, 1], I32)
        nodecol = sb("nodecol", [128, 2])
        levelk = sb("levelk", [NT, 8])

        block = ctx.enter_context(nc.Block())

        def bank_pair(w):
            return [(w, 0, HALF[0]), (w + 1, HALF[0], N)]

        def hidden_slot(b, m):
            return PS[:, 2 + b, m * BS:m * BS + BS]

        def tile_range(eng, t):
            return (eng.value_load(rng[0:1, 0, t:t + 1], min_val=0, max_val=CH - G),
                    eng.value_load(rng[0:1, 1, t:t + 1], min_val=1, max_val=CHP - G + 1),
                    eng.value_load(rng[0:1, 2, t:t + 1], min_val=0, max_val=(NT + 1) * CHP))

        def pass_length(eng):
            return eng.value_load(rng[0:1, 3, 0:1], min_val=G, max_val=NT * CHP)

        def edge_bank(layer, t):
            return 2 + 3 * (t % 2) if layer else 4 * (t % 2)

        def mixture_bodies(eng, second):
            n = eng.value_load(bexi[0:1, MAXB:MAXB + 1], min_val=1, max_val=MAXB // UB)
            before = eng.value_load(bexi[0:1, MAXB + 1:MAXB + 2], min_val=1, max_val=MAXB // UB) if second else 0
            return n, before

        def block_expert(eng, i, b, second):
            return eng.value_load(bexi[0:1, bass.ds(i * UB + b, 1)], min_val=0, max_val=(E2 if second else E0) - 1)

        def yslot(t, base):
            return PS[0:P, base + t // 2, (t % 2) * D:(t % 2) * D + D]

        def tree_weights(eng, half):
            tw = a["L3_ffn_w2s"].rearrange("j (p k) n -> j p k n", k=KD)
            eng.wait_ge(sem("tree_lists"), 1)
            done = 0
            for t in range(NT):
                n = eng.value_load(tcnt[t:t + 1, 0:1], min_val=1, max_val=STEPS // TU)
                with eng.Fori(0, n) as i:
                    for u in range(half, TU, 2):
                        node = eng.value_load(tnode[t:t + 1, bass.ds(i * TU + u, 1)], min_val=0, max_val=NODES - 1)
                        eng.wait_ge(sem(f"tree_w_free{u}"), i + done + 1)
                        eng.dma_start(TW[:, u].rearrange("p (j k) n -> p j k n", j=1),
                                      tw[bass.ds(node, 1)].rearrange("j p k n -> p j k n")).then_inc(sem(f"tree_w_in{u}"), 16)
                done = n + done

        @block.sync
        def _(_sp):
            def bc(x, n=P):
                return x.partition_broadcast(n)

            def feat(w):
                return w.rearrange("(p k) n -> p k n", k=KD)

            for i, n in enumerate(("src", "dst", "edge_type_8")):
                sp.dma_start(ei[:, i, :], a[n].rearrange("(c p) -> c p", p=P)).then_inc(sem("edges_in"), 16)
            sp.dma_start(ef[:, 3, :], a["edge_weight"].rearrange("(c p) -> c p", p=P)).then_inc(sem("edges_in"), 16)
            sp.dma_start(X[:], a["x"].rearrange("(t p) d -> p t d", p=P)).then_inc(sem("x_in"), 16)
            sp.dma_start(b1r[0:32, 0, :], a["L0_ffn_b1"].rearrange("e (m p) -> (e m) p", p=128)).then_inc(sem("prep_in"), 16)
            sp.dma_start(b1r[0:64, 1, :], a["L2_ffn_b1"].rearrange("e (m p) -> (e m) p", p=128)).then_inc(sem("prep_in"), 16)
            sp.dma_start(bxr, a["L1_ffn_b_x"].rearrange("(m p) -> m p", p=128)).then_inc(sem("prep_in"), 16)
            sp.dma_start(w2r, a["L2_gnn_W"].rearrange("(o p) f -> p o f", p=128)).then_inc(sem("prep_in"), 16)
            if stop > 0:
                for b in range(2):
                    sp.dma_start(RW[:, b], a["L0_gnn_W1"].rearrange("r (p k) n -> r p k n", k=KD)[b]).then_inc(sem(f"rw_in{b}"), 16)
            for dst, src in [(selfw[:, 0], feat(a["L0_gnn_self_w1"])), (selfw[:, 1], feat(a["L0_gnn_self_w2"])),
                             (bias[:, 0, :], bc(a["L0_gnn_b1"])), (bias[:, 1, :], bc(a["L0_gnn_b2"]))]:
                sp.dma_start(dst, src).then_inc(sem("layer_weights_in"), 16)

            def later_weights():
                loads = [
                    (wg0[:], feat(a["L0_ffn_Wg"])), (wg2[:], feat(a["L2_ffn_gate_w"])),
                    (wfx[:], feat(a["L1_ffn_W_fx"])), (wx[:], feat(a["L1_ffn_W_x"])),
                    (wout[:], a["L1_ffn_W_out"].rearrange("(m p) n -> p m n", p=128)),
                    (l3w[:], feat(a["L3_gnn_weight"][0:D, :])), (l3we[:], a["L3_gnn_weight"][D:D + FE, :]),
                    (bfx[:], bc(a["L1_ffn_b_fx"])), (bsl[:], bc(a["L1_ffn_b_slice"])),
                    (temp[:], bc(a["L1_ffn_temperature"].rearrange("a h b c -> (a h b c)"))),
                    (bg0[:], bc(a["L0_ffn_bg"])), (bg2[:], bc(a["L2_ffn_gate_b"])),
                ]
                loads += [(cheb[:, k], feat(a["L1_gnn_weight"][k])) for k in range(4)]
                loads += [(bias[:, 2 + i, :], bc(a[n])) for i, n in enumerate(
                    ("L1_gnn_bias", "L1_ffn_b_out", "L2_gnn_b", "L2_ffn_gamma", "L2_ffn_beta", "L3_gnn_bias"))]
                for dst, src in loads:
                    sp.dma_start(dst, src).then_inc(sem("weights_in"), 16)
                sp.wait_ge(sem("bd_zeroed"), 1)
                for i, n in enumerate(("L1_ffn_W_slice", "L1_ffn_W_q", "L1_ffn_W_k", "L1_ffn_W_v")):
                    for h in range(2):
                        sp.dma_start(bd[h * HD:h * HD + HD, i, h * HD:h * HD + HD], a[n]).then_inc(sem("weights_in"), 16)
                assert 16 * (len(loads) + 8) == WEIGHTS_IN

            def zero_slots(tag):
                sp.dma_start(slots[tag].rearrange("(b p) d -> p b d", p=BS),
                             zrow[:].unsqueeze(1).to_broadcast([BS, MAXB, D])).then_inc(sem("slots_zeroed"), 16)

            if stop > 0:
                for b in range(2):
                    sp.sem_inc(sem(f"xw_stored{b}"), 16)
                    sp.sem_inc(sem(f"xw_copied{b}"), 1)
                for layer, n in enumerate(("L0_gnn_W1", "L0_gnn_W2")):
                    wv = a[n].rearrange("r (p k) n -> r p k n", k=KD)
                    tv = table.rearrange("(r t p) d -> r p t d", t=NT, p=P)
                    if layer:
                        sp.wait_ge(sem("msg_copied"), CHP)
                        later_weights()
                        sp.wait_ge(sem("edge_tile_mm"), NT)
                        for b in range(2):
                            sp.dma_start(RW[:, b], wv[b]).then_inc(sem(f"rw_in{b}"), 16)

                    def store(i, b):
                        sp.wait_ge(sem(f"xw_copied{b}"), i + (layer * (R // 2) + 2))
                        sp.dma_start(tv[bass.ds(i * 2 + b, 1)].rearrange("r p t d -> p (r t) d"),
                                     XW[:, b]).then_inc(sem(f"xw_stored{b}"), 16)

                    def attributes(i):
                        if layer == 0:
                            q = CH // 4
                            sp.dma_start(EA[:, bass.ds(i * q, q), :], a["edge_attr_64"].rearrange("(c p) f -> p c f", p=P)[:, bass.ds(i * q, q), :]).then_inc(sem("attr_in"), 16)

                    with sp.Fori(0, R // 2 - 1) as i:
                        for b in range(2):
                            sp.wait_ge(sem(f"rel_mm{b}"), i + (layer * (R // 2) + 1))
                            sp.dma_start(RW[:, b].rearrange("p (r k) n -> p r k n", r=1),
                                         wv[bass.ds(i * 2 + (b + 2), 1)].rearrange("r p k n -> p r k n")).then_inc(sem(f"rw_in{b}"), 16)
                            store(i, b)
                        attributes(i)
                    for b in range(2):
                        store(R // 2 - 1, b)
                    attributes(R // 2 - 1)
                sp.wait_ge(sem("msg_copied"), 2 * CHP)
                zero_slots("moe0_")

            def experts(tag, second, w1, w2, b2):
                w2v = a[w2].rearrange("e (m p) n -> e p m n", p=128)
                w1v = a[w1].rearrange("e (p k) h -> e p k h", k=KD)
                xv = slots[tag].rearrange("(b p) d -> b p d", p=BS)
                sp.wait_ge(sem("routed"), second + 1)
                sp.dma_start(B2[0:(E2 if second else E0), :], a[b2]).then_inc(sem("b2_in"), 16)
                n, before = mixture_bodies(sp, second)
                with sp.Fori(0, n) as i:
                    expert = [block_expert(sp, i, b, second) for b in range(UB)]

                    def load_w1(b):
                        sp.wait_ge(sem(f"w1_free{b}"), i + before + 1)
                        sp.dma_start(W1[:, b].rearrange("p (e k) h -> p e k h", e=1),
                                     w1v[bass.ds(expert[b], 1)].rearrange("e p k h -> p e k h")).then_inc(sem(f"w1_in{b}"), 16)

                    def load_tokens(b):
                        sp.wait_ge(sem(f"xb_free{b}"), i + before + 1)
                        sp.wait_ge(sem("dispatched"), 16 * 2 * NT * (second + 1))
                        sp.dma_start(XB[:, b].rearrange("p (e d) -> p e d", e=1),
                                     xv[bass.ds(i * UB + b, 1)].rearrange("e p d -> p e d")).then_inc(sem(f"x_block_in{b}"), 16)

                    def load_w2(b):
                        sp.wait_ge(sem(f"w2_free{b}"), i + before + 1)
                        sp.dma_start(W2[:, b].rearrange("p (e m) h -> p e m h", e=1),
                                     w2v[bass.ds(expert[b], 1)].rearrange("e p m h -> p e m h")).then_inc(sem(f"w2_in{b}"), 16)

                    load_w1(0)
                    load_w1(1)
                    load_tokens(0)
                    load_tokens(1)
                    load_w2(0)
                    load_tokens(2)
                    load_w1(2)
                    load_w2(1)
                    load_w2(2)

            if stop > 1:
                experts("moe0_", 0, "L0_ffn_W1", "L0_ffn_W2", "L0_ffn_b2")
            if stop > 5:
                zero_slots("moe2_")
            if stop > 5:
                experts("moe2_", 1, "L2_ffn_w1", "L2_ffn_w2", "L2_ffn_b2")
            if stop > 7:
                sp.wait_ge(sem("arena_free_for_tree"), 1)
                sp.dma_start(w1r[:, 0, :], a["L3_ffn_w1s"][0:128, :]).then_inc(sem("tree_in"), 16)
                sp.dma_start(w1r[0:127, 1, :], a["L3_ffn_w1s"][128:255, :]).then_inc(sem("tree_in"), 16)
                sp.dma_start(b2s[:, 0, :], a["L3_ffn_b2s"][0:128, :]).then_inc(sem("tree_in"), 16)
                sp.dma_start(b2s[0:127, 1, :], a["L3_ffn_b2s"][128:255, :]).then_inc(sem("tree_in"), 16)
                sp.dma_start(b1s[:, 0:NODES], bc(a["L3_ffn_b1s"])).then_inc(sem("tree_in"), 16)
                sp.wait_ge(sem("tree_features_stored"), 16 * NT)
                sp.dma_start(XN[:], features_by_leaf.rearrange("(t p) d -> p t d", p=P)).then_inc(sem("tree_features_in"), 16)
                sp.wait_ge(sem("tree_rows_stored"), 16 * NT)
                sp.dma_start(CXS, rows_by_leaf.rearrange("(t p) d -> p t d", p=P)).then_inc(sem("tree_rows_in"), 16)
                tree_weights(sp, 0)
            if stop < 8:
              sp.wait_ge(sem("x_final"), 1)
              sp.dma_start(out.rearrange("(t p) d -> p t d", p=P), X[:]).then_inc(sem("out_stored"), 16)
              sp.wait_ge(sem("out_stored"), 16)

        @block.gpsimd
        def _(_p):
            pool.memset(ident[:], 0.0)
            pool.memset(eps[:], EPS)
            pool.memset(ones[:], 1.0)
            pool.memset(zeros[:], 0.0)
            pool.memset(bd[:], 0.0)
            pool.memset(zrow[:], 0.0)
            pool.memset(ones_b[:], 1.0)
            pool.memset(upper_b[:], 1.0)
            for d in range(DEPTH):
                pool.memset(levelk[:, d:d + 1], float(2 ** d - 1))
            pool.drain().then_inc(sem("bd_zeroed"), 1)
            pool.affine_select(out=ident[:], in_=ident[:], compare_op=ALU.not_equal, fill=1.0, base=0,
                               pattern=[[-1, 128]], channel_multiplier=1)
            pool.affine_select(out=upper_b[:], in_=upper_b[:], compare_op=ALU.is_gt, fill=0.0, base=0,
                               pattern=[[1, P]], channel_multiplier=-1)
            pool.iota(pcoli[:], pattern=[[1, 1]], base=0, channel_multiplier=1)
            pool.iota(iot, pattern=[[1, N]], base=0, channel_multiplier=0)
            pool.iota(TH[:, 0].bitcast(I32), pattern=[[P, NT], [0, CH]], base=0, channel_multiplier=0)
            pool.iota(TH[:, 1].bitcast(I32), pattern=[[P, NT], [0, CH]], base=P, channel_multiplier=0)
            pool.iota(TH[:, 2].bitcast(I32), pattern=[[0, NT], [1, CH]], base=0, channel_multiplier=0)
            pool.memset(EF[:, :, CH:CHP], -1.0)
            pool.memset(WP3[:, :, CH:CHP], 0.0)
            pool.memset(EA[:, CH:CHP, :], 0.0)
            pool.memset(MSG[:, CH:CHP, :], 0.0)
            pool.drain().then_inc(sem("consts"), 1)
            def experts(tag, second):
                pool.wait_ge(sem("slots_zeroed"), 16 * (second + 1))
                pool.wait_ge(sem("routed"), second + 1)
                for k in range(2):
                    for t in range(NT):
                        pool.indirect_dma_start(
                            out=slots[tag], out_offset=bass.IndirectOffsetOnAxis(ap=slot[:, k, t:t + 1], axis=0),
                            in_=XN[:, t, :], in_offset=None).then_inc(sem("dispatched"), 16)
                n, before = mixture_bodies(pool, second)
                for b in range(UB):
                    pool.wait_ge(sem(f"y_stored{b}"), (n + before) * 16 + 16)
                pool.sem_inc(sem("seen"), 1)
                for t in range(NT):
                    for k in range(2):
                        pool.indirect_dma_start(
                            out=YG[:, k, t, :], out_offset=None, in_=slots[tag],
                            in_offset=bass.IndirectOffsetOnAxis(ap=slot[:, k, t:t + 1], axis=0)).then_inc(sem(f"collected{t}"), 16)

            if stop > 0:
                pool.wait_ge(sem("edge_fields"), 1)
                for layer in range(2):
                    for b in range(2):
                        pool.wait_ge(sem(f"xw_stored{b}"), 16 * (R // 2) * (layer + 1) + 16)
                    groups = CH // (2 * SLOTS)
                    with pool.Fori(0, groups) as g:
                        for h in range(2):
                            pool.wait_ge(sem(f"slots_free{h}"), g * SLOTS + (layer * groups + 1) * SLOTS)
                            pool.tensor_copy(gis[:, h, :], GI[:, bass.ds(g * (2 * SLOTS) + h * SLOTS, SLOTS)]).then_inc(sem("idx_staged"), 1)
                            pool.wait_ge(sem("idx_staged"), g * 2 + (layer * groups * 2 + h + 1))
                            pool.sem_inc(sem("seen"), 1)
                            for s in range(SLOTS):
                                pool.indirect_dma_start(
                                    out=RING[:, h, s, :], out_offset=None, in_=table,
                                    in_offset=bass.IndirectOffsetOnAxis(ap=gis[:, h, s:s + 1], axis=0),
                                ).then_inc(sem(f"gathered{h}_{s}"), 16)

            if stop > 1:
                experts("moe0_", 0)
            if stop > 5:
                experts("moe2_", 1)
            if stop > 7:
                for n, (to, rows, stored) in enumerate(((features_by_leaf, XN, "tree_features_stored"), (rows_by_leaf, CXI, "tree_rows_stored"))):
                    pool.wait_ge(sem("tree_operands"), 4 + n)
                    for t in range(NT):
                        pool.indirect_dma_start(
                            out=to, out_offset=bass.IndirectOffsetOnAxis(ap=placei[:, t:t + 1], axis=0),
                            in_=rows[:, t, :], in_offset=None).then_inc(sem(stored), 16)
                for t in range(NT):
                    pool.wait_ge(sem("x_final"), t + 1)
                    pool.indirect_dma_start(
                        out=out, out_offset=bass.IndirectOffsetOnAxis(ap=sid[:, t:t + 1], axis=0),
                        in_=CXS[:, t, D:2 * D], in_offset=None).then_inc(sem("out_stored"), 16)
                pool.wait_ge(sem("out_stored"), 16 * NT)

        @block.scalar
        def _(_a):
            def stats(li):
                if li == 0:
                    act.wait_ge(sem("consts"), 1)
                for t in range(NT):
                    act.wait_ge(sem("var_ready"), NT * li + t + 1)
                    act.activation(std5[:, t:t + 1], mv[:, t, 1:2], ACT.Sqrt, bias=eps[:]).then_inc(sem("std_ready"), 1)

            def features(fi):
                act.wait_ge(sem("xt_mm"), 2 * fi + 1)
                act.copy(XT[:, 0, 0:500], PS[:, 0, 0:500]).then_inc(sem("xt_ready_act"), 1)
                act.wait_ge(sem("xt_mm"), 2 * fi + 2)
                act.copy(XT[:, :, 500:N], PS[:, 2, 0:2 * P].rearrange("p (k n) -> p k n", k=2)).then_inc(sem("xt_ready_act"), 1)

            def degrees():
                act.wait_ge(sem("degrees"), 1)
                act.activation(sc5[:, 1:4, :], sc5[:, 1:4, :], ACT.Sqrt).then_inc(sem("degree_roots"), 1)

            def relational(layer):
                with act.Fori(0, R // 2) as i:
                    for b in range(2):
                        act.wait_ge(sem(f"rel_mm{b}"), i + (layer * (R // 2) + 1))
                        act.wait_ge(sem(f"xw_stored{b}"), i * 16 + (layer * (R // 2) + 1) * 16)
                        act.copy(XW[:, b, 0:2, :], PS[0:P, 3 * b, :].rearrange("p (t d) -> p t d", t=2))
                        act.copy(XW[:, b, 2:4, :], PS[0:P, 3 * b + 1, :].rearrange("p (t d) -> p t d", t=2))
                        act.copy(XW[:, b, 4, :], PS[0:P, 3 * b + 2, 0:D]).then_inc(sem(f"xw_copied{b}"), 1)
                if layer:
                    act.wait_ge(sem("edge_tile_mm"), NT)
                else:
                    act.wait_ge(sem("prep_out"), 1)
                groups = CH // (2 * SLOTS)
                with act.Fori(0, groups) as g:
                    for h in range(2):
                        for s in range(SLOTS):
                            act.wait_ge(sem(f"gathered{h}_{s}"), g * 16 + (layer * groups + 1) * 16)
                            act.copy(MSG[:, bass.ds(g * (2 * SLOTS) + (h * SLOTS + s), 1), :], RING[:, h, s:s + 1, :]).then_inc(sem("msg_copied"), 1)
                        act.drain().then_inc(sem(f"slots_free{h}"), SLOTS)
                act.sem_inc(sem("msg_copied"), CHP - CH)

            def experts(tag, second, func, b1off):
                yv = slots[tag].rearrange("(b p) d -> b p d", p=BS)
                act.wait_ge(sem("routed"), second + 1)
                n, before = mixture_bodies(act, second)
                if not second:
                    degrees()
                with act.Fori(0, n) as i:
                    experts_of = [block_expert(act, i, b, second) for b in range(UB)]
                    for b, e in enumerate(experts_of):
                        act.wait_ge(sem(f"w2_free{b}"), i + before + 1)
                        act.wait_ge(sem(f"w1_free{b}"), i + before + 2)
                        act.sem_inc(sem("seen"), 1)
                        for m in range(MH):
                            act.activation(HT[:, b, m, :], hidden_slot(b, m), func,
                                           bias=b1T[:, bass.ds(e * MH + (b1off + m), 1)]).then_inc(sem("hidden"), 1)
                    for b in range(UB):
                        act.wait_ge(sem(f"y_out{b}"), i + before + 2)
                        act.dma_start(yv[bass.ds(i * UB + b, 1)].rearrange("e p d -> p e d"),
                                      YB[:, b].rearrange("p (e d) -> p e d", e=1)).then_inc(sem(f"y_stored{b}"), 16)

            if stop > 0:
                for h in range(2):
                    act.sem_inc(sem(f"slots_free{h}"), SLOTS)
            if stop > 0:
                stats(0)
                features(0)
                relational(0)
                features(1)
                relational(1)
                stats(1)
            if stop > 1:
                features(2)
                experts("moe0_", 0, ACT.Gelu, 0)
                stats(2)
            if stop > 2:
                features(3)
                stats(3)
            if stop > 3:
                features(4)
                for m in range(HP):
                    act.wait_ge(sem("xmt_mm"), m + 1)
                    for bank, c0, c1 in bank_pair((m % 2) * 2):
                        last = act.activation(XMT[:, m, c0:c1], PS[:, bank, 0:c1 - c0], ACT.Identity, bias=bxT[:, m:m + 1])
                    last.then_inc(sem("xmt"), 1)
                for t in range(NT):
                    act.wait_ge(sem("slice_shifted"), t + 1)
                    act.activation(SW[:, t, :], SW[:, t, :], ACT.Exp).then_inc(sem("slice_exp"), 1)
                for m in range(HP):
                    act.wait_ge(sem("swt_mm"), m + 1)
                    b0 = 2 + (m % 2) * 2
                    act.copy(SWT[:, m, 0:500], PS[:, b0, 0:500])
                    act.copy(SWT[:, m, 500:N], PS[:, b0 + 1, 0:P]).then_inc(sem("swt"), 1)
                act.wait_ge(sem("attn_shifted"), 1)
                act.activation(AT, AT, ACT.Exp, scale=HD ** -0.5).then_inc(sem("attn_exp"), 1)
                for m in range(HP):
                    act.wait_ge(sem("oxt_mm"), m + 1)
                    for bank, c0, c1 in bank_pair(4 if m % 2 == 0 else 0):
                        last = act.copy(OXT[:, m, c0:c1], PS[:, bank, 0:c1 - c0])
                    last.then_inc(sem("oxt"), 1)
                stats(4)
            if stop > 4:
                features(5)
                stats(5)
            if stop > 5:
                features(6)
                act.wait_ge(sem("top2_diff"), 1)
                act.activation(gwt[:, :, 1], gwt[:, :, 0], ACT.Exp).then_inc(sem("top2_exp"), 1)
                experts("moe2_", 1, ACT.Relu, 32)
                stats(6)
                stats(7)
            if stop > 6:
                features(7)
                stats(8)
            if stop > 7:
                features(8)
                act.wait_ge(sem("tree_scores"), 1)
                act.activation(CXI[:, :, 0:NODES], SCO[:, :, 0:NODES], ACT.Abs).then_inc(sem("tree_abs"), 1)
                act.wait_ge(sem("tree_abs"), 1)
                act.activation(CXI[:, :, 0:NODES], CXI[:, :, 0:NODES], ACT.Gelu).then_inc(sem("tree_gelu"), 1)
                act.wait_ge(sem("tree_products"), 5)
                for k in range(KD):
                    act.copy(XT[:, k, 0:500], PS[:, 5 + k, 0:500])
                act.copy(XT[:, :, 500:N], PS[:, 7, 0:2 * P].rearrange("p (k n) -> p k n", k=2)).then_inc(sem("tree_sorted_out"), 1)
                act.wait_ge(sem("tree_products"), 7)
                for j in range(0, 2 * NT, 4):
                    n = min(4, 2 * NT - j)
                    last = act.copy(COS[:].rearrange("p t o n -> p (t o n)")[:, j * P:(j + n) * P], PS[:, 5 + j // 4, 0:n * P])
                last.then_inc(sem("tree_sorted_out"), 1)
                for t in range(NT):
                    act.wait_ge(sem("tree_products"), 8 + t)
                    act.copy(CL[:, t, :], PS[0:P, t, 0:STEPS]).then_inc(sem("tree_sorted_out"), 1)
                tree_weights(act, 1)

        @block.tensor
        def _(_t):
            edges = EdgePasses()

            def rows(j=0):
                return slice(j * P, j * P + P)

            def features(fi):
                for t in range(NT - 1):
                    pe.wait_ge(sem("xn_ready"), NT * fi + t + 1)
                    for k in range(KD):
                        last = pe.transpose(PS[:, k, rows(t)], XNk[:, t, k, :], ident[0:P, 0:P])
                last.then_inc(sem("xt_mm"), 1)
                pe.wait_ge(sem("xn_ready"), NT * fi + NT)
                for k in range(KD):
                    last = pe.transpose(PS[:, 2, rows(k)], XNk[:, NT - 1, k, :], ident[0:P, 0:P])
                last.then_inc(sem("xt_mm"), 1)
                pe.wait_ge(sem("xt_ready"), fi + 1)
                pe.wait_ge(sem("xt_ready_act"), 2 * fi + 2)

            def rowprod(dst, w, t, n=None, start=True, stop_=True):
                for k in range(KD):
                    last = pe.matmul(dst, XT[:, k, rows(t)], w[:, k, :] if n is None else w[:, k, n],
                                     start=start and k == 0, stop=stop_ and k == KD - 1, skip_group_check=True)
                return last

            def edge_fields():
                pe.wait_ge(sem("edge_rows"), 1)
                for i in range(4):
                    pe.transpose(PS[0:P, 3, i * CH:i * CH + CH], ef[:, i, :], ident[0:CH, 0:CH])
                for i in range(2):
                    last = pe.transpose(PS[0:1, 4, i * CH:i * CH + CH], red[:, i:i + 1], ident[0:CH, 0:CH])
                last.then_inc(sem("edge_cols"), 1)
                pe.wait_ge(sem("prep_in"), 64)
                pe.transpose(PS[:, 6, 0:32], b1r[0:32, 0, :], ident[0:32, 0:32])
                pe.transpose(PS[:, 6, 32:96], b1r[0:64, 1, :], ident[0:64, 0:64])
                pe.transpose(PS[:, 6, 96:100], bxr, ident[0:HP, 0:HP])
                w2rk = w2r.rearrange("p o (f k) -> p o k f", k=KD)
                for k in range(KD):
                    for o in range(2):
                        last = pe.transpose(PS[:, 7, (k * 2 + o) * 128:(k * 2 + o) * 128 + 128], w2rk[:, o, k, :], ident[:])
                last.then_inc(sem("prep_mm"), 1)

            def over_edges(t, opening, step_of_chunk, closing):
                if t not in edges.ranges:
                    edges.ranges[t] = tile_range(pe, t)
                lo, hi, count = edges.ranges[t]
                count = edges.done + count
                opening()
                with pe.Fori(lo, hi, G) as c:
                    for b in range(G):
                        pe.wait_ge(sem("oh_ready"), c + count + (b + 1))
                        step_of_chunk(c + b, b).then_inc(sem("oh_free"), 1)
                return closing()

            def zero_products(banks, start):
                for bank, n in banks:
                    last = pe.matmul(PS[0:P, bank, 0:n], zeros[0:P, 0:P], zeros[0:P, 0:n],
                                     start=start, stop=not start, skip_group_check=True)
                return last

            def edge_tiles(layer):
                pe.wait_ge(sem("layer_weights_in"), 64)
                for t in range(NT):
                    b0 = edge_bank(layer, t)
                    banks = [(b0, HALF[0]), (b0 + 1, HALF[1])] + ([] if layer else [(b0 + 3, FE)])
                    acc = PS[0:P, b0 + 2, 0:D]
                    if t >= 2:
                        pe.wait_ge(sem("edge_tile_done"), layer * NT + t - 1)

                    def opening():
                        zero_products(banks, True)
                        rowprod(acc, selfw[:, layer], t, stop_=False)

                    def chunk(c, b):
                        for i in range(3 if layer else 1):
                            for bank, c0, c1 in bank_pair(b0):
                                pe.matmul(PS[0:P, bank, 0:c1 - c0], OHB[:, b, i, 0:P], OHS[:, b, c0:c1],
                                          start=False, stop=False, skip_group_check=True)
                        if layer == 0:
                            pe.matmul(PS[0:P, b0 + 3, 0:FE], OHF[:, b, :], EA[:, bass.ds(c, 1), :],
                                      start=False, stop=False, skip_group_check=True)
                        pe.wait_ge(sem("msg_copied"), c + (layer * CHP + 1))
                        return pe.matmul(acc, OHF[:, b, :], MSG[:, bass.ds(c, 1), :],
                                         start=False, stop=False, skip_group_check=True)

                    over_edges(t, opening, chunk,
                               lambda: zero_products(banks + [(b0 + 2, D)], False)).then_inc(sem("edge_tile_mm"), 1)
                edges.done = edges.all + edges.done
                pe.wait_ge(sem("edge_tile_done"), (layer + 1) * NT)

            def transposed_counts():
                for j in range(NT):
                    last = pe.transpose(PS[0:FE, 4 + j // 4, rows(j % 4)], AE[:, j, :], ident[0:P, 0:P])
                last.then_inc(sem("ct_mm"), 1)
                for i in range(NT):
                    if i >= 2:
                        pe.wait_ge(sem("ct_copied"), i)
                    for j in range(NT):
                        last = pe.transpose(PS[0:P, (6 if i % 2 == 0 else 0) + j // 4, rows(j % 4)], C[:, j, rows(i)], ident[0:P, 0:P])
                    last.then_inc(sem("ct_mm"), 1)
                pe.wait_ge(sem("ct_copied"), NT + 1)

            def relational(layer):
                with pe.Fori(0, R // 2) as i:
                    for b in range(2):
                        pe.wait_ge(sem(f"rw_in{b}"), i * 16 + (layer * (R // 2) + 1) * 16)
                        pe.wait_ge(sem(f"xw_copied{b}"), i + (layer * (R // 2) + 1))
                        for t in range(NT):
                            last = rowprod(yslot(t, 3 * b), RW[:, b], t)
                        last.then_inc(sem(f"rel_mm{b}"), 1)
                for b in range(2):
                    pe.wait_ge(sem(f"xw_copied{b}"), (R // 2) * (layer + 1) + 1)
                if layer == 0:
                    pe.wait_ge(sem("ranges"), 1)
                    pe.sem_inc(sem("oh_free"), CHP + G)
                    edges.all = pass_length(pe)
                    pe.wait_ge(sem("attr_in"), 64)
                if layer:
                    transposed_counts()
                edge_tiles(layer)

            def experts(second, ne, wg):
                for t in range(NT):
                    last = rowprod(PS[0:P, 7, t * ne:t * ne + ne], wg, t)
                last.then_inc(sem("route_mm"), 1)
                pe.wait_ge(sem("chosen"), second + 1)
                for t in range(NT):
                    dst = PS[0:P, 6, t * ne:t * ne + ne]
                    for u in range(t):
                        pe.matmul(dst, ones_b[:], chosen[:, u, 0:ne], start=(u == 0), stop=False, skip_group_check=True)
                    pe.matmul(dst, upper_b[:], chosen[:, t, 0:ne], start=(t == 0), stop=True, skip_group_check=True)
                for t in range(NT):
                    last = pe.matmul(PS[0:P, 5, 0:ne], ones_b[:], chosen[:, t, 0:ne], start=(t == 0), stop=(t == NT - 1), skip_group_check=True)
                last.then_inc(sem("route_mm"), 1)
                pe.wait_ge(sem("routed"), second + 1)
                if not second:
                    for b in range(UB):
                        for name in ("w1_free", "w2_free", "xb_free", "y_out"):
                            pe.sem_inc(sem(f"{name}{b}"), 1)
                    pe.sem_inc(sem("hidden"), UB * MH)
                pe.wait_ge(sem("bias_operands"), 2 * second + 1)
                for t in range(NT):
                    last = pe.transpose(PS[0:ne, 5 + t // 4, rows(t % 4)], GW[:, t, 0:ne], ident[0:P, 0:P])
                last.then_inc(sem("bias_mm"), 1)
                pe.wait_ge(sem("bias_operands"), 2 * second + 2)
                pe.wait_ge(sem("b2_in"), 16 * (second + 1))
                for t in range(NT):
                    last = pe.matmul(yslot(t, 5), GWT[0:ne, rows(t)], B2[0:ne, :], start=True, stop=True)
                last.then_inc(sem("bias_mm"), 1)
                pe.wait_ge(sem("bias_added"), second + 1)
                n, before = mixture_bodies(pe, second)
                def tokens(i, b):
                    pe.wait_ge(sem(f"x_block_in{b}"), (i + before) * 16 + 16)
                    for k in range(KD):
                        last = pe.transpose(PS[:, b % 2, k * BS:k * BS + BS],
                                            XB[:, b, :].rearrange("p (f k) -> p k f", k=KD)[:, k, :], ident[:])
                    last.then_inc(sem(f"xb_free{b}"), 1)

                def hidden(i, b):
                    pe.wait_ge(sem(f"w1_in{b}"), (i + before) * 16 + 16)
                    pe.wait_ge(sem("xbt"), (i + before) * UB + b + 1)
                    pe.wait_ge(sem("hidden"), (i + before) * (UB * MH) + (b + 1) * MH)
                    for m in range(MH):
                        for k in range(KD):
                            last = pe.matmul(hidden_slot(b, m), W1[:, b, k, m * 128:m * 128 + 128], XBT[:, b, k, :],
                                             start=(k == 0), stop=(k == KD - 1), skip_group_check=True)
                    last.then_inc(sem(f"w1_free{b}"), 1)

                def outputs(i, b):
                    pe.wait_ge(sem(f"w2_in{b}"), (i + before) * 16 + 16)
                    pe.wait_ge(sem(f"y_out{b}"), i + before + 1)
                    for m in range(MH):
                        pe.wait_ge(sem("hidden"), (i + before) * (UB * MH) + (UB * MH + b * MH + m + 1))
                        last = pe.matmul(PS[:, 5 + b, 0:D], HT[:, b, m, :], W2[:, b, m, :], start=(m == 0), stop=(m == MH - 1))
                    last.then_inc(sem(f"w2_free{b}"), 1)

                with pe.Fori(0, n) as i:
                    tokens(i, 0)
                    tokens(i, 1)
                    hidden(i, 0)
                    tokens(i, 2)
                    hidden(i, 1)
                    outputs(i, 0)
                    hidden(i, 2)
                    outputs(i, 1)
                    outputs(i, 2)

            def spmm(mat, rhs, i, dst, stop_=True):
                for j in range(NT):
                    last = pe.matmul(dst, mat[:, j, rows(i)], rhs(j), start=(j == 0), stop=stop_ and j == NT - 1,
                                     skip_group_check=True)
                return last

            pe.wait_ge(sem("consts"), 1)
            if stop > 0:
                edge_fields()
                features(0)
                pe.wait_ge(sem("edge_fields"), 1)
                relational(0)
                features(1)
                relational(1)
            pe.wait_ge(sem("weights_in"), WEIGHTS_IN)
            if stop > 1:
                features(2)
                experts(0, E0, wg0)
            if stop > 2:
                features(3)
                def filtered(w, base):
                    for t in range(NT):
                        last = rowprod(yslot(t, base), cheb[:, w], t)
                    last.then_inc(sem("cheb_mm"), 1)

                def neighbours(r):
                    pe.wait_ge(sem("cheb_u"), NT * (r + 1))
                    for i in range(NT):
                        spmm(C, lambda j: (U, S1, U)[r][:, j, :], i, PS[0:P, 3 + i, 0:D]).then_inc(sem("cheb_spmm"), 1)

                filtered(3, 3)
                filtered(2, 0)
                neighbours(0)
                pe.wait_ge(sem("cheb_y"), 2)
                filtered(1, 0)
                neighbours(1)
                pe.wait_ge(sem("cheb_y"), 3)
                filtered(0, 0)
                neighbours(2)
            if stop > 3:
                features(4)
                for m in range(HP):
                    for bank, c0, c1 in bank_pair((m % 2) * 2):
                        if m >= 2:
                            pe.wait_ge(sem("xmt"), m - 1)
                        for k in range(KD):
                            last = pe.matmul(PS[:, bank, 0:c1 - c0], wx[:, k, m * 128:m * 128 + 128], XT[:, k, c0:c1],
                                             start=(k == 0), stop=(k == KD - 1))
                    last.then_inc(sem("xmt_mm"), 1)
                pe.wait_ge(sem("xmt"), HP)
                for t in range(NT):
                    if t >= 2:
                        pe.wait_ge(sem("slice_shifted"), t - 1)
                    for m in range(HP):
                        last = pe.matmul(PS[0:P, 6 + t % 2, m * 128:m * 128 + 128], XMT[:, m, rows(t)], bd[:, 0, :],
                                         start=True, stop=True)
                    last.then_inc(sem("logit_mm"), 1)
                    if t >= 2:
                        pe.wait_ge(sem("fx"), t - 1)
                    rowprod(PS[0:P, 4 + t % 2, :], wfx, t).then_inc(sem("fx_mm"), 1)
                pe.wait_ge(sem("fx"), NT)
                for c0 in (0, D):
                    pe.matmul(PS[:, 0, c0:c0 + D], zeros[:, 0:128], zeros[:, 0:D], start=True, stop=False, skip_group_check=True)
                for t in range(NT):
                    pe.wait_ge(sem("slice_w"), t + 1)
                    pe.matmul(PS[:, 1, :], ones[:, :], SW[:, t, :], start=(t == 0), stop=(t == NT - 1), skip_group_check=True)
                    for m in range(HP):
                        last = pe.matmul(PS[:, 0, m * 128:m * 128 + 128], FX[:, t, m * 128:m * 128 + 128],
                                         SW[:, t, m * 128:m * 128 + 128], start=False, stop=(t == NT - 1), skip_group_check=True)
                last.then_inc(sem("attn_products"), 1)
                for m in range(HP):
                    if m >= 2:
                        pe.wait_ge(sem("swt"), m - 1)
                    for t in range(NT):
                        last = pe.transpose(PS[:, 2 + (m % 2) * 2 + t // 4, rows(t % 4)], SW[:, t, m * 128:m * 128 + 128], ident[0:P, 0:P])
                    last.then_inc(sem("swt_mm"), 1)
                pe.wait_ge(sem("attn_operands"), 1)
                pe.wait_ge(sem("swt"), HP)
                for w, bank in ((1, 2), (2, 3)):
                    for m in range(HP):
                        last = pe.matmul(PS[:, bank, m * 128:m * 128 + 128], bd[:, w, :], STT[:, m, :], start=True, stop=True)
                for m in range(HP):
                    last = pe.matmul(PS[:, 4, m * 128:m * 128 + 128], STT[:, m, :], bd[:, 3, :], start=True, stop=True)
                last.then_inc(sem("attn_products"), 1)
                pe.wait_ge(sem("attn_operands"), 2)
                for m in range(HP):
                    last = pe.matmul(PS[:, 0, m * 128:m * 128 + 128], QT[:, m, :], KT[:, m, :], start=True, stop=True)
                last.then_inc(sem("attn_products"), 1)
                pe.wait_ge(sem("attn_operands"), 3)
                for m in range(HP):
                    last = pe.transpose(PS[:, 1, m * 128:m * 128 + 128], ABD[:, m, :], ident[:])
                last.then_inc(sem("attn_products"), 1)
                pe.wait_ge(sem("attn_operands"), 4)
                for m in range(HP):
                    last = pe.matmul(PS[:, 2, m * 128:m * 128 + 128], ATT[:, m, :], VV[:, m, :], start=True, stop=True)
                last.then_inc(sem("attn_products"), 1)
                pe.wait_ge(sem("attn_operands"), 5)
                for m in range(HP):
                    for bank, c0, c1 in bank_pair(4 if m % 2 == 0 else 0):
                        if m >= 2:
                            pe.wait_ge(sem("oxt"), m - 1)
                        last = pe.matmul(PS[:, bank, 0:c1 - c0], OS[:, m, :], SWT[:, m, c0:c1], start=True, stop=True)
                    last.then_inc(sem("oxt_mm"), 1)
                pe.wait_ge(sem("oxt"), HP)
                for t in range(NT):
                    for m in range(HP):
                        last = pe.matmul(PS[0:P, 3 + t, 0:D], OXT[:, m, rows(t)], wout[:, m, :], start=(m == 0), stop=(m == HP - 1))
                    last.then_inc(sem("attn_out_mm"), 1)
            if stop > 4:
                features(5)
                for t in range(NT):
                    last = rowprod(yslot(t, 3), w2T, t)
                last.then_inc(sem("wg_y_mm"), 1)
                pe.wait_ge(sem("wg_y"), 1)
                for i in range(NT):
                    spmm(CW, lambda j: U[:, j, :], i, PS[0:P, 3 + i, 0:D]).then_inc(sem("wg_mm"), 1)
            if stop > 5:
                features(6)
                experts(1, E2, wg2)
            if stop > 6:
                features(7)
                for t in range(NT):
                    last = rowprod(yslot(t, 3), l3w, t)
                last.then_inc(sem("ng_y_mm"), 1)
                pe.wait_ge(sem("ng_y"), 1)
                for i in range(NT):
                    spmm(CT, lambda j: U[:, j, :], i, PS[0:P, 3 + i, 0:D], stop_=False)
                    pe.matmul(PS[0:P, 3 + i, 0:D], AET[:, rows(i)], l3we[:], start=False, stop=True,
                              skip_group_check=True).then_inc(sem("ng_mm"), 1)
            if stop > 7:
                features(8)
                pe.wait_ge(sem("tree_in"), 16 * 5)
                w1rk = w1r.rearrange("p o (f k) -> p o k f", k=KD)
                for k in range(KD):
                    pe.transpose(PS[:, 3, k * 256:k * 256 + 128], w1rk[:, 0, k, :], ident[:])
                    last = pe.transpose(PS[:, 3, k * 256 + 128:k * 256 + 255], w1rk[0:127, 1, k, :], ident[0:127, 0:127])
                last.then_inc(sem("tree_products"), 1)
                pe.wait_ge(sem("tree_operands"), 1)
                for t in range(NT):
                    last = rowprod(yslot(t, 4)[:, 0:NODES], w1T, t, n=slice(0, NODES))
                last.then_inc(sem("tree_products"), 1)
                pe.wait_ge(sem("tree_operands"), 2)
                for o in range(2):
                    for t in range(NT):
                        last = pe.transpose(PS[0:128 - o, 2 * o + t // 4, rows(t % 4)], CXI[:, t, o * 128:o * 128 + 128 - o], ident[0:P, 0:P])
                last.then_inc(sem("tree_products"), 1)
                pe.wait_ge(sem("tree_leaves"), 1)
                for t in range(NT):
                    pe.matmul(PS[0:P, 4, 0:LEAVES], ones_b[:], LB[:, t, :], start=(t == 0), stop=False, skip_group_check=True)
                    pe.matmul(PS[0:P, 4, 0:LEAVES], ones_b[:], GB[:, t, :], start=False, stop=(t == NT - 1), skip_group_check=True)
                for t in range(NT):
                    place = PS[0:P, 5 + t // 4, (t % 4) * LEAVES:(t % 4) * LEAVES + LEAVES]
                    for u in range(NT):
                        pe.matmul(place, ones_b[:], GB[:, u, :], start=(u == 0), stop=False, skip_group_check=True)
                    for u in range(t):
                        pe.matmul(place, ones_b[:], LB[:, u, :], start=False, stop=False, skip_group_check=True)
                    last = pe.matmul(place, upper_b[:], LB[:, t, :], start=False, stop=True, skip_group_check=True)
                last.then_inc(sem("tree_places"), 1)
                pe.wait_ge(sem("tree_operands"), 3)
                for t in range(NT):
                    for o in range(2):
                        last = pe.matmul(yslot(t, 0), COT[0:128 - o, o, rows(t)], b2s[0:128 - o, o, :], start=(o == 0), stop=(o == 1))
                last.then_inc(sem("tree_products"), 1)
                pe.wait_ge(sem("tree_features_in"), 16)
                pe.wait_ge(sem("tree_operands"), 4)
                for k in range(KD):
                    for t in range(NT - 1):
                        pe.transpose(PS[:, 5 + k, rows(t)], XNk[:, t, k, :], ident[0:P, 0:P])
                for k in range(KD):
                    last = pe.transpose(PS[:, 7, rows(k)], XNk[:, NT - 1, k, :], ident[0:P, 0:P])
                last.then_inc(sem("tree_products"), 1)
                pe.wait_ge(sem("tree_operands"), 5)
                pe.wait_ge(sem("tree_lists"), 1)
                for t in range(NT):
                    last = pe.matmul(PS[:, t, 0:STEPS], ident[0:NT, t:t + 1].to_broadcast([NT, 128]), tn[:, 2, :], start=True, stop=True)
                last.then_inc(sem("tree_products"), 1)
                pe.wait_ge(sem("tree_rows_in"), 16)
                pe.wait_ge(sem("tree_sorted_out"), 1)
                for t in range(NT):
                    for o in range(2):
                        j = 2 * t + o
                        last = pe.transpose(PS[:, 5 + j // 4, rows(j % 4)], CXS[:, t, o * 128:o * 128 + 128], ident[0:P, 0:P])
                last.then_inc(sem("tree_products"), 1)
                pe.wait_ge(sem("tree_sorted_out"), 2)
                for t in range(NT):
                    pe.wait_ge(sem("tree_operands"), 6 + t)
                    for o in range(2):
                        last = pe.matmul(PS[0:P, t, 0:STEPS], COS[:, t, o, :], SO[:, t, o, :], start=(o == 0), stop=(o == 1))
                    last.then_inc(sem("tree_products"), 1)
                pe.wait_ge(sem("tree_sorted_out"), 2 + NT)
                for u in range(TU):
                    pe.sem_inc(sem(f"tree_added{u}"), 1)
                    pe.sem_inc(sem(f"tree_w_free{u}"), 1)
                done = 0
                for t in range(NT):
                    n = pe.value_load(tcnt[t:t + 1, 0:1], min_val=1, max_val=STEPS // TU)
                    with pe.Fori(0, n) as i:
                        for u in range(TU):
                            pe.wait_ge(sem(f"tree_w_in{u}"), (i + done) * 16 + 16)
                            pe.wait_ge(sem(f"tree_added{u}"), i + done + 1)
                            rowprod(PS[0:P, u, 0:D], TW[:, u], t).then_inc(sem(f"tree_w_free{u}"), 1)
                    done = n + done

        @block.vector
        def _(_v):
            edges = EdgePasses()

            def layer_norm(li, src, dst, produce=None, signal=True):
                def normalise(t):
                    v.wait_ge(sem("std_ready"), NT * li + t + 1)
                    v.reciprocal(rstd[:, t:t + 1], std5[:, t:t + 1])
                    v.drain()
                    i = v.tensor_scalar(dst[:, t, :], src[:, t, :], mv[:, t, 0:1], rstd[:, t:t + 1], ALU.subtract, ALU.mult)
                    if signal:
                        i.then_inc(sem("xn_ready"), 1)

                for t in range(NT):
                    if produce:
                        produce(t)
                        v.drain()
                    v.bn_stats(out=bst[:, t, :], in_=src[:, t, :])
                    v.drain()
                    v.bn_aggr(out=mv[:, t, :], in_=bst[:, t, :]).then_inc(sem("var_ready"), 1)
                    if t:
                        normalise(t - 1)
                normalise(NT - 1)

            def features(fi):
                v.wait_ge(sem("xt_mm"), 2 * fi + 1)
                v.tensor_copy(XT[:, 1, 0:500], PS[:, 1, 0:500]).then_inc(sem("xt_ready"), 1)

            def over_edges(t, one_hots):
                lo, hi, count = edges.ranges[t]
                count = edges.done + count
                with v.Fori(lo, hi, G) as c:
                    for b in range(G):
                        v.wait_ge(sem("oh_free"), c + count + (b + 1))
                        one_hots(b, bass.ds(c + b, 1), io16[:, t * P:t * P + P]).then_inc(sem("oh_ready"), 1)

            def edge_rows():
                v.wait_ge(sem("edges_in"), 64)
                for i in range(2):
                    v.tensor_copy(ef[:, i, :], ei[:, i, :])
                v.tensor_copy(ef[:, 2, :], ei[:, 2, :])
                v.drain()
                v.scalar_tensor_tensor(out=ef[:, 2, :], in0=ef[:, 2, :], scalar=float(N), in1=ef[:, 0, :], op0=ALU.mult, op1=ALU.add)
                v.tensor_reduce(red[:, 0:1], ef[:, 1, :], AX.X, ALU.min)
                v.tensor_reduce(red[:, 1:2], ef[:, 1, :], AX.X, ALU.max)
                v.drain().then_inc(sem("edge_rows"), 1)

            def edge_fields():
                v.wait_ge(sem("consts"), 1)
                v.tensor_copy(io16[:], iot)
                v.tensor_copy(ioe[:], iot[:, 0:E2])
                v.tensor_copy(ioleaf[:], iot[:, 0:STEPS])
                v.tensor_copy(pcol[:, 0:1], pcoli[0:P])
                v.tensor_copy(nodecol[:, 0:1], pcoli[:])
                v.drain()
                v.tensor_scalar(nodecol[:, 1:2], nodecol[:, 0:1], 128.0, None, ALU.add)
                v.tensor_scalar(pcol[:, 1:2], pcol[:, 0:1], float(P), None, ALU.mult)
                THi = TH.bitcast(I32)
                v.tensor_copy(TH, THi)
                v.wait_ge(sem("edge_cols"), 1)
                v.tensor_copy(EF[:, :, 0:CH], PS[0:P, 3, 0:4 * CH].rearrange("p (i c) -> p i c", i=4))
                v.tensor_copy(mm_, PS[0:1, 4, 0:2 * CH].rearrange("p (i c) -> p i c", i=2))
                v.drain()
                v.tensor_copy(GI[:], EF[:, 2, 0:CH])
                v.drain().then_inc(sem("edge_fields"), 1)
                w = EF[:, 3, 0:CH]
                v.tensor_copy(wtb, w)
                v.drain()
                v.tensor_copy(WP3[:, 0, 0:CH], wtb)
                v.drain()
                v.tensor_tensor(wtmp[:, 0, :], w, WP3[:, 0, 0:CH], ALU.subtract)
                v.drain()
                v.tensor_copy(wtb, wtmp[:, 0, :])
                v.drain()
                v.tensor_copy(WP3[:, 1, 0:CH], wtb)
                v.drain()
                v.tensor_tensor(WP3[:, 2, 0:CH], wtmp[:, 0, :], WP3[:, 1, 0:CH], ALU.subtract)
                def over_tiles(x):
                    return x.unsqueeze(1).to_broadcast([1, NT, CH])
                v.tensor_tensor(tou[:, 0], over_tiles(mm_[:, 0, :]), TH[:, 1], ALU.is_lt)
                v.tensor_tensor(tou[:, 1], over_tiles(mm_[:, 1, :]), TH[:, 0], ALU.is_ge)
                v.drain()
                v.tensor_tensor(tou[:, 0], tou[:, 0], tou[:, 1], ALU.mult)
                v.drain()
                v.tensor_scalar(tou[:, 1], tou[:, 0], -1000.0, 1000.0, ALU.mult, ALU.add)
                v.drain()
                v.tensor_tensor(tou[:, 1], tou[:, 1], TH[:, 2], ALU.add)
                v.scalar_tensor_tensor(out=tou[:, 2], in0=TH[:, 2], scalar=1.0, in1=tou[:, 0], op0=ALU.add, op1=ALU.mult)
                v.drain()
                v.tensor_reduce(lh[:, 0, :], tou[:, 1], AX.X, ALU.min)
                v.tensor_reduce(lh[:, 1, :], tou[:, 2], AX.X, ALU.max)
                v.drain()
                v.tensor_scalar(lh[:, 0, :], lh[:, 0, :], float(CH - G), None, ALU.min)
                v.drain()
                v.tensor_tensor(lh[:, 3, :], lh[:, 1, :], lh[:, 0, :], ALU.subtract)
                v.drain()
                v.tensor_scalar(lh[:, 3, :], lh[:, 3, :], 1.0, None, ALU.max)
                v.tensor_scalar(nmul[:, 0, :], ioleaf[0:1, 0:BODIES], float(G), None, ALU.mult)
                v.drain()
                for t in range(1, NT):
                    v.tensor_copy(nmul[:, t, :], nmul[:, 0, :])
                v.drain()
                v.tensor_tensor(nmul, nmul, lh[:, 3, :].unsqueeze(2).to_broadcast([1, NT, BODIES]), ALU.is_lt)
                v.drain()
                v.tensor_reduce(lh[:, 5, :], nmul, AX.X, ALU.add)
                v.drain()
                v.tensor_scalar(lh[:, 4, :], lh[:, 5, :], float(-G), float(CHP), ALU.mult, ALU.add)
                v.drain()
                v.tensor_tensor(lh[:, 0, :], lh[:, 0, :], lh[:, 4, :], ALU.min)
                v.drain()
                v.tensor_scalar(lh[:, 5, :], lh[:, 5, :], float(G), None, ALU.mult)
                v.memset(lh[:, 2, :], float(CHP))
                v.drain()
                for t in range(NT - 1):
                    v.tensor_tensor(lh[:, 2, t + 1:t + 2], lh[:, 2, t:t + 1], lh[:, 5, t:t + 1], ALU.add)
                    v.drain()
                v.scalar_tensor_tensor(out=lh[:, 1, :], in0=lh[:, 5, :], scalar=float(1 - G), in1=lh[:, 0, :], op0=ALU.add, op1=ALU.add)
                v.tensor_tensor(lh[:, 2, :], lh[:, 2, :], lh[:, 0, :], ALU.subtract)
                v.tensor_reduce(lh[:, 3, 0:1], lh[:, 5, :], AX.X, ALU.add)
                v.drain()
                v.tensor_copy(rng[:], lh[:, 0:4, :])
                v.drain().then_inc(sem("ranges"), 1)
                edges.all = pass_length(v)
                for t in range(NT):
                    edges.ranges[t] = tile_range(v, t)
                v.wait_ge(sem("prep_mm"), 1)
                v.tensor_copy(b1T[:], PS[:, 6, 0:96])
                v.tensor_copy(bxT[:], PS[:, 6, 96:100])
                v.tensor_copy(w2T[:], PS[:, 7, :].rearrange("p (k o) -> p k o", k=KD))
                v.drain().then_inc(sem("prep_out"), 1)

            def transposed_counts():
                v.wait_ge(sem("ct_mm"), 1)
                v.tensor_copy(AET[:, 0:500], PS[0:FE, 4, 0:500])
                v.tensor_copy(AET[:, 500:N], PS[0:FE, 5, 0:P]).then_inc(sem("ct_copied"), 1)
                for i in range(NT):
                    v.wait_ge(sem("ct_mm"), i + 2)
                    bank = 6 if i % 2 == 0 else 0
                    v.tensor_copy(CT[:, i, 0:500], PS[0:P, bank, 0:500])
                    v.tensor_copy(CT[:, i, 500:N], PS[0:P, bank + 1, 0:P]).then_inc(sem("ct_copied"), 1)
                v.drain()

            def in_degrees():
                v.tensor_reduce(sc5[:, 0, :], C, AX.X, ALU.add)
                for t in range(NT):
                    v.tensor_tensor(DG[:, t, :], C[:, t, t * P:t * P + P], ident[0:P, 0:P], ALU.mult)
                v.drain()
                v.tensor_reduce(dg5[:], DG, AX.X, ALU.add)
                v.drain()

            def degrees():
                v.tensor_reduce(dis[:], CT, AX.X, ALU.add)
                v.drain()
                v.tensor_scalar(sc5[:, 1, :], dis[:], 1.0, None, ALU.add)
                v.tensor_scalar(sc5[:, 2, :], dis[:], 1.0, None, ALU.max)
                v.tensor_scalar(sc5[:, 3, :], sc5[:, 0, :], 1.0, None, ALU.max)
                v.drain().then_inc(sem("degrees"), 1)
                v.wait_ge(sem("degree_roots"), 1)
                v.reciprocal(dis[:], sc5[:, 1, :])
                v.reciprocal(nout[:], sc5[:, 2, :])
                v.reciprocal(nin[:], sc5[:, 3, :])
                v.drain()
                v.tensor_tensor(q5[:], dis[:], dis[:], ALU.mult)
                v.drain()
                v.scalar_tensor_tensor(out=q5[:], in0=dg5[:], scalar=1.0, in1=q5[:], op0=ALU.add, op1=ALU.subtract)
                v.drain()

            def relational(layer):
                if layer == 0:
                    v.sem_inc(sem("oh_ready"), CHP)
                v.wait_ge(sem("layer_weights_in"), 64)

                def one_hots(b, col, own):
                    v.tensor_scalar(OHS[:, b, 0:N], io16[:], EF[:, 0, col], None, ALU.is_equal)
                    if layer == 0:
                        v.tensor_scalar(OHB[:, b, 0, 0:P], own, EF[:, 1, col], None, ALU.is_equal)
                    else:
                        for i in range(3):
                            v.tensor_scalar(OHB[:, b, i, 0:P], own, EF[:, 1, col], WP3[:, i, col], ALU.is_equal, ALU.mult)
                    return v.tensor_scalar(OHF[:, b, :], own, EF[:, 1, col], None, ALU.is_equal)

                def finish(t):
                    v.wait_ge(sem("edge_tile_mm"), layer * NT + t + 1)
                    b0 = edge_bank(layer, t)
                    acc = PS[0:P, b0 + 2, 0:D]
                    v.tensor_tensor(XN[:, t, :], acc, bias[:, layer, :], ALU.add)
                    for bank, c0, c1 in bank_pair(b0):
                        last = v.tensor_copy((CW if layer else C)[:, t, c0:c1], PS[0:P, bank, 0:c1 - c0])
                    if layer == 0:
                        last = v.tensor_copy(AE[:, t, :], PS[0:P, b0 + 3, 0:FE])
                    last.then_inc(sem("edge_tile_done"), 1)
                    v.drain()
                    if layer == 0:
                        v.tensor_scalar(XN[:, t, :], XN[:, t, :], 0.0, None, ALU.max).then_inc(sem("xn_ready"), 1)
                    else:
                        v.tensor_tensor(X[:, t, :], X[:, t, :], XN[:, t, :], ALU.add)

                def produce(t):
                    if t == 0:
                        over_edges(0, one_hots)
                    if t + 1 < NT:
                        over_edges(t + 1, one_hots)
                    finish(t)

                if layer == 0:
                    for t in range(NT):
                        produce(t)
                else:
                    layer_norm(1, X, XN, produce)
                edges.done = edges.all + edges.done

            def experts(second, ne, bg, soft, base, total):
                v.wait_ge(sem("route_mm"), 2 * second + 1)
                v.tensor_tensor(gate[:, :, 0:ne], PS[0:P, 7, 0:NT * ne].rearrange("p (t e) -> p t e", e=ne),
                                bg[:].unsqueeze(1).to_broadcast([P, NT, ne]), ALU.add)
                v.drain()
                for t in range(NT):
                    v.max(gmax[:, t, :], gate[:, t, 0:ne])
                v.drain()
                for t in range(NT):
                    v.max_index(gidx[:, t, :], gmax[:, t, :], gate[:, t, 0:ne])
                v.drain()
                v.tensor_copy(gidf[:], gidx[:, :, 0:2])
                if soft:
                    v.tensor_tensor(gwt[:, :, 0], gmax[:, :, 1], gmax[:, :, 0], ALU.subtract).then_inc(sem("top2_diff"), 1)
                    v.wait_ge(sem("top2_exp"), 1)
                    v.tensor_scalar(gwt[:, :, 2], gwt[:, :, 1], 1.0, None, ALU.add)
                    v.drain()
                    v.reciprocal(gwt[:, :, 2], gwt[:, :, 2])
                    v.drain()
                    v.tensor_tensor(gwt[:, :, 3], gwt[:, :, 1], gwt[:, :, 2], ALU.mult)
                else:
                    v.memset(gwt[:], 1.0)
                v.drain()
                for k in range(2):
                    for t in range(NT):
                        v.tensor_scalar(one_hot[:, k, t, 0:ne], ioleaf[:, 0:ne], gidf[:, t, k:k + 1], None, ALU.is_equal)
                v.drain()
                v.tensor_tensor(chosen[:, :, 0:ne], one_hot[:, 0, :, 0:ne], one_hot[:, 1, :, 0:ne], ALU.add).then_inc(sem("chosen"), 1)
                v.wait_ge(sem("route_mm"), 2 * second + 2)
                v.tensor_scalar(blocksi[:, 0:ne], PS[0:P, 5, 0:ne], float(BS - 1), None, ALU.add)
                v.drain()
                v.tensor_scalar(blocksi[:, 0:ne], blocksi[:, 0:ne], 7, None, ALU.arith_shift_right)
                v.drain()
                v.tensor_scalar(blocks[:, 0, 0:ne], blocksi[:, 0:ne], 1.0, None, ALU.max)
                v.drain()
                src, n = 0, 1
                if second:
                    v.tensor_copy(bexi[:, MAXB + 1:MAXB + 2], bexi[:, MAXB:MAXB + 1])
                while n < ne:
                    dst = 1 + src % 2
                    v.tensor_copy(blocks[:, dst, 0:n], blocks[:, src, 0:n])
                    v.tensor_tensor(blocks[:, dst, n:ne], blocks[:, src, n:ne], blocks[:, src, 0:ne - n], ALU.add)
                    v.drain()
                    src, n = dst, 2 * n
                ends = blocks[:, src, 0:ne]
                v.tensor_tensor(blocks[:, 3, 0:ne], ends, blocks[:, 0, 0:ne], ALU.subtract)
                v.tensor_tensor(bexp[:, :, 0:ne], ioleaf[0:1, 0:MAXB].unsqueeze(2).to_broadcast([1, MAXB, ne]),
                                blocks[0:1, src, 0:ne].unsqueeze(1).to_broadcast([1, MAXB, ne]), ALU.is_ge)
                v.tensor_scalar(bodies, ioleaf[0:1, 0:MAXB // UB], float(UB), blocks[0:1, src, ne - 1:ne], ALU.mult, ALU.is_lt)
                v.drain()
                v.tensor_reduce(bex[:, 0:MAXB], bexp[:, :, 0:ne], AX.X, ALU.add)
                v.tensor_reduce(bex[:, MAXB:MAXB + 1], bodies, AX.X, ALU.add)
                v.tensor_scalar(blocks[:, 3, 0:ne], blocks[:, 3, 0:ne], float(BS), None, ALU.mult)
                v.drain()
                v.tensor_scalar(bex[:, 0:MAXB], bex[:, 0:MAXB], float(ne - 1), None, ALU.min)
                v.tensor_tensor(place[:, 0, :, 0:ne], PS[0:P, 6, 0:NT * ne].rearrange("p (t e) -> p t e", e=ne),
                                blocks[:, 3, 0:ne].unsqueeze(1).to_broadcast([P, NT, ne]), ALU.add)
                v.drain()
                v.tensor_copy(bexi[:, 0:MAXB], bex[:, 0:MAXB])
                v.tensor_copy(bexi[:, MAXB:MAXB + 1], bex[:, MAXB:MAXB + 1])
                v.tensor_tensor(place[:, 1, :, 0:ne], place[:, 0, :, 0:ne], one_hot[:, 1, :, 0:ne], ALU.mult)
                v.drain()
                v.tensor_tensor(place[:, 0, :, 0:ne], place[:, 0, :, 0:ne], one_hot[:, 0, :, 0:ne], ALU.mult)
                v.drain()
                for k in range(2):
                    v.tensor_reduce(slotf[:, k, :], place[:, k, :, 0:ne], AX.X, ALU.add)
                v.drain()
                v.tensor_copy(slot[:], slotf[:])
                v.drain().then_inc(sem("routed"), 1)
                for t in range(NT):
                    v.tensor_scalar(GW[:, t, 0:ne], one_hot[:, 0, t, 0:ne], gwt[:, t, 2:3], None, ALU.mult)
                v.drain()
                for t in range(NT):
                    v.scalar_tensor_tensor(out=GW[:, t, 0:ne], in0=one_hot[:, 1, t, 0:ne], scalar=gwt[:, t, 3:4], in1=GW[:, t, 0:ne], op0=ALU.mult, op1=ALU.add)
                v.drain().then_inc(sem("bias_operands"), 1)
                v.wait_ge(sem("bias_mm"), 2 * second + 1)
                v.tensor_copy(GWT[0:ne, 0:500], PS[0:ne, 5, 0:500])
                v.tensor_copy(GWT[0:ne, 500:N], PS[0:ne, 6, 0:P])
                v.drain().then_inc(sem("bias_operands"), 1)
                v.wait_ge(sem("bias_mm"), 2 * second + 2)
                for t in range(NT):
                    v.tensor_tensor(total[:, t, :], yslot(t, 5), base[:, t, :], ALU.add)
                v.drain().then_inc(sem("bias_added"), 1)
                if not second:
                    degrees()
                n, before = mixture_bodies(v, second)
                if not second:
                    for b in range(UB):
                        v.sem_inc(sem(f"y_stored{b}"), 16)

                def tokens(i, b):
                    v.wait_ge(sem(f"xb_free{b}"), i + before + 2)
                    v.tensor_copy(XBT[:, b], PS[:, b % 2, 0:2 * BS].rearrange("p (k n) -> p k n", k=KD)).then_inc(sem("xbt"), 1)

                def outputs(i, b):
                    v.wait_ge(sem(f"w2_free{b}"), i + before + 2)
                    v.wait_ge(sem(f"y_stored{b}"), (i + before) * 16 + 16)
                    v.tensor_copy(YB[:, b, :], PS[:, 5 + b, 0:D]).then_inc(sem(f"y_out{b}"), 1)

                with v.Fori(0, n) as i:
                    tokens(i, 0)
                    tokens(i, 1)
                    tokens(i, 2)
                    outputs(i, 0)
                    outputs(i, 1)
                    outputs(i, 2)
            def collect(t, second, acc):
                v.wait_ge(sem(f"collected{t}"), 32 * (second + 1))
                for k in range(2):
                    v.scalar_tensor_tensor(out=acc[:, t, :], in0=YG[:, k, t, :], scalar=gwt[:, t, 2 + k:3 + k],
                                           in1=acc[:, t, :], op0=ALU.mult, op1=ALU.add)
                    v.drain()

            def bank_tiles(base, n=D):
                for g, (t0, t1) in enumerate(((0, 2), (2, 4), (4, 5))):
                    yield t0, t1, PS[0:P, base + g, 0:(t1 - t0) * D].rearrange("p (t d) -> p t d", d=D)[:, :, 0:n]

            if stop > 0:
                edge_rows()
                v.wait_ge(sem("x_in"), 16)
                layer_norm(0, X, XN)
                features(0)
                edge_fields()
                relational(0)
                features(1)
                in_degrees()
                transposed_counts()
                relational(1)
            v.wait_ge(sem("weights_in"), WEIGHTS_IN)
            if stop > 1:
                features(2)
                experts(0, E0, bg0, False, X, X)
                layer_norm(2, X, XN, lambda t: collect(t, 0, X))
            if stop > 2:
                features(3)
                b3, b2, b1 = Y[:, 3], Y[:, 2], Y[:, 1]

                def filtered(n, w, base):
                    v.wait_ge(sem("cheb_mm"), n)
                    for t0, t1, src in bank_tiles(base):
                        last = v.tensor_copy(Y[:, w, t0:t1, :], src)
                    last.then_inc(sem("cheb_y"), 1)

                filtered(1, 3, 3)
                v.drain()
                for t in range(NT):
                    v.tensor_scalar(U[:, t, :], b3[:, t, :], dis[:, t:t + 1], None, ALU.mult).then_inc(sem("cheb_u"), 1)
                v.tensor_scalar(sc5[:, 0, :], q5[:], 2.0, None, ALU.mult)
                v.tensor_scalar(sc5[:, 1, :], dis[:], -2.0, None, ALU.mult)
                v.tensor_scalar(sc5[:, 2, :], dis[:], -1.0, None, ALU.mult)
                filtered(2, 2, 0)
                v.drain()
                for t in range(NT):
                    v.scalar_tensor_tensor(out=b2[:, t, :], in0=b3[:, t, :], scalar=sc5[:, 0, t:t + 1], in1=b2[:, t, :], op0=ALU.mult, op1=ALU.add)
                v.tensor_tensor(X[:], X[:], bias[:, 2, :].unsqueeze(1).to_broadcast([P, NT, D]), ALU.add)
                v.drain()
                for t in range(NT):
                    v.wait_ge(sem("cheb_spmm"), t + 1)
                    v.scalar_tensor_tensor(out=b2[:, t, :], in0=PS[0:P, 3 + t, 0:D], scalar=sc5[:, 1, t:t + 1], in1=b2[:, t, :], op0=ALU.mult, op1=ALU.add)
                    v.drain()
                    v.tensor_scalar(S1[:, t, :], b2[:, t, :], dis[:, t:t + 1], None, ALU.mult).then_inc(sem("cheb_u"), 1)
                filtered(3, 1, 0)
                v.drain()
                v.tensor_tensor(b1, b1, b3, ALU.subtract)
                v.tensor_tensor(X[:], X[:], b2, ALU.subtract)
                v.drain()
                for t in range(NT):
                    v.scalar_tensor_tensor(out=b1[:, t, :], in0=b2[:, t, :], scalar=sc5[:, 0, t:t + 1], in1=b1[:, t, :], op0=ALU.mult, op1=ALU.add)
                v.drain()
                for t in range(NT):
                    v.wait_ge(sem("cheb_spmm"), NT + t + 1)
                    v.scalar_tensor_tensor(out=b1[:, t, :], in0=PS[0:P, 3 + t, 0:D], scalar=sc5[:, 1, t:t + 1], in1=b1[:, t, :], op0=ALU.mult, op1=ALU.add)
                    v.drain()
                    v.tensor_scalar(U[:, t, :], b1[:, t, :], dis[:, t:t + 1], None, ALU.mult).then_inc(sem("cheb_u"), 1)
                filtered(4, 0, 0)
                for t in range(NT):
                    v.scalar_tensor_tensor(out=X[:, t, :], in0=b1[:, t, :], scalar=q5[:, t:t + 1], in1=X[:, t, :], op0=ALU.mult, op1=ALU.add)
                v.drain()
                v.tensor_tensor(X[:], X[:], Y[:, 0], ALU.add)
                v.drain()

                def cheb_out(t):
                    v.wait_ge(sem("cheb_spmm"), NT * 2 + t + 1)
                    v.scalar_tensor_tensor(out=X[:, t, :], in0=PS[0:P, 3 + t, 0:D], scalar=sc5[:, 2, t:t + 1], in1=X[:, t, :], op0=ALU.mult, op1=ALU.add)

                layer_norm(3, X, XN, cheb_out)
            if stop > 3:
                features(4)
                v.tensor_scalar(rtemp[:], temp[:], 0.1, 5.0, ALU.max, ALU.min)
                v.drain()
                v.reciprocal(rtemp[:], rtemp[:])
                v.memset(blk, 0.0)
                v.drain()
                for h in range(2):
                    v.memset(blk[h * HD:h * HD + HD, h * HD:h * HD + HD], 1.0)
                v.memset(ABD, 0.0)
                for t in range(NT):
                    v.wait_ge(sem("logit_mm"), t + 1)
                    sw = SW[:, t, :].rearrange("p (h g) -> p h g", h=8)
                    v.tensor_tensor(sw, PS[0:P, 6 + t % 2, :].rearrange("p (h g) -> p h g", h=8),
                                    bsl[:].unsqueeze(1).to_broadcast([P, 8, HD]), ALU.add)
                    v.drain()
                    v.tensor_tensor(sw, sw, rtemp[:].unsqueeze(2).to_broadcast([P, 8, HD]), ALU.mult)
                    v.drain()
                    v.tensor_reduce(hm[:, t, :], sw, AX.X, ALU.max)
                    v.drain()
                    v.tensor_tensor(sw, sw, hm[:, t, :].unsqueeze(2).to_broadcast([P, 8, HD]), ALU.subtract).then_inc(sem("slice_shifted"), 1)
                    v.wait_ge(sem("fx_mm"), t + 1)
                    v.tensor_tensor(FX[:, t, :], PS[0:P, 4 + t % 2, :], bfx[:], ALU.add).then_inc(sem("fx"), 1)
                for t in range(NT):
                    sw = SW[:, t, :].rearrange("p (h g) -> p h g", h=8)
                    v.wait_ge(sem("slice_exp"), t + 1)
                    v.tensor_reduce(hs[:, t, :], sw, AX.X, ALU.add)
                    v.drain()
                    v.reciprocal(hr[:, t, :], hs[:, t, :])
                    v.drain()
                    v.tensor_tensor(sw, sw, hr[:, t, :].unsqueeze(2).to_broadcast([P, 8, HD]), ALU.mult).then_inc(sem("slice_w"), 1)
                v.wait_ge(sem("attn_products"), 1)
                v.tensor_scalar(rn, PS[:, 1, :], 1e-5, None, ALU.add)
                v.drain()
                v.reciprocal(rn, rn)
                v.drain()
                blk4 = blk.unsqueeze(1).to_broadcast([128, HP, 128])
                rn4 = rn.rearrange("p (m g) -> p m g", m=HP)
                v.tensor_tensor(rn4, rn4, blk4, ALU.mult)
                v.drain()
                v.tensor_tensor(STT, PS[:, 0, :].rearrange("p (m g) -> p m g", m=HP), rn4, ALU.mult).then_inc(sem("attn_operands"), 1)
                v.wait_ge(sem("attn_products"), 2)
                for dst, bank in ((QT, 2), (KT, 3), (VV, 4)):
                    last = v.tensor_copy(dst, PS[:, bank, :].rearrange("p (m g) -> p m g", m=HP))
                last.then_inc(sem("attn_operands"), 1)
                v.wait_ge(sem("attn_products"), 3)
                for h in range(2):
                    hr_ = slice(h * HD, h * HD + HD)
                    v.tensor_copy(AT[hr_], PS[hr_, 0, :].rearrange("p (m g) -> p m g", m=HP)[:, :, hr_])
                v.drain()
                v.tensor_reduce(am[:, 0, :], AT, AX.X, ALU.max)
                v.drain()
                v.tensor_tensor(AT, AT, am[:, 0, :].unsqueeze(2).to_broadcast([128, HP, HD]), ALU.subtract).then_inc(sem("attn_shifted"), 1)
                v.wait_ge(sem("attn_exp"), 1)
                v.tensor_reduce(am[:, 1, :], AT, AX.X, ALU.add)
                v.drain()
                v.reciprocal(am[:, 2, :], am[:, 1, :])
                v.drain()
                for h in range(2):
                    hr_ = slice(h * HD, h * HD + HD)
                    last = v.tensor_tensor(ABD[hr_, :, hr_], AT[hr_], am[hr_, 2, :].unsqueeze(2).to_broadcast([HD, HP, HD]), ALU.mult)
                last.then_inc(sem("attn_operands"), 1)
                v.wait_ge(sem("attn_products"), 4)
                v.tensor_copy(ATT, PS[:, 1, :].rearrange("p (m g) -> p m g", m=HP)).then_inc(sem("attn_operands"), 1)
                v.wait_ge(sem("attn_products"), 5)
                v.tensor_copy(OS, PS[:, 2, :].rearrange("p (m g) -> p m g", m=HP)).then_inc(sem("attn_operands"), 1)
                v.tensor_tensor(X[:], X[:], bias[:, 3, :].unsqueeze(1).to_broadcast([P, NT, D]), ALU.add)
                v.drain()

                def attn_out(t):
                    v.wait_ge(sem("attn_out_mm"), t + 1)
                    v.tensor_tensor(X[:, t, :], PS[0:P, 3 + t, 0:D], X[:, t, :], ALU.add)

                layer_norm(4, X, XN, attn_out)
            if stop > 4:
                features(5)
                v.wait_ge(sem("wg_y_mm"), 1)
                for t0, t1, src in bank_tiles(3):
                    last = v.tensor_copy(U[:, t0:t1, :], src)
                last.then_inc(sem("wg_y"), 1)
                v.tensor_tensor(X[:], X[:], bias[:, 4, :].unsqueeze(1).to_broadcast([P, NT, D]), ALU.add)
                v.drain()

                def wg_out(t):
                    v.wait_ge(sem("wg_mm"), t + 1)
                    v.tensor_tensor(X[:, t, :], PS[0:P, 3 + t, 0:D], X[:, t, :], ALU.add)

                layer_norm(5, X, XN, wg_out)
            if stop > 5:
                features(6)
                experts(1, E2, bg2, True, XN, MO)
                v.tensor_tensor(X[:], X[:], bias[:, 6, :].unsqueeze(1).to_broadcast([P, NT, D]), ALU.add)
                layer_norm(6, MO, XN, lambda t: collect(t, 1, MO), signal=False)
                v.drain()

                def moe_out(t):
                    v.tensor_tensor(XN[:, t, :], XN[:, t, :], bias[:, 5, :], ALU.mult)
                    v.drain()
                    v.tensor_tensor(X[:, t, :], X[:, t, :], XN[:, t, :], ALU.add)

                layer_norm(7, X, XN, moe_out)
            if stop > 6:
                features(7)
                v.wait_ge(sem("ng_y_mm"), 1)
                for t in range(NT):
                    last = v.tensor_scalar(U[:, t, :], yslot(t, 3), nout[:, t:t + 1], None, ALU.mult)
                last.then_inc(sem("ng_y"), 1)

                def ng_out(t):
                    v.wait_ge(sem("ng_mm"), t + 1)
                    v.scalar_tensor_tensor(out=S1[:, t, :], in0=PS[0:P, 3 + t, 0:D], scalar=nin[:, t:t + 1], in1=bias[:, 7, :], op0=ALU.mult, op1=ALU.add)
                    v.drain()
                    v.scalar_tensor_tensor(out=X[:, t, :], in0=S1[:, t, :], scalar=0.0, in1=X[:, t, :], op0=ALU.max, op1=ALU.add)
                    if t == NT - 1:
                        v.drain().then_inc(sem("arena_free_for_tree"), 1)

                layer_norm(8, X, XN, ng_out)
            if stop > 7:
                features(8)
                v.wait_ge(sem("tree_products"), 1)
                v.tensor_copy(w1T[:, :, 0:NODES], PS[:, 3, :].rearrange("p (k j) -> p k j", k=KD)[:, :, 0:NODES]).then_inc(sem("tree_operands"), 1)
                v.wait_ge(sem("tree_products"), 2)
                for t0, t1, src in bank_tiles(4, NODES):
                    v.tensor_tensor(SCO[:, t0:t1, 0:NODES], src, b1s[:, 0:NODES].unsqueeze(1).to_broadcast([P, t1 - t0, NODES]), ALU.add)
                v.drain().then_inc(sem("tree_scores"), 1)
                v.memset(TM[:, :, 0:1], 1.0)
                for d in range(DEPTH - 1):
                    n0, n1 = 2 ** d - 1, 2 ** (d + 1) - 1
                    kids = TM[:, :, n1:2 * n1 + 1].rearrange("p t (j c) -> p t j c", c=2)
                    v.drain()
                    v.scalar_tensor_tensor(out=kids[:, :, :, 1], in0=SCO[:, :, n0:n1], scalar=0.0, in1=TM[:, :, n0:n1], op0=ALU.is_gt, op1=ALU.mult)
                    v.scalar_tensor_tensor(out=kids[:, :, :, 0], in0=SCO[:, :, n0:n1], scalar=0.0, in1=TM[:, :, n0:n1], op0=ALU.is_le, op1=ALU.mult)
                v.drain()
                v.wait_ge(sem("tree_gelu"), 1)
                v.tensor_tensor(CXI[:, :, 0:NODES], CXI[:, :, 0:NODES], TM[:, :, 0:NODES], ALU.mult).then_inc(sem("tree_operands"), 1)
                leaf = TM[:, :, LEAVES - 1:NODES]
                v.tensor_copy(LB, leaf)
                v.tensor_tensor(tl, leaf, ioleaf[:, 0:LEAVES].unsqueeze(1).to_broadcast([P, NT, LEAVES]), ALU.mult)
                v.drain()
                v.tensor_reduce(lid[:, 0, :], tl, AX.X, ALU.add)
                v.drain()
                for t in range(NT):
                    v.tensor_scalar(GB[:, t, :], ioleaf[:, 0:LEAVES], lid[:, 0, t:t + 1], None, ALU.is_gt)
                v.drain().then_inc(sem("tree_leaves"), 1)
                v.wait_ge(sem("tree_products"), 3)
                for o in range(2):
                    v.tensor_copy(COT[0:128 - o, o, 0:500], PS[0:128 - o, 2 * o, 0:500])
                    last = v.tensor_copy(COT[0:128 - o, o, 500:N], PS[0:128 - o, 2 * o + 1, 0:P])
                last.then_inc(sem("tree_operands"), 1)
                v.wait_ge(sem("tree_places"), 1)
                for i in range(2):
                    v.tensor_scalar(tls[:, i, :], PS[0:NT, 4, 0:LEAVES], pcol[0:NT, 1:2], float(i * (P - 1)), ALU.subtract, ALU.is_le)
                for t in range(NT):
                    v.tensor_tensor(tl[:, t, :], PS[0:P, 5 + t // 4, (t % 4) * LEAVES:(t % 4) * LEAVES + LEAVES], leaf[:, t, :], ALU.mult)
                v.drain()
                v.tensor_reduce(lid[:, 1, :], tl, AX.X, ALU.add)
                v.drain()
                v.tensor_copy(placei, lid[:, 1, :])
                v.drain().then_inc(sem("tree_operands"), 1)
                for t in range(NT):
                    v.tensor_scalar(CXI[:, t, NODES:D], pcol[:, 0:1], float(t * P), None, ALU.add)
                v.wait_ge(sem("tree_products"), 4)
                for t in range(NT):
                    v.tensor_tensor(CXI[:, t, D:2 * D], yslot(t, 0), X[:, t, :], ALU.add)
                v.drain().then_inc(sem("tree_operands"), 1)
                v.tensor_reduce(tb[:, 0, 0:2], tls, AX.X, ALU.add)
                v.drain()
                for d in range(DEPTH):
                    v.tensor_copy(tbi[:, 0, d, :], tb[:, 0, 0:2])
                v.drain()
                for d in range(DEPTH):
                    v.tensor_scalar(tbi[:, 1, d, :], tbi[:, 0, d, :], DEPTH - 1 - d, None, ALU.arith_shift_right)
                v.drain()
                v.tensor_copy(tb[:, 1, 0:8], tbi[:, 1, :, 0])
                v.tensor_copy(tb[:, 2, 0:8], tbi[:, 1, :, 1])
                v.memset(tb[:, 4, 0:1], 0.0)
                v.drain()
                v.scalar_tensor_tensor(out=tb[:, 3, 0:8], in0=tb[:, 2, 0:8], scalar=1.0, in1=tb[:, 1, 0:8], op0=ALU.add, op1=ALU.subtract)
                for d in range(DEPTH):
                    v.drain()
                    v.tensor_tensor(tb[:, 4, d + 1:d + 2], tb[:, 4, d:d + 1], tb[:, 3, d:d + 1], ALU.add)
                v.drain()
                v.tensor_tensor(tb[:, 5, 0:8], tb[:, 1, 0:8], tb[:, 4, 0:8], ALU.subtract)
                v.drain()
                v.tensor_tensor(tb[:, 5, 0:8], tb[:, 5, 0:8], levelk[:], ALU.add)
                v.drain()
                v.tensor_tensor(tb[:, 6, 1:8], tb[:, 5, 1:8], tb[:, 5, 0:7], ALU.subtract)
                v.tensor_copy(tb[:, 6, 0:1], tb[:, 5, 0:1])
                v.memset(tb[:, 6, 8:9], 1000.0)
                v.drain()
                for d in range(9):
                    v.tensor_scalar(tn[:, d, :], ioleaf[0:NT, :], tb[:, 4, d:d + 1], tb[:, 6, d:d + 1], ALU.is_ge, ALU.mult)
                v.tensor_scalar(tls[:, 0, 0:STEPS // TU], ioleaf[0:NT, 0:STEPS // TU], float(TU), tb[:, 4, 8:9], ALU.mult, ALU.is_lt)
                v.drain()
                v.tensor_reduce(tb[:, 7, 0:1], tls[:, 0, 0:STEPS // TU], AX.X, ALU.add)
                for d in range(1, 9):
                    v.tensor_tensor(tn[:, 0, :], tn[:, 0, :], tn[:, d, :], ALU.add)
                    v.drain()
                v.tensor_tensor(tn[:, 0, :], tn[:, 0, :], ioleaf[0:NT, :], ALU.add)
                v.drain()
                v.tensor_copy(tcnt[:, 0:1], tb[:, 7, 0:1])
                v.tensor_scalar(tn[:, 1, :], tn[:, 0, :], float(NODES - 1), None, ALU.min)
                v.tensor_scalar(tn[:, 2, :], tn[:, 0, :], float(NODES + 1), None, ALU.min)
                v.drain()
                v.tensor_copy(tnode, tn[:, 1, :])
                v.drain().then_inc(sem("tree_lists"), 1)
                v.wait_ge(sem("tree_products"), 6)
                for t in range(NT):
                    for o in range(2):
                        last = v.tensor_scalar(SO[:, t, o, :], PS[:, t, 0:STEPS], nodecol[:, o:o + 1], None, ALU.is_equal)
                    last.then_inc(sem("tree_operands"), 1)
                v.wait_ge(sem("tree_rows_in"), 16)
                v.tensor_copy(sid, CXS[:, :, NODES])
                v.drain()
                v.wait_ge(sem("tree_sorted_out"), 2 + NT)
                done = 0
                for t in range(NT):
                    n = v.value_load(tcnt[t:t + 1, 0:1], min_val=1, max_val=STEPS // TU)
                    own = CXS[:, t, D:2 * D]
                    with v.Fori(0, n) as i:
                        for u in range(TU):
                            v.drain()
                            v.wait_ge(sem(f"tree_w_free{u}"), i + done + 2)
                            v.scalar_tensor_tensor(out=own, in0=PS[0:P, u, 0:D], scalar=CL[:, t, bass.ds(i * TU + u, 1)],
                                                   in1=own, op0=ALU.mult, op1=ALU.add).then_inc(sem(f"tree_added{u}"), 1)
                    done = n + done
                    v.drain().then_inc(sem("x_final"), 1)
            if stop < 8:
                v.drain().then_inc(sem("x_final"), 1)


_INS = ['x', 'src', 'dst', 'edge_attr_64', 'edge_type_8', 'edge_weight', 'L0_gnn_W1', 'L0_gnn_self_w1', 'L0_gnn_b1',
        'L0_gnn_W2', 'L0_gnn_self_w2', 'L0_gnn_b2', 'L0_ffn_Wg', 'L0_ffn_bg', 'L0_ffn_W1', 'L0_ffn_b1', 'L0_ffn_W2',
        'L0_ffn_b2', 'L1_gnn_weight', 'L1_gnn_bias', 'L1_ffn_W_fx', 'L1_ffn_b_fx', 'L1_ffn_W_x', 'L1_ffn_b_x',
        'L1_ffn_W_slice', 'L1_ffn_b_slice', 'L1_ffn_W_q', 'L1_ffn_W_k', 'L1_ffn_W_v', 'L1_ffn_W_out', 'L1_ffn_b_out',
        'L1_ffn_temperature', 'L2_gnn_W', 'L2_gnn_b', 'L2_ffn_gate_w', 'L2_ffn_gate_b', 'L2_ffn_w1', 'L2_ffn_b1',
        'L2_ffn_w2', 'L2_ffn_b2', 'L2_ffn_gamma', 'L2_ffn_beta', 'L3_gnn_weight', 'L3_gnn_bias', 'L3_ffn_w1s',
        'L3_ffn_b1s', 'L3_ffn_w2s', 'L3_ffn_b2s']


def kernel(**inputs):
    import numpy as _np
    import concourse.bacc as _bacc
    from concourse import mybir as _mybir
    from concourse.bass_utils import run_bass_kernel_spmd as _run

    nc = _bacc.Bacc("TRN2", target_bir_lowering=False, num_devices=1)
    arrays, args = {}, {}
    for name in _INS:
        x = _np.ascontiguousarray(inputs[name])
        arrays[f"in_{name}"] = x
        args[name] = nc.dram_tensor(f"in_{name}", x.shape, _mybir.dt.from_np(x.dtype), kind="ExternalInput").ap()
    out = nc.dram_tensor("out_x", (N, D), F32, kind="ExternalOutput").ap()
    build(nc, args, out)
    r = _run(nc, [arrays], core_ids=[0])
    return r.results[0]["out_x"]
```
